# Optimizing a Trainium2 kernel written in Bass

```python
import numpy as np
import jax
import jax.numpy as jnp

def _softmax(x, axis=-1):
    return jax.nn.softmax(x, axis=axis)

def _gelu(x):
    return jax.nn.gelu(x, approximate=True)

def _silu(x):
    return jax.nn.silu(x)

def _sigmoid(x):
    return jax.nn.sigmoid(x)

def _layernorm(x, axis=-1, eps=1e-05):
    m = jnp.mean(x, axis=axis, keepdims=True)
    v = jnp.var(x, axis=axis, keepdims=True)
    return (x - m) / jnp.sqrt(v + eps)

def _scatter_add(tgt, idx, src, axis=0):
    return tgt.at[idx].add(src)

def _segment_sum(src, seg, n):
    return jax.ops.segment_sum(src, seg, n)
kernel_name = 'mk_xattn_ffn_d4_seqx_r8_394291'

def setup_inputs(seed: int=0):
    np.random.seed(seed)
    _w = jnp.asarray

    def _rec_inputs():
        import jax
        import jax.numpy as jnp
        _rk = jax.random.key(seed)
        x = 7.22e-05 + 1 * jax.random.normal(jax.random.fold_in(_rk, 1), (16, 256, 128), jnp.float32)
        _lenS = 256 - jax.random.randint(jax.random.fold_in(_rk, 7), (16,), 0, max(1, 256 // 4) + 1, jnp.int32)
        _lenS2 = 64 - jax.random.randint(jax.random.fold_in(_rk, 8), (16,), 0, max(1, 64 // 4) + 1, jnp.int32)
        _ctx_1024P = jax.random.normal(jax.random.fold_in(_rk, 11), (16, 16, 128), jnp.float32)
        _ctx_1024c = jax.random.dirichlet(jax.random.fold_in(_rk, 511), 0.3 * jnp.ones((16,), jnp.float32), (16, 64))
        _ctx_1024t = jnp.einsum('bsk,bkd->bsd', _ctx_1024c, _ctx_1024P)
        _ctx_1024t = _ctx_1024t * jax.lax.rsqrt(jnp.mean(jnp.square(_ctx_1024t)) + 1e-12) * 0.953939
        ctx_1024 = -1.39393e-06 + 0.999914 * (_ctx_1024t + 0.3 * jax.random.normal(jax.random.fold_in(_rk, 611), (16, 64, 128), jnp.float32))
        _validS = jnp.arange(256)[None, :] < _lenS[:, None]
        _validS2 = jnp.arange(64)[None, :] < _lenS2[:, None]
        _causal = jnp.tril(jnp.ones((256, 256), dtype=bool))
        mask_BxS2_bf1 = jnp.ones((16, 64), dtype=bool)
        return (x, ctx_1024, mask_BxS2_bf1)
    x, ctx_1024, mask_BxS2_bf1 = _rec_inputs()

    def _L0_xattn_setup():
        import jax, jax.numpy as jnp
        import numpy as np
        HEADS = 16
        DIM_HEAD = 64
        SCALE = DIM_HEAD ** (-0.5)
        key = jax.random.key(seed)
        ks = jax.random.split(key, 6)
        B, Nq, Nkv, D = (4, 256, 128, 128)
        inner = HEADS * DIM_HEAD
        return {'x': jax.random.normal(ks[0], (B, Nq, D), dtype=jnp.float32), 'context': jax.random.normal(ks[1], (B, Nkv, D), dtype=jnp.float32), 'mask': jnp.ones((B, Nkv), dtype=bool), 'Wq': jax.random.normal(ks[2], (inner, D), dtype=jnp.float32) * D ** (-0.5), 'Wkv': jax.random.normal(ks[3], (2 * inner, D), dtype=jnp.float32) * D ** (-0.5), 'Wout': jax.random.normal(ks[4], (D, inner), dtype=jnp.float32) * inner ** (-0.5), 'b_out': jnp.zeros((D,), dtype=jnp.float32)}
    _L0_xattn_all = _L0_xattn_setup()
    _L0_xattn_in = {k: v for k, v in _L0_xattn_all.items() if k in ('Wq', 'Wkv', 'Wout', 'b_out')}
    del _L0_xattn_all

    def _L0_ffn_setup():
        import jax, jax.numpy as jnp
        import numpy as np
        DIM = 128
        DEPTH = 6
        HEADS = 16
        DIM_HEAD = 64
        WINDOW = 32
        INNER = HEADS * DIM_HEAD
        DIM_INNER = int(DIM * 4 * 2 / 3)
        QK_SCALE = 8.0

        def shift_tokens(t):
            a, s = jnp.split(t, 2, -1)
            s = jnp.pad(s, ((0, 0), (1, 0), (0, 0)))[:, :-1]
            return jnp.concatenate([a, s], -1)

        def l2norm(t):
            return t / jnp.maximum(jnp.linalg.norm(t, axis=-1, keepdims=True), 1e-12)

        def rotate_half(x):
            x1, x2 = jnp.split(x, 2, -1)
            return jnp.concatenate([-x2, x1], -1)

        def rotary_tables(n):
            half = jnp.arange(0, DIM_HEAD, 2, dtype=jnp.float32)
            inv_freq = 1.0 / 10000.0 ** (half / DIM_HEAD)
            t = jnp.arange(n, dtype=jnp.float32)
            freqs = t[:, None] * inv_freq[None, :]
            freqs = jnp.concatenate([freqs, freqs], -1)
            base_scale = (half + 0.4 * DIM_HEAD) / (1.4 * DIM_HEAD)
            power = (t - n // 2) / (WINDOW // 2)
            scale = base_scale[None, :] ** power[:, None]
            scale = jnp.concatenate([scale, scale], -1)
            return (freqs, scale)

        def local_attention(q, k, v):
            b, h, n, d = q.shape
            w = WINDOW
            nw = n // w
            bq = q.reshape(b, h, nw, w, d)
            bk = k.reshape(b, h, nw, w, d)
            bv = v.reshape(b, h, nw, w, d)

            def look(t):
                p = jnp.pad(t, ((0, 0), (0, 0), (1, 0), (0, 0), (0, 0)))
                return jnp.concatenate([p[:, :, :nw], p[:, :, 1:]], axis=3)
            bk2, bv2 = (look(bk), look(bv))
            seq = jnp.arange(n).reshape(nw, w)
            seq_p = jnp.pad(seq, ((1, 0), (0, 0)), constant_values=-1)
            jt = jnp.concatenate([seq_p[:nw], seq_p[1:]], axis=1)
            it = seq[:, :, None]
            jb = jt[:, None, :]
            mask = (it < jb) | (it > jb + w) | (jb == -1)
            sim = jnp.einsum('bhwie,bhwje->bhwij', bq, bk2) * QK_SCALE
            sim = jnp.where(mask, -jnp.finfo(sim.dtype).max, sim)
            attn = jax.nn.softmax(sim, -1)
            out = jnp.einsum('bhwij,bhwje->bhwie', attn, bv2)
            return out.reshape(b, h, n, d)

        def attn_layer(x, Wqkv, qs, ksc, Wo):
            b, n, _ = x.shape
            qkv = x @ Wqkv
            q, k, v = jnp.split(qkv, 3, -1)
            sh = lambda t: t.reshape(b, n, HEADS, DIM_HEAD).transpose(0, 2, 1, 3)
            q, k, v = (sh(q), sh(k), sh(v))
            q = l2norm(q) * qs
            k = l2norm(k) * ksc
            freqs, scale = rotary_tables(n)
            cos, sin = (jnp.cos(freqs), jnp.sin(freqs))
            q = q * cos * scale + rotate_half(q) * sin * scale
            inv = 1.0 / scale
            k = k * cos * inv + rotate_half(k) * sin * inv
            out = local_attention(q, k, v)
            out = out.transpose(0, 2, 1, 3).reshape(b, n, INNER)
            return out @ Wo

        def ffn_layer(x, g, bln, W1, b1, W2, b2):
            mu = x.mean(-1, keepdims=True)
            var = ((x - mu) ** 2).mean(-1, keepdims=True)
            xn = (x - mu) / jnp.sqrt(var + 1e-05) * g + bln
            hg = xn @ W1 + b1
            a, gate = jnp.split(hg, 2, -1)
            return a * jax.nn.gelu(gate, approximate=False) @ W2 + b2
        key = jax.random.key(seed)
        ks = jax.random.split(key, 8)
        B, N = (2, 256)
        init = lambda k, shape: jax.random.normal(k, shape, jnp.float32) * 0.02
        return {'x': jax.random.normal(ks[0], (B, N, DIM), jnp.float32), 'Wqkv': init(ks[1], (DEPTH, DIM, 3 * INNER)), 'q_scale': jnp.ones((DEPTH, DIM_HEAD), jnp.float32), 'k_scale': jnp.ones((DEPTH, DIM_HEAD), jnp.float32), 'Wo': init(ks[2], (DEPTH, INNER, DIM)), 'ln_g': jnp.ones((DEPTH, DIM), jnp.float32), 'ln_b': jnp.zeros((DEPTH, DIM), jnp.float32), 'W1': init(ks[3], (DEPTH, DIM, 2 * DIM_INNER)), 'b1': jnp.zeros((DEPTH, 2 * DIM_INNER), jnp.float32), 'W2': init(ks[4], (DEPTH, DIM_INNER, DIM)), 'b2': jnp.zeros((DEPTH, DIM), jnp.float32)}
    _L0_ffn_all = _L0_ffn_setup()
    _L0_ffn_in = {k: v for k, v in _L0_ffn_all.items() if k in ('Wqkv', 'q_scale', 'k_scale', 'Wo', 'ln_g', 'ln_b', 'W1', 'b1', 'W2', 'b2')}
    del _L0_ffn_all

    def _L1_xattn_setup():
        import jax, jax.numpy as jnp
        import numpy as np
        import math
        B, L, D = (4, 512, 128)
        M = 32
        EPS = 1e-06
        key = jax.random.key(seed)
        kq, kk, kv, kp = jax.random.split(key, 4)
        Q = jax.random.normal(kq, (B, L, D), dtype=jnp.float32)
        K = jax.random.normal(kk, (B, L, D), dtype=jnp.float32)
        V = jax.random.normal(kv, (B, L, D), dtype=jnp.float32)
        projection = jax.random.normal(kp, (M, D), dtype=jnp.float32)
        return {'Q': Q, 'K': K, 'V': V, 'projection': projection}
    _L1_xattn_all = _L1_xattn_setup()
    _L1_xattn_in = {k: v for k, v in _L1_xattn_all.items() if k in ('projection',)}
    del _L1_xattn_all

    def _L1_ffn_setup():
        import jax, jax.numpy as jnp
        import numpy as np
        QMAX = 127.0

        def _ste_round(v):
            return v + jax.lax.stop_gradient(jnp.round(v) - v)

        def _act_fake_quant(x, clip_factor):
            scale = jax.nn.sigmoid(clip_factor) * jnp.max(jnp.abs(x)) / QMAX
            return jnp.clip(_ste_round(x / scale), -QMAX - 1.0, QMAX) * scale

        def _weight_fake_quant(w):
            scale = jnp.max(jnp.abs(w), axis=1, keepdims=True) / QMAX
            return jnp.clip(_ste_round(w / scale), -QMAX - 1.0, QMAX) * scale
        key = jax.random.key(seed)
        k1, k2, k3, k4 = jax.random.split(key, 4)
        B, S, H, I = (8, 1024, 128, 352)
        return {'x': jax.random.normal(k1, (B, S, H), dtype=jnp.float32), 'clip_x': jnp.full((1,), 4.0, dtype=jnp.float32), 'clip_down': jnp.full((1,), 4.0, dtype=jnp.float32), 'w_gate': jax.random.normal(k2, (I, H), dtype=jnp.float32) * 0.02, 'w_up': jax.random.normal(k3, (I, H), dtype=jnp.float32) * 0.02, 'w_down': jax.random.normal(k4, (H, I), dtype=jnp.float32) * 0.02}
    _L1_ffn_all = _L1_ffn_setup()
    _L1_ffn_in = {k: v for k, v in _L1_ffn_all.items() if k in ('clip_x', 'clip_down', 'w_gate', 'w_up', 'w_down')}
    del _L1_ffn_all

    def _L2_xattn_setup():
        import jax, jax.numpy as jnp
        import numpy as np
        EPS = 0.001
        LEAKY_ALPHA = 0.2

        def layer_norm(x, gamma, beta):
            mu = jnp.mean(x, axis=-1, keepdims=True)
            var = jnp.mean(jnp.square(x - mu), axis=-1, keepdims=True)
            return (x - mu) * jax.lax.rsqrt(var + EPS) * gamma + beta

        def attention_head(x_k, x_v, x_q, Wk, Wq, Wv, use_mask):
            K = x_k @ Wk
            V = x_v @ Wv
            Q = x_q @ Wq
            Lq, Lk = (Q.shape[1], K.shape[1])
            score = jnp.einsum('bqd,bkd->bqk', Q, K) / jnp.sqrt(jnp.float32(Lk))
            if use_mask:
                mask = jnp.triu(jnp.full((Lq, Lk), -jnp.inf, dtype=score.dtype), k=1)
                score = score + mask
            return jax.nn.softmax(score, axis=-1) @ V
        key = jax.random.key(seed)
        ks = jax.random.split(key, 12)
        B, S, D = (8, 256, 128)
        inp = {'inputs': jax.random.normal(ks[0], (B, S, D), jnp.float32), 'context_sequence': jax.random.normal(ks[1], (B, S, D), jnp.float32), 'Wk1': jax.random.normal(ks[2], (D, D), jnp.float32) * 0.01, 'Wq1': jax.random.normal(ks[3], (D, D), jnp.float32) * 0.01, 'Wv1': jax.random.normal(ks[4], (D, D), jnp.float32) * 0.01, 'Wk2': jax.random.normal(ks[5], (D, D), jnp.float32) * 0.01, 'Wq2': jax.random.normal(ks[6], (D, D), jnp.float32) * 0.01, 'Wv2': jax.random.normal(ks[7], (D, D), jnp.float32) * 0.01, 'W1': jax.random.normal(ks[8], (D, D), jnp.float32) * (1.0 / np.sqrt(D)), 'b1': jnp.zeros((D,), jnp.float32), 'W2': jax.random.normal(ks[9], (D, D), jnp.float32) * (1.0 / np.sqrt(D)), 'b2': jnp.zeros((D,), jnp.float32), 'gamma': jnp.ones((D,), jnp.float32), 'beta': jnp.zeros((D,), jnp.float32)}
        return inp
    _L2_xattn_all = _L2_xattn_setup()
    _L2_xattn_in = {k: v for k, v in _L2_xattn_all.items() if k in ('Wk1', 'Wq1', 'Wv1', 'Wk2', 'Wq2', 'Wv2', 'W1', 'b1', 'W2', 'b2', 'gamma', 'beta')}
    del _L2_xattn_all

    def _L2_ffn_setup():
        import jax, jax.numpy as jnp
        import numpy as np
        EPS = 1e-06
        LN_EPS = 1e-05

        def _absmean_core(W):
            gamma = jnp.mean(jnp.abs(W)) + EPS
            Ws = W / gamma
            Wq = jnp.sign(Ws) * jnp.minimum(jnp.round(jnp.abs(Ws)), 1.0)
            return (Wq, gamma)

        @jax.custom_vjp
        def absmean(W):
            return _absmean_core(W)[0]

        def _absmean_fwd(W):
            Wq, gamma = _absmean_core(W)
            return (Wq, gamma)

        def _absmean_bwd(gamma, g):
            return (g / gamma,)
        absmean.defvjp(_absmean_fwd, _absmean_bwd)

        def layernorm(x, w, b, eps=LN_EPS):
            mu = jnp.mean(x, axis=-1, keepdims=True)
            var = jnp.mean((x - mu) ** 2, axis=-1, keepdims=True)
            return (x - mu) * jax.lax.rsqrt(var + eps) * w + b
        key = jax.random.key(seed)
        k1, k2, k3 = jax.random.split(key, 3)
        d, h = (128, 512)
        B, T = (8, 256)
        return {'x': jax.random.normal(k1, (B, T, d), jnp.float32), 'W_fc': jax.random.normal(k2, (h, d), jnp.float32), 'ln_w': jnp.ones((h,), jnp.float32), 'ln_b': jnp.zeros((h,), jnp.float32), 'W_proj': jax.random.normal(k3, (d, h), jnp.float32)}
    _L2_ffn_all = _L2_ffn_setup()
    _L2_ffn_in = {k: v for k, v in _L2_ffn_all.items() if k in ('W_fc', 'ln_w', 'ln_b', 'W_proj')}
    del _L2_ffn_all

    def _L3_xattn_setup():
        import jax, jax.numpy as jnp
        import numpy as np
        B, SX, SY, D = (64, 64, 64, 128)
        key = jax.random.key(seed)
        k1, k2, k3, k4 = jax.random.split(key, 4)
        x = jax.random.normal(k1, (B, SX, D), dtype=jnp.float32)
        y = jax.random.normal(k2, (B, SY, D), dtype=jnp.float32)
        W = jax.random.uniform(k3, (D, D), dtype=jnp.float32, minval=-0.05, maxval=0.05)
        b = jax.random.uniform(k4, (D,), dtype=jnp.float32, minval=-0.05, maxval=0.05)
        return {'x': x, 'y': y, 'W': W, 'b': b}
    _L3_xattn_all = _L3_xattn_setup()
    _L3_xattn_in = {k: v for k, v in _L3_xattn_all.items() if k in ('W', 'b')}
    del _L3_xattn_all

    def _L3_ffn_setup():
        import jax, jax.numpy as jnp
        import numpy as np
        CAPACITY_FACTOR = 1.0
        key = jax.random.key(seed)
        ks = jax.random.split(key, 5)
        B, S, D, E, F = (2, 256, 128, 8, 512)
        x = jax.random.normal(ks[0], (B, S, D), dtype=jnp.float32)
        Ws = jax.random.normal(ks[1], (D, E), dtype=jnp.float32) * (1.0 / np.sqrt(D))
        bs = jnp.zeros((E,), dtype=jnp.float32)
        W1 = jax.random.normal(ks[2], (E, D, F), dtype=jnp.float32) * (1.0 / np.sqrt(D))
        b1 = jnp.zeros((E, F), dtype=jnp.float32)
        W2 = jax.random.normal(ks[3], (E, F, D), dtype=jnp.float32) * (1.0 / np.sqrt(F))
        b2 = jnp.zeros((E, D), dtype=jnp.float32)
        return {'x': x, 'Ws': Ws, 'bs': bs, 'W1': W1, 'b1': b1, 'W2': W2, 'b2': b2}
    _L3_ffn_all = _L3_ffn_setup()
    _L3_ffn_in = {k: v for k, v in _L3_ffn_all.items() if k in ('Ws', 'bs', 'W1', 'b1', 'W2', 'b2')}
    del _L3_ffn_all
    return {'x': x, 'ctx_1024': ctx_1024, 'mask_BxS2_bf1': mask_BxS2_bf1, 'L0_xattn_Wq': _L0_xattn_in['Wq'], 'L0_xattn_Wkv': _L0_xattn_in['Wkv'], 'L0_xattn_Wout': _L0_xattn_in['Wout'], 'L0_xattn_b_out': _L0_xattn_in['b_out'], 'L0_ffn_Wqkv': _L0_ffn_in['Wqkv'], 'L0_ffn_q_scale': _L0_ffn_in['q_scale'], 'L0_ffn_k_scale': _L0_ffn_in['k_scale'], 'L0_ffn_Wo': _L0_ffn_in['Wo'], 'L0_ffn_ln_g': _L0_ffn_in['ln_g'], 'L0_ffn_ln_b': _L0_ffn_in['ln_b'], 'L0_ffn_W1': _L0_ffn_in['W1'], 'L0_ffn_b1': _L0_ffn_in['b1'], 'L0_ffn_W2': _L0_ffn_in['W2'], 'L0_ffn_b2': _L0_ffn_in['b2'], 'L1_xattn_projection': _L1_xattn_in['projection'], 'L1_ffn_clip_x': _L1_ffn_in['clip_x'], 'L1_ffn_clip_down': _L1_ffn_in['clip_down'], 'L1_ffn_w_gate': _L1_ffn_in['w_gate'], 'L1_ffn_w_up': _L1_ffn_in['w_up'], 'L1_ffn_w_down': _L1_ffn_in['w_down'], 'L2_xattn_Wk1': _L2_xattn_in['Wk1'], 'L2_xattn_Wq1': _L2_xattn_in['Wq1'], 'L2_xattn_Wv1': _L2_xattn_in['Wv1'], 'L2_xattn_Wk2': _L2_xattn_in['Wk2'], 'L2_xattn_Wq2': _L2_xattn_in['Wq2'], 'L2_xattn_Wv2': _L2_xattn_in['Wv2'], 'L2_xattn_W1': _L2_xattn_in['W1'], 'L2_xattn_b1': _L2_xattn_in['b1'], 'L2_xattn_W2': _L2_xattn_in['W2'], 'L2_xattn_b2': _L2_xattn_in['b2'], 'L2_xattn_gamma': _L2_xattn_in['gamma'], 'L2_xattn_beta': _L2_xattn_in['beta'], 'L2_ffn_W_fc': _L2_ffn_in['W_fc'], 'L2_ffn_ln_w': _L2_ffn_in['ln_w'], 'L2_ffn_ln_b': _L2_ffn_in['ln_b'], 'L2_ffn_W_proj': _L2_ffn_in['W_proj'], 'L3_xattn_W': _L3_xattn_in['W'], 'L3_xattn_b': _L3_xattn_in['b'], 'L3_ffn_Ws': _L3_ffn_in['Ws'], 'L3_ffn_bs': _L3_ffn_in['bs'], 'L3_ffn_W1': _L3_ffn_in['W1'], 'L3_ffn_b1': _L3_ffn_in['b1'], 'L3_ffn_W2': _L3_ffn_in['W2'], 'L3_ffn_b2': _L3_ffn_in['b2']}

def reference(x, ctx_1024, mask_BxS2_bf1, L0_xattn_Wq, L0_xattn_Wkv, L0_xattn_Wout, L0_xattn_b_out, L0_ffn_Wqkv, L0_ffn_q_scale, L0_ffn_k_scale, L0_ffn_Wo, L0_ffn_ln_g, L0_ffn_ln_b, L0_ffn_W1, L0_ffn_b1, L0_ffn_W2, L0_ffn_b2, L1_xattn_projection, L1_ffn_clip_x, L1_ffn_clip_down, L1_ffn_w_gate, L1_ffn_w_up, L1_ffn_w_down, L2_xattn_Wk1, L2_xattn_Wq1, L2_xattn_Wv1, L2_xattn_Wk2, L2_xattn_Wq2, L2_xattn_Wv2, L2_xattn_W1, L2_xattn_b1, L2_xattn_W2, L2_xattn_b2, L2_xattn_gamma, L2_xattn_beta, L2_ffn_W_fc, L2_ffn_ln_w, L2_ffn_ln_b, L2_ffn_W_proj, L3_xattn_W, L3_xattn_b, L3_ffn_Ws, L3_ffn_bs, L3_ffn_W1, L3_ffn_b1, L3_ffn_W2, L3_ffn_b2):
    import jax
    import jax.numpy as jnp

    def _L0_xattn_ref(x, context, mask, Wq, Wkv, Wout, b_out):
        import jax, jax.numpy as jnp
        import numpy as np
        HEADS = 16
        DIM_HEAD = 64
        SCALE = DIM_HEAD ** (-0.5)
        B, Nq, _ = x.shape
        Nkv = context.shape[1]
        q = x @ Wq.T
        kv = context @ Wkv.T
        k, v = jnp.split(kv, 2, axis=-1)
        q = q.reshape(B, Nq, HEADS, DIM_HEAD).transpose(0, 2, 1, 3)
        k = k.reshape(B, Nkv, HEADS, DIM_HEAD).transpose(0, 2, 1, 3)
        v = v.reshape(B, Nkv, HEADS, DIM_HEAD).transpose(0, 2, 1, 3)
        sim = jnp.einsum('bhid,bhjd->bhij', q, k) * SCALE
        max_neg = -jnp.finfo(sim.dtype).max
        sim = jnp.where(mask[:, None, None, :], sim, max_neg)
        attn = jax.nn.softmax(sim, axis=-1)
        out = jnp.einsum('bhij,bhjd->bhid', attn, v)
        out = out.transpose(0, 2, 1, 3).reshape(B, Nq, HEADS * DIM_HEAD)
        return out @ Wout.T + b_out

    def _L0_ffn_ref(x, Wqkv, q_scale, k_scale, Wo, ln_g, ln_b, W1, b1, W2, b2):
        import jax, jax.numpy as jnp
        import numpy as np
        DIM = 128
        DEPTH = 6
        HEADS = 16
        DIM_HEAD = 64
        WINDOW = 32
        INNER = HEADS * DIM_HEAD
        DIM_INNER = int(DIM * 4 * 2 / 3)
        QK_SCALE = 8.0

        def shift_tokens(t):
            a, s = jnp.split(t, 2, -1)
            s = jnp.pad(s, ((0, 0), (1, 0), (0, 0)))[:, :-1]
            return jnp.concatenate([a, s], -1)

        def l2norm(t):
            return t / jnp.maximum(jnp.linalg.norm(t, axis=-1, keepdims=True), 1e-12)

        def rotate_half(x):
            x1, x2 = jnp.split(x, 2, -1)
            return jnp.concatenate([-x2, x1], -1)

        def rotary_tables(n):
            half = jnp.arange(0, DIM_HEAD, 2, dtype=jnp.float32)
            inv_freq = 1.0 / 10000.0 ** (half / DIM_HEAD)
            t = jnp.arange(n, dtype=jnp.float32)
            freqs = t[:, None] * inv_freq[None, :]
            freqs = jnp.concatenate([freqs, freqs], -1)
            base_scale = (half + 0.4 * DIM_HEAD) / (1.4 * DIM_HEAD)
            power = (t - n // 2) / (WINDOW // 2)
            scale = base_scale[None, :] ** power[:, None]
            scale = jnp.concatenate([scale, scale], -1)
            return (freqs, scale)

        def local_attention(q, k, v):
            b, h, n, d = q.shape
            w = WINDOW
            nw = n // w
            bq = q.reshape(b, h, nw, w, d)
            bk = k.reshape(b, h, nw, w, d)
            bv = v.reshape(b, h, nw, w, d)

            def look(t):
                p = jnp.pad(t, ((0, 0), (0, 0), (1, 0), (0, 0), (0, 0)))
                return jnp.concatenate([p[:, :, :nw], p[:, :, 1:]], axis=3)
            bk2, bv2 = (look(bk), look(bv))
            seq = jnp.arange(n).reshape(nw, w)
            seq_p = jnp.pad(seq, ((1, 0), (0, 0)), constant_values=-1)
            jt = jnp.concatenate([seq_p[:nw], seq_p[1:]], axis=1)
            it = seq[:, :, None]
            jb = jt[:, None, :]
            mask = (it < jb) | (it > jb + w) | (jb == -1)
            sim = jnp.einsum('bhwie,bhwje->bhwij', bq, bk2) * QK_SCALE
            sim = jnp.where(mask, -jnp.finfo(sim.dtype).max, sim)
            attn = jax.nn.softmax(sim, -1)
            out = jnp.einsum('bhwij,bhwje->bhwie', attn, bv2)
            return out.reshape(b, h, n, d)

        def attn_layer(x, Wqkv, qs, ksc, Wo):
            b, n, _ = x.shape
            qkv = x @ Wqkv
            q, k, v = jnp.split(qkv, 3, -1)
            sh = lambda t: t.reshape(b, n, HEADS, DIM_HEAD).transpose(0, 2, 1, 3)
            q, k, v = (sh(q), sh(k), sh(v))
            q = l2norm(q) * qs
            k = l2norm(k) * ksc
            freqs, scale = rotary_tables(n)
            cos, sin = (jnp.cos(freqs), jnp.sin(freqs))
            q = q * cos * scale + rotate_half(q) * sin * scale
            inv = 1.0 / scale
            k = k * cos * inv + rotate_half(k) * sin * inv
            out = local_attention(q, k, v)
            out = out.transpose(0, 2, 1, 3).reshape(b, n, INNER)
            return out @ Wo

        def ffn_layer(x, g, bln, W1, b1, W2, b2):
            mu = x.mean(-1, keepdims=True)
            var = ((x - mu) ** 2).mean(-1, keepdims=True)
            xn = (x - mu) / jnp.sqrt(var + 1e-05) * g + bln
            hg = xn @ W1 + b1
            a, gate = jnp.split(hg, 2, -1)
            return a * jax.nn.gelu(gate, approximate=False) @ W2 + b2
        for i in range(DEPTH):
            x = attn_layer(shift_tokens(x), Wqkv[i], q_scale[i], k_scale[i], Wo[i]) + x
            x = ffn_layer(shift_tokens(x), ln_g[i], ln_b[i], W1[i], b1[i], W2[i], b2[i]) + x
        return x

    def _L1_xattn_ref(Q, K, V, projection):
        import jax, jax.numpy as jnp
        import numpy as np
        import math
        B, L, D = (4, 512, 128)
        M = 32
        EPS = 1e-06
        d_model = Q.shape[-1]
        m = projection.shape[0]
        inv_sqrt_d = 1.0 / math.sqrt(d_model)
        rf_q = jnp.exp(jnp.einsum('bld,md->blm', Q * inv_sqrt_d, projection)) / math.sqrt(m)
        rf_k = jnp.exp(jnp.einsum('bld,md->blm', K * inv_sqrt_d, projection))
        KV = jnp.einsum('blm,bld->bmd', rf_k, V)
        Z = jnp.sum(rf_k, axis=1)
        out = jnp.einsum('blm,bmd->bld', rf_q, KV)
        normalizer = jnp.einsum('blm,bm->bl', rf_q, Z) + EPS
        return out / normalizer[..., None]

    def _L1_ffn_ref(x, clip_x, clip_down, w_gate, w_up, w_down):
        import jax, jax.numpy as jnp
        import numpy as np
        QMAX = 127.0

        def _ste_round(v):
            return v + jax.lax.stop_gradient(jnp.round(v) - v)

        def _act_fake_quant(x, clip_factor):
            scale = jax.nn.sigmoid(clip_factor) * jnp.max(jnp.abs(x)) / QMAX
            return jnp.clip(_ste_round(x / scale), -QMAX - 1.0, QMAX) * scale

        def _weight_fake_quant(w):
            scale = jnp.max(jnp.abs(w), axis=1, keepdims=True) / QMAX
            return jnp.clip(_ste_round(w / scale), -QMAX - 1.0, QMAX) * scale
        xq = _act_fake_quant(x, clip_x[0])
        gate = jnp.einsum('bsh,ih->bsi', xq, _weight_fake_quant(w_gate))
        up = jnp.einsum('bsh,ih->bsi', xq, _weight_fake_quant(w_up))
        h = _act_fake_quant(jax.nn.silu(gate) * up, clip_down[0])
        return jnp.einsum('bsi,hi->bsh', h, _weight_fake_quant(w_down))

    def _L2_xattn_ref(inputs, context_sequence, Wk1, Wq1, Wv1, Wk2, Wq2, Wv2, W1, b1, W2, b2, gamma, beta):
        import jax, jax.numpy as jnp
        import numpy as np
        EPS = 0.001
        LEAKY_ALPHA = 0.2

        def layer_norm(x, gamma, beta):
            mu = jnp.mean(x, axis=-1, keepdims=True)
            var = jnp.mean(jnp.square(x - mu), axis=-1, keepdims=True)
            return (x - mu) * jax.lax.rsqrt(var + EPS) * gamma + beta

        def attention_head(x_k, x_v, x_q, Wk, Wq, Wv, use_mask):
            K = x_k @ Wk
            V = x_v @ Wv
            Q = x_q @ Wq
            Lq, Lk = (Q.shape[1], K.shape[1])
            score = jnp.einsum('bqd,bkd->bqk', Q, K) / jnp.sqrt(jnp.float32(Lk))
            if use_mask:
                mask = jnp.triu(jnp.full((Lq, Lk), -jnp.inf, dtype=score.dtype), k=1)
                score = score + mask
            return jax.nn.softmax(score, axis=-1) @ V
        att = attention_head(inputs, inputs, inputs, Wk1, Wq1, Wv1, use_mask=True)
        norm = layer_norm(att + inputs, gamma, beta)
        att2 = attention_head(context_sequence, context_sequence, att, Wk2, Wq2, Wv2, use_mask=False)
        norm2 = layer_norm(att2 + norm, gamma, beta)
        h = jax.nn.leaky_relu(norm2 @ W1 + b1, negative_slope=LEAKY_ALPHA)
        ff = h @ W2 + b2
        norm3 = layer_norm(ff + norm2, gamma, beta)
        return jax.nn.relu(norm3)

    def _L2_ffn_ref(x, W_fc, ln_w, ln_b, W_proj):
        import jax, jax.numpy as jnp
        import numpy as np
        EPS = 1e-06
        LN_EPS = 1e-05

        def _absmean_core(W):
            gamma = jnp.mean(jnp.abs(W)) + EPS
            Ws = W / gamma
            Wq = jnp.sign(Ws) * jnp.minimum(jnp.round(jnp.abs(Ws)), 1.0)
            return (Wq, gamma)

        @jax.custom_vjp
        def absmean(W):
            return _absmean_core(W)[0]

        def _absmean_fwd(W):
            Wq, gamma = _absmean_core(W)
            return (Wq, gamma)

        def _absmean_bwd(gamma, g):
            return (g / gamma,)
        absmean.defvjp(_absmean_fwd, _absmean_bwd)

        def layernorm(x, w, b, eps=LN_EPS):
            mu = jnp.mean(x, axis=-1, keepdims=True)
            var = jnp.mean((x - mu) ** 2, axis=-1, keepdims=True)
            return (x - mu) * jax.lax.rsqrt(var + eps) * w + b
        h = jnp.einsum('btd,hd->bth', x, absmean(W_fc))
        h = jax.nn.gelu(h, approximate=False)
        h = layernorm(h, ln_w, ln_b)
        return jnp.einsum('bth,dh->btd', h, absmean(W_proj))

    def _L3_xattn_ref(x, y, W, b):
        import jax, jax.numpy as jnp
        import numpy as np
        B, SX, SY, D = (64, 64, 64, 128)
        proj = jnp.einsum('bsd,de->bse', x, W) + b
        att = jnp.einsum('bsd,btd->bst', proj, y)
        nor = jax.nn.softmax(att, axis=-1)
        return jnp.einsum('bst,btd->bsd', nor, y)

    def _L3_ffn_ref(x, Ws, bs, W1, b1, W2, b2):
        import jax, jax.numpy as jnp
        import numpy as np
        CAPACITY_FACTOR = 1.0
        B, S, D = x.shape
        E = Ws.shape[1]
        N = B * S
        k = int(CAPACITY_FACTOR * N / E)
        xf = x.reshape(N, D)
        route_prob = jax.nn.softmax(xf @ Ws + bs, axis=-1).T
        route_vals, routes = jax.lax.top_k(route_prob, k)
        xin = xf[routes]
        h = jax.nn.gelu(jnp.einsum('ekd,edf->ekf', xin, W1) + b1[:, None, :])
        out = jnp.einsum('ekf,efd->ekd', h, W2) + b2[:, None, :]
        out = out * route_vals[..., None]
        final = jnp.zeros((N, D), dtype=x.dtype).at[routes.reshape(-1)].add(out.reshape(-1, D))
        return final.reshape(B, S, D)
    x = x + _L0_xattn_ref(_layernorm(x, axis=-1), ctx_1024, mask_BxS2_bf1, L0_xattn_Wq, L0_xattn_Wkv, L0_xattn_Wout, L0_xattn_b_out)
    x = x + _L0_ffn_ref(_layernorm(x, axis=-1), L0_ffn_Wqkv, L0_ffn_q_scale, L0_ffn_k_scale, L0_ffn_Wo, L0_ffn_ln_g, L0_ffn_ln_b, L0_ffn_W1, L0_ffn_b1, L0_ffn_W2, L0_ffn_b2)
    x = x + _L1_xattn_ref(_layernorm(x, axis=-1), ctx_1024, ctx_1024, L1_xattn_projection)
    x = x + _L1_ffn_ref(_layernorm(x, axis=-1), L1_ffn_clip_x, L1_ffn_clip_down, L1_ffn_w_gate, L1_ffn_w_up, L1_ffn_w_down)
    x = x + _L2_xattn_ref(_layernorm(x, axis=-1), ctx_1024, L2_xattn_Wk1, L2_xattn_Wq1, L2_xattn_Wv1, L2_xattn_Wk2, L2_xattn_Wq2, L2_xattn_Wv2, L2_xattn_W1, L2_xattn_b1, L2_xattn_W2, L2_xattn_b2, L2_xattn_gamma, L2_xattn_beta)
    x = x + _L2_ffn_ref(_layernorm(x, axis=-1), L2_ffn_W_fc, L2_ffn_ln_w, L2_ffn_ln_b, L2_ffn_W_proj)
    x = x + _L3_xattn_ref(_layernorm(x, axis=-1), ctx_1024, L3_xattn_W, L3_xattn_b)
    x = x + _L3_ffn_ref(_layernorm(x, axis=-1), L3_ffn_Ws, L3_ffn_bs, L3_ffn_W1, L3_ffn_b1, L3_ffn_W2, L3_ffn_b2)
    return x

_drawn_inputs = setup_inputs


def setup_inputs(seed=0):
    import zlib

    import numpy as np

    out = dict(_drawn_inputs(seed))
    spreads = {'L0_xattn_b_out': (0.0, 0.1),
     'L0_ffn_q_scale': (1.0, 0.6),
     'L0_ffn_k_scale': (1.0, 0.6),
     'L0_ffn_ln_g': (1.0, 0.6),
     'L0_ffn_ln_b': (0.0, 0.8),
     'L0_ffn_b1': (0.0, 0.8),
     'L0_ffn_b2': (0.0, 0.1),
     'L2_xattn_b1': (0.0, 0.525),
     'L2_xattn_b2': (0.0, 0.318),
     'L2_xattn_gamma': (1.0, 0.2),
     'L2_xattn_beta': (0.0, 0.1),
     'L2_ffn_ln_w': (1.0, 0.2),
     'L2_ffn_ln_b': (0.0, 0.1),
     'L3_ffn_bs': (0.0, 0.8),
     'L3_ffn_b1': (0.0, 0.8),
     'L3_ffn_b2': (0.0, 2.0)}
    factors = {'L0_ffn_W1': 3.361,
     'L0_ffn_W2': 3.295,
     'L1_ffn_w_gate': 8.0,
     'L1_ffn_w_up': 8.0,
     'L1_ffn_w_down': 8.0,
     'L2_xattn_Wk1': 25.3,
     'L2_xattn_Wq1': 23.455,
     'L2_xattn_Wv1': 2.707,
     'L2_xattn_Wk2': 29.76,
     'L2_xattn_Wq2': 27.962,
     'L2_xattn_Wv2': 3.392,
     'L3_xattn_b': 8.0,
     'L3_ffn_Ws': 4.419,
     'L3_ffn_W1': 4.868,
     'L3_ffn_W2': 4.372}
    for name, (base, spread) in spreads.items():
        noise = np.random.default_rng([zlib.crc32(name.encode()), seed]).standard_normal(out[name].shape)
        drawn = base * np.exp(spread * noise) if base else spread * noise
        out[name] = jnp.asarray(drawn.astype(out[name].dtype))
    for name, factor in factors.items():
        out[name] = (out[name] * factor).astype(out[name].dtype)
    return out
```

```python
from contextlib import ExitStack

import numpy as np

import concourse.bass as bass
from concourse import mybir

F32 = mybir.dt.float32
BF16 = mybir.dt.bfloat16
I32 = mybir.dt.int32
U8 = mybir.dt.uint8
ALU = mybir.AluOpType
ACT = mybir.ActivationFunctionType
AX_X = mybir.AxisListType.X

BATCH, SEQ, DIM = 16, 256, 128
CTX = 64
TILES = BATCH * SEQ // 128
PASS_TOK = 512
PASS_TILES = PASS_TOK // 128
PASSES = BATCH * SEQ // PASS_TOK
HEADS, HEAD_DIM = 16, 64
INNER = HEADS * HEAD_DIM
GROUP = 8
PAIRS = HEADS // 2
ROUND = 12582912.0
RSQRT_SEED = 1597463007.0


class Chain:

    def __init__(self, engine, semaphore):
        self.engine, self.semaphore, self.count = engine, semaphore, 0

    def link(self, instruction):
        instruction.then_inc(self.semaphore, 1)
        self.count += 1
        self.engine.wait_ge(self.semaphore, self.count)

    def mark(self, instruction):
        instruction.then_inc(self.semaphore, 1)
        self.count += 1

    def wait(self):
        self.engine.wait_ge(self.semaphore, self.count)

    def reset(self):
        self.engine.wait_ge(self.semaphore, self.count)
        self.engine.sem_clear(self.semaphore)
        self.count = 0


def clear(nc, semaphores):
    with nc.Block() as block:

        @block.sync
        def _(sp):
            for semaphore in semaphores:
                sp.sem_clear(semaphore)


def rsqrt(vector, chain, out, value, work):
    chain.link(vector.tensor_scalar(out.bitcast(I32), value.bitcast(I32), -0.5, RSQRT_SEED, ALU.mult, ALU.add))
    for _ in range(4):
        chain.link(vector.tensor_tensor(work, out, out, ALU.mult))
        chain.link(vector.scalar_tensor_tensor(work, work, -0.5, value, ALU.mult, ALU.mult))
        chain.link(vector.scalar_tensor_tensor(out, work, 1.5, out, ALU.add, ALU.mult))


def alone(engine):
    engine.nop(nofuse=True)


def over(ap, shape):
    return ap.unsqueeze(len(ap.shape)).broadcast_to(shape)


def layer_norm_tiles(nc, dve, chain, source, out, work, eps=1e-5):
    stats, mv, var = work
    for t in range(PASS_TILES):
        chain.mark(nc.vector.bn_stats(stats[:, t, :], source(t)))
    chain.wait()
    for t in range(PASS_TILES):
        chain.mark(nc.vector.bn_aggr(mv[:, t, :], stats[:, t, :]))
    chain.wait()
    chain.link(nc.vector.tensor_scalar(var[:, 0, :], mv[:, :, 1], eps, None, ALU.add))
    rsqrt(nc.vector, chain, var[:, 1, :], var[:, 0, :], var[:, 2, :])
    for t in range(PASS_TILES):
        last = nc.vector.tensor_scalar(out(t), source(t), mv[:, t, 0:1], var[:, 1, t:t + 1], ALU.subtract, ALU.mult)
        if t < PASS_TILES - 1:
            chain.mark(last)
    return last


def norm_all(nc, x_all, s_all, name):
    with ExitStack() as ctx:
        stats = ctx.enter_context(nc.sbuf_tensor(name + "_stats", [128, PASS_TILES, 6], F32))
        mv = ctx.enter_context(nc.sbuf_tensor(name + "_mv", [128, PASS_TILES, 2], F32))
        var = ctx.enter_context(nc.sbuf_tensor(name + "_var", [128, 3, PASS_TILES], F32))
        own = ctx.enter_context(nc.semaphore(name + "_own_vector"))
        ctx.callback(clear, nc, [own])
        block = ctx.enter_context(nc.Block())

        @block.vector
        def _(dve):
            chain = Chain(dve, own)
            with dve.Fori(0, PASSES) as p:
                def tile(source):
                    return lambda t: source[:, bass.ds(p * PASS_TOK + 128 * t, 128)]
                chain.link(layer_norm_tiles(nc, dve, chain, tile(x_all), tile(s_all), (stats, mv, var)))
                chain.reset()


def add_all(nc, x_all, s_all):
    with nc.Block() as block:
        half = TILES * DIM // 2

        @block.vector
        def _(dve):
            nc.vector.tensor_tensor(x_all[:, 0:half], x_all[:, 0:half], s_all[:, 0:half], ALU.add)

        @block.gpsimd
        def _(pool):
            nc.gpsimd.tensor_tensor(x_all[:, half:], x_all[:, half:], s_all[:, half:], ALU.add)


def cross_attention(nc, x_all, ident, ident_bf, dram):
    SCALE = HEAD_DIM ** -0.5
    MASKED = 3e38
    CHUNKS = PASS_TILES * 2
    UNITS = 12
    UNIT_BANKS = (0, 1, 5, 6)
    with ExitStack() as ctx:
        def sb(name, shape, dt=F32):
            return ctx.enter_context(nc.sbuf_tensor("x_" + name, shape, dt))

        used = []

        def sem(name):
            used.append(ctx.enter_context(nc.semaphore("x_" + name)))
            return used[-1]

        bank = [ctx.enter_context(nc.psum_tensor(f"x_bank{i}", [128, 512], F32)) for i in range(8)]
        w_q = sb("w_q", [128, INNER])
        w_kv = sb("w_kv", [128, 2 * INNER])
        w_out = sb("w_out", [128, PAIRS, DIM])
        b_out = sb("b_out", [1, DIM])
        ctx_all = sb("ctx_all", [128, BATCH * CTX])
        mask_in = sb("mask_in", [1, BATCH * CTX], U8)
        mask_f = sb("mask_f", [1, BATCH * CTX])
        mask_b = sb("mask_b", [1, BATCH, CTX], BF16)
        mask_4 = sb("mask_4", [1, 2, 4, CTX], BF16)
        ones = sb("ones", [1, 128])
        ones_b = sb("ones_b", [1, 128], BF16)
        work = (sb("stats", [128, PASS_TILES, 6]), sb("mv", [128, PASS_TILES, 2]), sb("var", [128, 3, PASS_TILES]))
        xn = sb("xn", [128, PASS_TOK])
        xn_t = sb("xn_t", [128, PASS_TOK])
        ctx_t = sb("ctx_t", [128, 2 * CTX])
        k_t = sb("k_t", [128, PAIRS, 2 * CTX])
        v = sb("v", [128, 2, 512])
        q_t = sb("q_t", [128, PAIRS, PASS_TOK])
        score = sb("score", [128, 2, GROUP, CTX])
        stat = sb("stat", [128, 3, GROUP])
        prob = sb("prob", [128, GROUP, CTX])
        prob_t = sb("prob_t", [128, 4, 128])
        out_t = sb("out_t", [128, PAIRS, PASS_TOK])

        loaded, consts, mask_made, own_v = sem("loaded"), sem("consts"), sem("mask_made"), sem("own_vector")
        normed, x_turned, xn_t_made, ctx_taken = sem("normed"), sem("x_turned"), sem("xn_t_made"), sem("ctx_taken")
        unit_done, unit_made = sem("unit_done"), sem("unit_made")
        scores_done, score_banks_free, exped = sem("scores_done"), sem("score_banks_free"), sem("exped")
        prob_made, prob_turned, prob_t_made = sem("prob_made"), sem("prob_turned"), sem("prob_t_made")
        mixed, mix_out, o_done, o_added = sem("mixed"), sem("mix_out"), sem("o_done"), sem("o_added")

        ctx.callback(clear, nc, used)
        block = ctx.enter_context(nc.Block())

        @block.sync
        def _(sp):
            for to, name in ((ctx_all, "ctx_t"), (w_q, "x_Wq"), (w_kv, "x_Wkv"), (b_out, "x_b"), (mask_in, "mask")):
                sp.dma_start(to[:, :], dram[name]).then_inc(loaded, 16)
            sp.dma_start(w_out[:, :, :], dram["x_Wout"]).then_inc(loaded, 16)

        @block.gpsimd
        def _(pool):
            nc.gpsimd.memset(ones[:, :], 1.0).then_inc(consts, 1)
            nc.gpsimd.memset(ones_b[:, :], 1.0).then_inc(consts, 1)
            pool.wait_ge(loaded, 96)
            pool.wait_ge(mask_made, 3)
            with pool.Fori(0, PASSES) as p:
                pool.wait_ge(scores_done, p * CHUNKS)
                nc.gpsimd.tensor_copy(mask_4[:, :, :, :], mask_b[:, bass.ds(p * 2, 2), :].unsqueeze(2).broadcast_to([1, 2, 4, CTX])).then_inc(ctx_taken, 1)
                nc.gpsimd.tensor_copy(ctx_t[:, :], ctx_all[:, bass.ds(p * 2 * CTX, 2 * CTX)]).then_inc(ctx_taken, 1)

        @block.tensor
        def _(pe):
            pe.wait_ge(loaded, 96)
            pe.wait_ge(consts, 2)
            with pe.Fori(0, PASSES) as p:
                pe.wait_ge(normed, p + 1)
                for t in range(PASS_TILES):
                    last = nc.tensor.transpose(bank[3][:, 128 * t:128 * t + 128], xn[:, 128 * t:128 * t + 128], ident[:, :])
                last.then_inc(x_turned, 1)
                pe.wait_ge(ctx_taken, p * 2 + 2)
                for u in range(UNITS):
                    to = bank[UNIT_BANKS[u % 4]]
                    if u >= 4:
                        pe.wait_ge(unit_made, p * UNITS + (u - 3))
                    if u < 2:
                        for b in range(4):
                            at = 128 * (4 * u + b)
                            last = nc.tensor.matmul(to[:, 128 * b:128 * b + 128], w_kv[:, at:at + 128], ctx_t[:, :], start=True, stop=True)
                    elif u < 4:
                        for n in range(2):
                            last = nc.tensor.matmul(to[64 * n:64 * n + 64, :], ctx_t[:, CTX * (u - 2):CTX * (u - 1)],
                                                    w_kv[:, INNER + 512 * n:INNER + 512 * n + 512], start=True, stop=True)
                    else:
                        if u == 4:
                            pe.wait_ge(xn_t_made, p + 1)
                        last = nc.tensor.matmul(to[:, :], w_q[:, 128 * (u - 4):128 * (u - 3)], xn_t[:, :], start=True, stop=True)
                    last.then_inc(unit_done, 1)
                pe.wait_ge(unit_made, p * UNITS + UNITS)

                def scores(j):
                    t, g = j // 2, j % 2
                    pe.wait_ge(score_banks_free, p * CHUNKS + (j + 1))
                    for n in range(2):
                        nc.tensor.matmul(bank[5 + n][:, 0:256], ones_b[:, :], mask_4[:, t // 2, :, :].rearrange("a b c -> a (b c)"), start=True, stop=True)
                    for b in range(4):
                        for n in range(2):
                            r = 64 * n
                            last = nc.tensor.matmul(bank[5 + n][:, 64 * b:64 * b + 64], q_t[r:r + 64, 4 * g + b, 128 * t:128 * t + 128],
                                                    k_t[r:r + 64, 4 * g + b, CTX * (t // 2):CTX * (t // 2) + CTX],
                                                    start=False, stop=True, skip_group_check=True)
                    last.then_inc(scores_done, 1)

                def turn_prob(j):
                    pe.wait_ge(prob_made, p * CHUNKS + (j + 1))
                    if j >= 1:
                        pe.wait_ge(prob_t_made, p * CHUNKS + j)
                    for b in range(4):
                        last = nc.tensor.transpose(bank[7][:, 128 * b:128 * b + 128], prob[:, 2 * b:2 * b + 2, :].rearrange("p a c -> p (a c)"), ident[:, :])
                    last.then_inc(prob_turned, 1)

                def mix(j):
                    t, g = j // 2, j % 2
                    pe.wait_ge(prob_t_made, p * CHUNKS + (j + 1))
                    if j >= 1:
                        pe.wait_ge(mix_out, p * CHUNKS + j)
                    alone(pe)
                    for b in range(4):
                        for n in range(2):
                            r = 64 * n
                            last = nc.tensor.matmul(bank[3][r:r + 64, 128 * b:128 * b + 128],
                                                    v[r:r + 64, t // 2, 64 * (4 * g + b):64 * (4 * g + b) + 64],
                                                    prob_t[r:r + 64, b, :], start=True, stop=True)
                    last.then_inc(mixed, 1)

                def project_out(t):
                    pe.wait_ge(mix_out, p * CHUNKS + 2 * (t + 1))
                    if t:
                        pe.wait_ge(o_added, p * PASS_TILES + t)
                    for b in range(PAIRS):
                        nc.tensor.matmul(bank[2][:, 0:128], out_t[:, b, 128 * t:128 * t + 128], w_out[:, b, :], start=(b == 0), stop=False)
                    nc.tensor.matmul(bank[2][:, 0:128], ones[:, :], b_out[:, :], start=False, stop=True).then_inc(o_done, 1)

                for i in range(CHUNKS + 3):
                    if i < CHUNKS:
                        scores(i)
                    if 1 <= i <= CHUNKS:
                        turn_prob(i - 1)
                    if 2 <= i <= CHUNKS + 1:
                        mix(i - 2)
                    if i >= 4 and i % 2 == 0:
                        project_out((i - 4) // 2)

        @block.vector
        def _(dve):
            chain = Chain(dve, own_v)
            dve.sem_inc(score_banks_free, 1)
            dve.wait_ge(loaded, 96)
            nc.vector.tensor_copy(mask_f[:, :], mask_in[:, :]).then_inc(mask_made, 1)
            dve.wait_ge(mask_made, 1)
            nc.vector.tensor_scalar(mask_f[:, :], mask_f[:, :], 1.0, MASKED, ALU.subtract, ALU.mult).then_inc(mask_made, 1)
            dve.wait_ge(mask_made, 2)
            nc.vector.tensor_copy(mask_b[:, :, :], mask_f[:, :].rearrange("a (b c) -> a b c", c=CTX)).then_inc(mask_made, 1)
            with dve.Fori(0, PASSES) as p:
                dve.wait_ge(x_turned, p)
                layer_norm_tiles(nc, dve, chain, lambda t: x_all[:, bass.ds(p * PASS_TOK + 128 * t, 128)],
                                 lambda t: xn[:, 128 * t:128 * t + 128], work).then_inc(normed, 1)

                def soften(j):
                    dve.wait_ge(scores_done, p * CHUNKS + (j + 1))
                    heads = score[:, j % 2, :, :].rearrange("p (b n) c -> p b n c", n=2)
                    top = stat[:, 0, :].rearrange("p (b n) -> p b n", n=2)
                    for n in range(2):
                        chain.mark(nc.vector.tensor_reduce(top[:, :, n], bank[5 + n][:, 0:256].rearrange("p (b c) -> p b c", c=64), AX_X, ALU.max))
                    chain.wait()
                    for n in range(2):
                        last = nc.vector.tensor_tensor(heads[:, :, n, :], bank[5 + n][:, 0:256].rearrange("p (b c) -> p b c", c=64),
                                                       over(top[:, :, n], [128, 4, 64]), ALU.subtract)
                        if n == 0:
                            chain.mark(last)
                    last.then_inc(score_banks_free, 1)

                def normalise(j):
                    dve.wait_ge(exped, p * CHUNKS + (j + 1))
                    chain.link(nc.vector.tensor_reduce(stat[:, 1, :], score[:, j % 2, :, :], AX_X, ALU.add))
                    chain.link(nc.vector.reciprocal(stat[:, 2, :], stat[:, 1, :]))
                    if j >= 1:
                        dve.wait_ge(prob_turned, p * CHUNKS + j)
                    nc.vector.tensor_tensor(prob[:, :, :], score[:, j % 2, :, :], over(stat[:, 2, :], [128, GROUP, 64]), ALU.mult).then_inc(prob_made, 1)

                for i in range(CHUNKS + 3):
                    if i < CHUNKS:
                        soften(i)
                    if 1 <= i <= CHUNKS:
                        normalise(i - 1)
                    if i >= 4 and i % 2 == 0:
                        t = (i - 4) // 2
                        dve.wait_ge(o_done, p * PASS_TILES + (t + 1))
                        tile = x_all[:, bass.ds(p * PASS_TOK + 128 * t, 128)]
                        nc.vector.tensor_tensor(tile, tile, bank[2][:, 0:128], ALU.add).then_inc(o_added, 1)
                chain.reset()

        @block.scalar
        def _(act):
            with act.Fori(0, PASSES) as p:
                for u in range(UNITS):
                    if u == 4:
                        act.wait_ge(x_turned, p + 1)
                        nc.scalar.activation(xn_t[:, :], bank[3][:, :], ACT.Copy).then_inc(xn_t_made, 1)
                    if u == 0:
                        act.wait_ge(mixed, p * CHUNKS)
                    act.wait_ge(unit_done, p * UNITS + (u + 1))
                    source = bank[UNIT_BANKS[u % 4]][:, :]
                    if u < 2:
                        to, source = k_t[:, 4 * u:4 * u + 4, :], source.rearrange("p (b n) -> p b n", b=4)
                    elif u < 4:
                        to = v[:, u - 2, :]
                    else:
                        to = q_t[:, u - 4, :]
                    nc.scalar.activation(to, source, ACT.Copy).then_inc(unit_made, 1)
                for i in range(CHUNKS + 2):
                    if i < CHUNKS:
                        act.wait_ge(score_banks_free, p * CHUNKS + (i + 2))
                        nc.scalar.activation(score[:, i % 2, :, :], score[:, i % 2, :, :], ACT.Exp, scale=SCALE).then_inc(exped, 1)
                    if 1 <= i <= CHUNKS:
                        j = i - 1
                        act.wait_ge(prob_turned, p * CHUNKS + (j + 1))
                        if j >= 1:
                            act.wait_ge(mixed, p * CHUNKS + j)
                        nc.scalar.activation(prob_t[:, :, :], bank[7][:, :].rearrange("p (b n) -> p b n", b=4), ACT.Copy).then_inc(prob_t_made, 1)
                    if i >= 2:
                        j = i - 2
                        t, g = j // 2, j % 2
                        act.wait_ge(mixed, p * CHUNKS + (j + 1))
                        nc.scalar.activation(out_t[:, 4 * g:4 * g + 4, 128 * t:128 * t + 128], bank[3][:, :].rearrange("p (b n) -> p b n", b=4), ACT.Copy).then_inc(mix_out, 1)


def shifted_layers(nc, x_all, ident, ident_bf, dram):
    DEPTH, WINDOW, QK_SCALE = 6, 32, 8.0
    HALF = 341
    CHUNKS = PASS_TILES * 2
    FF = [(0, 128), (128, 128), (256, 85)]
    ONES_ROW = 96
    with ExitStack() as ctx:
        def sb(name, shape, dt=F32):
            return ctx.enter_context(nc.sbuf_tensor("f_" + name, shape, dt))

        used = []

        def sem(name):
            used.append(ctx.enter_context(nc.semaphore("f_" + name)))
            return used[-1]

        bank = [ctx.enter_context(nc.psum_tensor(f"f_bank{i}", [128, 512], F32)) for i in range(8)]
        w_qkv = sb("w_qkv", [128, 3 * INNER])
        w_o = sb("w_o", [128, PAIRS, DIM])
        w_1 = sb("w_1", [128, 2 * HALF])
        w_2 = sb("w_2", [128, 3, DIM])
        cols = sb("cols", [128, 8])
        rot_const = sb("rot_const", [128, 2, 4, HEAD_DIM])
        head_scale = sb("head_scale", [128, 4, HEAD_DIM])
        rot = sb("rot", [128, 2, 4, HEAD_DIM])
        band_in = sb("band_in", [128, 2, 256])
        band = sb("band", [128, 2, 256], BF16)
        xw = sb("xw", [128, PASS_TOK])
        xs_t = sb("xs_t", [128, 2, SEQ])
        squares = sb("squares", [128, 2, 512])
        rot_a = sb("rot_a", [128, 2, 2, 512])
        rot_b = sb("rot_b", [128, 2, 2, 512])
        qk = sb("qk", [128, 2, 2, 512])
        norm = sb("norm", [128, 2, 16])
        norm_y = sb("norm_y", [128, 3, 16])
        q_t = sb("q_t", [128, 512])
        k_t = sb("k_t", [128, PAIRS, WINDOW + SEQ])
        v = sb("v", [128, 4, 512])
        v_off = sb("v_off", [128, 4, 512])
        score = sb("score", [128, GROUP, 64])
        prob = sb("prob", [128, GROUP, 64])
        stat = sb("stat", [128, 3, GROUP])
        prob_t = sb("prob_t", [128, GROUP, 64])
        out_t = sb("out_t", [128, PAIRS, PASS_TOK])
        fs_t = sb("fs_t", [128, 2, SEQ])
        f_stats = sb("f_stats", [128, PASS_TILES, 6])
        f_mv = sb("f_mv", [128, PASS_TILES, 2])
        f_var = sb("f_var", [128, 3, PASS_TILES])
        f_n = sb("f_n", [128, PASS_TOK])
        f_nt = sb("f_nt", [128, PASS_TOK])
        gate = sb("gate", [128, 3, PASS_TOK])
        hidden = sb("hidden", [128, 3, PASS_TOK])

        const_in = sem("const_in")
        w_qkv_in, w_o_in, w_ff_in, scale_in = sem("w_qkv_in"), sem("w_o_in"), sem("w_ff_in"), sem("scale_in")
        zeroed = sem("zeroed")
        own_v, own_s, own_p = sem("own_vector"), sem("own_scalar"), sem("own_pool")
        tables_made = sem("tables_made")
        x_taken, x_turned, xs_made = sem("x_taken"), sem("x_turned"), sem("xs_made")
        qk_proj, v_proj = sem("qk_proj"), sem("v_proj")
        squared = sem("squared")
        qk_free = sem("qk_free")
        v_made = sem("v_made")
        v_moved = [sem(f"v_moved{i}") for i in range(4)]
        v_carried = [sem(f"v_carried{i}") for i in range(2)]
        scaled = sem("scaled")
        norms_made = sem("norms_made")
        rot_free, q_rotated, k_rotated = sem("rot_free"), sem("q_rotated"), sem("k_rotated")
        qk_turned, qk_t_made = sem("qk_turned"), sem("qk_t_made")
        scores_done, maxed, shifted, exped = sem("scores_done"), sem("maxed"), sem("shifted"), sem("exped")
        score_banks_free = sem("score_banks_free")
        prob_made, prob_turned, prob_t_made = sem("prob_made"), sem("prob_turned"), sem("prob_t_made")
        mixed, mix_out = sem("mixed"), sem("mix_out")
        o_done, o_added = sem("o_done"), sem("o_added")
        f_turned, f_shifted, f_back, f_normed, f_again, f_affine = (
            sem("f_turned"), sem("f_shifted"), sem("f_back"), sem("f_normed"), sem("f_again"), sem("f_affine"))
        f_gate, f_up, f_gelu, f_hidden, f_done, x_stored = (
            sem("f_gate"), sem("f_up"), sem("f_gelu"), sem("f_hidden"), sem("f_done"), sem("x_stored"))

        def flat(i):
            return bank[i][:, :]

        ctx.callback(clear, nc, used)
        block = ctx.enter_context(nc.Block())

        @block.sync
        def _(sp):
            sp.dma_start(rot_const[:, :, :, :], dram["rot"]).then_inc(const_in, 16)
            sp.dma_start(band_in[:, :, :], dram["band"]).then_inc(const_in, 16)
            with sp.Fori(0, DEPTH) as layer:
                sp.wait_ge(v_proj, layer * (PASSES * CHUNKS))
                sp.dma_start(w_qkv[:, :], dram["Wqkv"][bass.ds(layer, 1)].rearrange("a p n -> (a p) n")).then_inc(w_qkv_in, 16)
                sp.wait_ge(tables_made, layer)
                sp.dma_start(head_scale[:, :, :], dram["qk_scale"][bass.ds(layer, 1)].rearrange("a p n d -> (a p) n d")).then_inc(scale_in, 16)
                sp.wait_ge(o_done, layer * (PASSES * PASS_TILES))
                sp.dma_start(w_o[:, :, :], dram["Wo"][bass.ds(layer, 1)].rearrange("a p n d -> (a p) n d")).then_inc(w_o_in, 16)
                sp.wait_ge(f_done, layer * PASSES)
                alone(sp)
                sp.wait_ge(f_hidden, layer * (PASSES * 3))
                sp.dma_start(w_1[:, :], dram["W1"][bass.ds(layer, 1)].rearrange("a p n -> (a p) n")).then_inc(w_ff_in, 16)
                sp.dma_start(w_2[:, :, :], dram["W2"][bass.ds(layer, 1)].rearrange("a p n d -> (a p) n d")).then_inc(w_ff_in, 16)
                sp.dma_start(cols[:, :], dram["cols"][bass.ds(layer, 1)].rearrange("a p n -> (a p) n")).then_inc(w_ff_in, 16)
                with sp.Fori(0, PASSES) as pair:
                    p = layer * PASSES + pair
                    for c in range(CHUNKS):
                        sp.wait_ge(v_made, p * CHUNKS + (c + 1))
                        sp.dma_start(v_off[32:128, c % 4, :], v[0:96, c % 4, :]).then_inc(v_moved[c % 4], 16)
                        if c % 4 < 2:
                            if c >= 2:
                                sp.wait_ge(mixed, p * CHUNKS + (c - 1))
                            sp.dma_start(v_off[0:32, c % 4 + 2, :], v[96:128, c % 4, :]).then_inc(v_carried[c % 2], 16)

        @block.tensor
        def _(pe):
            pe.wait_ge(const_in, 32)
            pe.wait_ge(zeroed, 4)
            with pe.Fori(0, DEPTH) as layer:
                pe.wait_ge(w_qkv_in, layer * 16 + 16)
                pe.wait_ge(w_o_in, layer * 16 + 16)
                pe.wait_ge(w_ff_in, layer * 48 + 48)
                alone(pe)
                with pe.Fori(0, PASSES) as pair:
                    p = layer * PASSES + pair

                    def turn_x(s):
                        for t in range(PASS_TILES):
                            last = nc.tensor.transpose(bank[3][:, 128 * t:128 * t + 128], xw[:, 128 * t:128 * t + 128], ident[:, :])
                        last.then_inc(s, 1)

                    def proj(i):
                        t, g = i // 2, i % 2
                        x_tile = xs_t[:, t // 2, 128 * (t % 2):128 * (t % 2) + 128]
                        for n in range(2):
                            pe.wait_ge(qk_free, p * (2 * CHUNKS) + (2 * i + n + 1))
                            nc.tensor.matmul(flat(n), x_tile, w_qkv[:, n * INNER + 512 * g:n * INNER + 512 * g + 512],
                                             start=True, stop=True).then_inc(qk_proj, 1)

                    def proj_v(i):
                        t, g = i // 2, i % 2
                        x_tile = xs_t[:, t // 2, 128 * (t % 2):128 * (t % 2) + 128]
                        pe.wait_ge(v_made, p * CHUNKS + i)
                        pe.wait_ge(o_added, p * PASS_TILES + max(0, (i - 3) // 2))
                        nc.tensor.matmul(flat(2), x_tile, w_qkv[:, 2 * INNER + 512 * g:2 * INNER + 512 * g + 512],
                                         start=True, stop=True).then_inc(v_proj, 1)

                    def turn_qk(j):
                        for n, ready in enumerate((q_rotated, k_rotated)):
                            pe.wait_ge(ready, p * CHUNKS + (j + 1))
                            if n == 0 and j >= 2:
                                pe.wait_ge(mix_out, p * (2 * CHUNKS) + 2 * (j - 1))
                            for b in range(4):
                                last = nc.tensor.transpose(bank[3 + n][:, 128 * b:128 * b + 128], qk[:, j % 2, n, 128 * b:128 * b + 128], ident[:, :])
                            last.then_inc(qk_turned, 1)

                    def turn_prob(j):
                        pe.wait_ge(prob_made, p * CHUNKS + (j + 1))
                        if j >= 1:
                            pe.wait_ge(prob_t_made, p * CHUNKS + j)
                        alone(pe)
                        for h in range(GROUP):
                            for b in range(2):
                                r = 64 * b
                                last = nc.tensor.matmul(bank[7][r:r + 64, 64 * h:64 * h + 64], prob[r:r + 64, h, :], ident[r:r + 64, r:r + 64], start=True, stop=True)
                        last.then_inc(prob_turned, 1)

                    def scores(j):
                        t, g = j // 2, j % 2
                        pe.wait_ge(score_banks_free, p * CHUNKS + (j + 1))
                        pe.wait_ge(qk_t_made, p * (2 * CHUNKS) + (2 * j + 2))
                        for n in range(2):
                            nc.tensor.matmul(bank[5 + n][:, 0:256], ident_bf[:, :], band[:, t % 2, :], start=True, stop=True)
                        for b in range(4):
                            for w in range(4):
                                for n in range(2):
                                    r = 64 * n
                                    at = WINDOW * (4 * (t % 2) + w)
                                    last = nc.tensor.matmul(
                                        bank[5 + n][32 * w:32 * w + 32, 64 * b:64 * b + 64],
                                        q_t[r:r + 64, 128 * b + 32 * w:128 * b + 32 * w + 32],
                                        k_t[r:r + 64, 4 * g + b, at:at + 64],
                                        start=False, stop=True, skip_group_check=True)
                        last.then_inc(scores_done, 1)

                    def mix(j):
                        t, g = j // 2, j % 2
                        pe.wait_ge(prob_t_made, p * CHUNKS + (j + 1))
                        pe.wait_ge(v_moved[j % 4], p * 32 + 16 * (j // 4 + 1))
                        if t % 2:
                            pe.wait_ge(v_carried[g], p * 32 + 16 * (j // 4 + 1))
                        if j < CHUNKS - 1:
                            pe.wait_ge(qk_t_made, p * (2 * CHUNKS) + (2 * j + 4))
                        alone(pe)
                        for h in range(GROUP):
                            for w in range(4):
                                r, o = 64 * (w // 2), 64 * (h % 2)
                                values = (v if w % 2 else v_off)[r:r + 64, j % 4, 64 * h:64 * h + 64]
                                last = nc.tensor.matmul(
                                    bank[3 + w // 2][o:o + 64, 64 * (h // 2) + 32 * (w % 2):64 * (h // 2) + 32 * (w % 2) + 32],
                                    values, prob_t[r:r + 64, h, 32 * (w % 2):32 * (w % 2) + 32],
                                    start=True, stop=True)
                        last.then_inc(mixed, 1)

                    def project_out(t):
                        pe.wait_ge(mix_out, p * (2 * CHUNKS) + 4 * (t + 1))
                        pe.wait_ge(v_made, p * CHUNKS + min(CHUNKS, 2 * t + 5))
                        if t:
                            pe.wait_ge(o_added, p * PASS_TILES + t)
                        for b in range(PAIRS):
                            last = nc.tensor.matmul(bank[2][:, 0:128], out_t[:, b, 128 * t:128 * t + 128], w_o[:, b, :],
                                                    start=(b == 0), stop=(b == PAIRS - 1))
                        last.then_inc(o_done, 1)

                    pe.wait_ge(x_taken, p + 1)
                    turn_x(x_turned)
                    pe.wait_ge(xs_made, p * 2 + 2)
                    for i in range(CHUNKS + 3):
                        if i < CHUNKS:
                            proj(i)
                            proj_v(i)
                        if 1 <= i <= CHUNKS:
                            turn_qk(i - 1)
                        if 2 <= i <= CHUNKS + 1:
                            turn_prob(i - 2)
                        if i >= 4 and i % 2 == 0:
                            project_out((i - 4) // 2)
                        if 1 <= i <= CHUNKS:
                            scores(i - 1)
                        if 2 <= i <= CHUNKS + 1:
                            mix(i - 2)
                    pe.wait_ge(o_added, p * PASS_TILES + PASS_TILES)
                    turn_x(f_turned)
                    pe.wait_ge(f_shifted, p * 2 + 2)
                    for t in range(PASS_TILES):
                        last = nc.tensor.transpose(bank[4][:, 128 * t:128 * t + 128], fs_t[:, t // 2, 128 * (t % 2):128 * (t % 2) + 128], ident[:, :])
                    last.then_inc(f_back, 1)
                    pe.wait_ge(f_normed, p + 1)
                    for t in range(PASS_TILES):
                        last = nc.tensor.transpose(bank[3][:, 128 * t:128 * t + 128], f_n[:, 128 * t:128 * t + 128], ident[:, :])
                    last.then_inc(f_again, 1)
                    pe.wait_ge(f_affine, p + 1)
                    for k, (at, n) in enumerate(FF):
                        nc.tensor.matmul(bank[k][0:n, :], w_1[:, HALF + at:HALF + at + n], f_nt[:, :], start=True, stop=True).then_inc(f_gate, 1)
                    for k, (at, n) in enumerate(FF):
                        nc.tensor.matmul(bank[5 + k][0:n, :], w_1[:, at:at + n], f_nt[:, :], start=True, stop=True).then_inc(f_up, 1)
                    pe.wait_ge(f_hidden, p * 3 + 3)
                    for t in range(PASS_TILES):
                        for k, rows in enumerate((128, 128, ONES_ROW + 1)):
                            last = nc.tensor.matmul(bank[4][:, 128 * t:128 * t + 128], hidden[0:rows, k, 128 * t:128 * t + 128], w_2[0:rows, k, :],
                                                    start=(k == 0), stop=(k == 2))
                    last.then_inc(f_done, 1)

        @block.vector
        def _(dve):
            chain = Chain(dve, own_v)
            chain.link(nc.vector.memset(xs_t[:, :, :], 0.0))
            chain.link(nc.vector.memset(fs_t[:, :, :], 0.0))
            chain.link(nc.vector.memset(hidden[:, :, :], 0.0))
            nc.vector.memset(k_t[:, :, :], 0.0).then_inc(zeroed, 1)
            nc.vector.memset(v_off[:, :, :], 0.0).then_inc(zeroed, 1)
            nc.vector.memset(hidden[ONES_ROW:ONES_ROW + 1, 2, :], 1.0).then_inc(zeroed, 1)
            dve.wait_ge(const_in, 32)
            nc.vector.tensor_copy(band[:, :, :], band_in[:, :, :]).then_inc(zeroed, 1)
            dve.wait_ge(zeroed, 4)
            dve.sem_inc(qk_free, 2)
            dve.sem_inc(score_banks_free, 1)
            chain.reset()
            with dve.Fori(0, DEPTH) as layer:
                dve.wait_ge(scale_in, layer * 16 + 16)
                nc.vector.tensor_tensor(rot[:, :, :, :], rot_const[:, :, :, :], head_scale[:, :, :].unsqueeze(1).broadcast_to([128, 2, 4, HEAD_DIM]), ALU.mult).then_inc(tables_made, 1)
                dve.wait_ge(tables_made, layer + 1)
                alone(dve)
                with dve.Fori(0, PASSES) as pair:
                    p = layer * PASSES + pair

                    def rotate(i):
                        half = (i // 2) % 2
                        dve.wait_ge(rot_free, p * CHUNKS + (i + 1))
                        for n in range(2):
                            dve.wait_ge(squared, p * (2 * CHUNKS) + (2 * i + n + 1))
                            source = flat(n).rearrange("p (h d) -> p h d", h=GROUP)
                            swapped = flat(n).rearrange("p (h s d) -> p h s d", h=GROUP, s=2)[:, :, ::-1, :]
                            c_tab = rot[:, half, 2 * n, :].unsqueeze(1).broadcast_to([128, GROUP, HEAD_DIM])
                            s_tab = rot[:, half, 2 * n + 1, :].rearrange("p (s d) -> p s d", s=2).unsqueeze(1).broadcast_to([128, GROUP, 2, 32])
                            chain.mark(nc.vector.tensor_tensor(rot_a[:, i % 2, n, :].rearrange("p (h d) -> p h d", h=GROUP), source, c_tab, ALU.mult))
                            nc.vector.tensor_tensor(rot_b[:, i % 2, n, :].rearrange("p (h s d) -> p h s d", h=GROUP, s=2), swapped, s_tab, ALU.mult).then_inc(qk_free, 1)
                        y = norm[:, i % 2, :]
                        if i >= 2:
                            dve.wait_ge(k_rotated, p * CHUNKS + (i - 1))
                        chain.link(nc.vector.tensor_reduce(norm_y[:, 0, :], squares[:, :, :].rearrange("p n (h d) -> p (n h) d", h=GROUP), AX_X, ALU.add))
                        chain.link(nc.vector.tensor_scalar(norm_y[:, 1, :], norm_y[:, 0, :], 1e-24, None, ALU.max))
                        rsqrt(nc.vector, chain, norm_y[:, 0, :], norm_y[:, 1, :], norm_y[:, 2, :])
                        nc.vector.tensor_copy(y, norm_y[:, 0, :]).then_inc(norms_made, 1)

                    def soften(j):
                        dve.wait_ge(scores_done, p * CHUNKS + (j + 1))
                        dve.wait_ge(norms_made, p * CHUNKS + (j + 1))
                        heads = score[:, :, :].rearrange("p (b n) c -> p b n c", n=2)
                        lengths = norm[:, j % 2, 0:GROUP].rearrange("p (b n) -> p b n", n=2)
                        for n in range(2):
                            last = nc.vector.tensor_tensor(heads[:, :, n, :], bank[5 + n][:, 0:256].rearrange("p (b c) -> p b c", c=64),
                                                           over(lengths[:, :, n], [128, 4, 64]), ALU.mult)
                            if n == 0:
                                chain.mark(last)
                        last.then_inc(score_banks_free, 1)
                        dve.wait_ge(score_banks_free, p * CHUNKS + (j + 2))
                        nc.vector.tensor_reduce(stat[:, 0, :], score[:, :, :], AX_X, ALU.max).then_inc(maxed, 1)

                    def normalise(j):
                        dve.wait_ge(exped, p * CHUNKS + (j + 1))
                        chain.link(nc.vector.tensor_reduce(stat[:, 1, :], score[:, :, :], AX_X, ALU.add))
                        chain.link(nc.vector.reciprocal(stat[:, 2, :], stat[:, 1, :]))
                        if j >= 1:
                            dve.wait_ge(prob_turned, p * CHUNKS + j)
                        nc.vector.tensor_tensor(prob[:, :, :], score[:, :, :], over(stat[:, 2, :], [128, GROUP, 64]), ALU.mult).then_inc(prob_made, 1)

                    for i in range(CHUNKS + 3):
                        if 2 <= i <= CHUNKS + 1:
                            normalise(i - 2)
                        if i < CHUNKS:
                            rotate(i)
                        if i >= 4 and i % 2 == 0:
                            t = (i - 4) // 2
                            dve.wait_ge(o_done, p * PASS_TILES + (t + 1))
                            nc.vector.tensor_tensor(xw[:, 128 * t:128 * t + 128], xw[:, 128 * t:128 * t + 128], bank[2][:, 0:128], ALU.add).then_inc(o_added, 1)
                        if 1 <= i <= CHUNKS:
                            soften(i - 1)
                    dve.wait_ge(f_back, p + 1)
                    for t in range(PASS_TILES):
                        chain.mark(nc.vector.bn_stats(f_stats[:, t, :], bank[4][:, 128 * t:128 * t + 128]))
                    chain.wait()
                    for t in range(PASS_TILES):
                        chain.mark(nc.vector.bn_aggr(f_mv[:, t, :], f_stats[:, t, :]))
                    chain.wait()
                    chain.link(nc.vector.tensor_scalar(f_var[:, 0, :], f_mv[:, :, 1], 1e-5, None, ALU.add))
                    rsqrt(nc.vector, chain, f_var[:, 1, :], f_var[:, 0, :], f_var[:, 2, :])
                    for t in range(PASS_TILES):
                        last = nc.vector.tensor_scalar(f_n[:, 128 * t:128 * t + 128], bank[4][:, 128 * t:128 * t + 128],
                                                       f_mv[:, t, 0:1], f_var[:, 1, t:t + 1], ALU.subtract, ALU.mult)
                        if t < PASS_TILES - 1:
                            chain.mark(last)
                    last.then_inc(f_normed, 1)
                    for k, (at, n) in enumerate(FF):
                        dve.wait_ge(f_up, p * 3 + (k + 1))
                        dve.wait_ge(f_gelu, p * 3 + (k + 1))
                        nc.vector.scalar_tensor_tensor(hidden[0:n, k, :], bank[5 + k][0:n, :], cols[0:n, 5 + k:6 + k], gate[0:n, k, :],
                                                       ALU.add, ALU.mult).then_inc(f_hidden, 1)
                    dve.wait_ge(f_done, p + 1)
                    nc.vector.tensor_tensor(x_all[:, bass.ds(pair * PASS_TOK, PASS_TOK)], xw[:, :], flat(4), ALU.add).then_inc(x_stored, 1)
                    chain.reset()

        @block.gpsimd
        def _(pool):
            chain = Chain(pool, own_p)
            pool.sem_inc(rot_free, 2)
            with pool.Fori(0, DEPTH) as layer:
                with pool.Fori(0, PASSES) as pair:
                    p = layer * PASSES + pair
                    pool.wait_ge(x_stored, p)
                    nc.gpsimd.tensor_copy(xw[:, :], x_all[:, bass.ds(pair * PASS_TOK, PASS_TOK)]).then_inc(x_taken, 1)

                    def sub_max(j):
                        pool.wait_ge(maxed, p * CHUNKS + (j + 1))
                        nc.gpsimd.tensor_tensor(score[:, :, :], score[:, :, :], over(stat[:, 0, :], [128, GROUP, 64]), ALU.subtract).then_inc(shifted, 1)

                    def add_up(i):
                        pool.wait_ge(qk_free, p * (2 * CHUNKS) + (2 * i + 3))
                        if i >= 2:
                            pool.wait_ge(qk_turned, p * (2 * CHUNKS) + (2 * i - 2))
                        nc.gpsimd.tensor_tensor(qk[:, i % 2, 0, :], rot_a[:, i % 2, 0, :], rot_b[:, i % 2, 0, :], ALU.add).then_inc(q_rotated, 1)
                        pool.wait_ge(qk_free, p * (2 * CHUNKS) + (2 * i + 4))
                        nc.gpsimd.tensor_tensor(qk[:, i % 2, 1, :], rot_a[:, i % 2, 1, :], rot_b[:, i % 2, 1, :], ALU.add).then_inc(rot_free, 1)
                        pool.wait_ge(rot_free, p * CHUNKS + (i + 3))
                        pool.wait_ge(norms_made, p * CHUNKS + (i + 1))
                        k_heads = qk[:, i % 2, 1, :].rearrange("p (h d) -> p h d", h=GROUP)
                        nc.gpsimd.tensor_tensor(k_heads, k_heads, over(norm[:, i % 2, GROUP:2 * GROUP], [128, GROUP, HEAD_DIM]), ALU.mult).then_inc(k_rotated, 1)

                    for i in range(CHUNKS + 2):
                        if 2 <= i:
                            sub_max(i - 2)
                        if i < CHUNKS:
                            add_up(i)

        @block.scalar
        def _(act):
            chain = Chain(act, own_s)
            act.wait_ge(zeroed, 4)
            with act.Fori(0, DEPTH) as layer:
                act.wait_ge(w_ff_in, layer * 48 + 48)
                with act.Fori(0, PASSES) as pair:
                    p = layer * PASSES + pair

                    def shift_in(s, to, ready):
                        act.wait_ge(ready, p + 1)
                        source = bank[3][:, :].rearrange("p (s n) -> p s n", s=2)
                        nc.scalar.activation(to[0:64, :, :], source[0:64, :, :], ACT.Copy).then_inc(s, 1)
                        nc.scalar.activation(to[64:128, :, 1:SEQ], source[64:128, :, 0:SEQ - 1], ACT.Copy).then_inc(s, 1)

                    shift_in(xs_made, xs_t, x_turned)
                    for i in range(CHUNKS + 2):
                        if 2 <= i:
                            j = i - 2
                            act.wait_ge(shifted, p * CHUNKS + (j + 1))
                            nc.scalar.activation(score[:, :, :], score[:, :, :], ACT.Exp, scale=QK_SCALE).then_inc(exped, 1)
                        if i < CHUNKS:
                            act.wait_ge(norms_made, p * CHUNKS + i)
                            for n in range(2):
                                act.wait_ge(qk_proj, p * (2 * CHUNKS) + (2 * i + n + 1))
                                nc.scalar.activation(squares[:, n, :], flat(n), ACT.Square).then_inc(squared, 1)
                            act.wait_ge(v_proj, p * CHUNKS + (i + 1))
                            act.wait_ge(v_moved[i % 4], p * 32 + 16 * (i // 4))
                            if i % 4 < 2:
                                act.wait_ge(v_carried[i % 2], p * 32 + 16 * (i // 4))
                            if i >= 4:
                                act.wait_ge(mixed, p * CHUNKS + (i - 3))
                            nc.scalar.activation(v[:, i % 4, :], flat(2), ACT.Copy).then_inc(v_made, 1)
                        if 1 <= i <= CHUNKS:
                            j = i - 1
                            t, g = j // 2, j % 2
                            act.wait_ge(qk_turned, p * (2 * CHUNKS) + (2 * j + 1))
                            if j >= 1:
                                act.wait_ge(scores_done, p * CHUNKS + j)
                            nc.scalar.activation(q_t[:, :], flat(3), ACT.Copy).then_inc(qk_t_made, 1)
                            act.wait_ge(qk_turned, p * (2 * CHUNKS) + (2 * j + 2))
                            at = WINDOW + 128 * (t % 2)
                            nc.scalar.activation(k_t[:, 4 * g:4 * g + 4, at:at + 128], flat(4).rearrange("p (b n) -> p b n", b=4), ACT.Copy).then_inc(qk_t_made, 1)
                        if 2 <= i:
                            j = i - 2
                            t, g = j // 2, j % 2
                            act.wait_ge(prob_turned, p * CHUNKS + (j + 1))
                            if j >= 1:
                                act.wait_ge(mixed, p * CHUNKS + j)
                            nc.scalar.activation(prob_t[:, :, :], flat(7).rearrange("p (h n) -> p h n", h=GROUP), ACT.Copy).then_inc(prob_t_made, 1)
                            act.wait_ge(mixed, p * CHUNKS + (j + 1))
                            for b in range(2):
                                at = 128 * t + 64 * b
                                nc.scalar.activation(out_t[:, 4 * g:4 * g + 4, at:at + 64], bank[3 + b][:, 0:256].rearrange("p (b n) -> p b n", b=4), ACT.Copy).then_inc(mix_out, 1)
                    shift_in(f_shifted, fs_t, f_turned)
                    act.wait_ge(f_again, p + 1)
                    nc.scalar.activation(f_nt[:, :], flat(3), ACT.Identity, scale=cols[:, 0:1], bias=cols[:, 1:2]).then_inc(f_affine, 1)
                    for k, (at, n) in enumerate(FF):
                        act.wait_ge(f_gate, p * 3 + (k + 1))
                        nc.scalar.activation(gate[0:n, k, :], bank[k][0:n, :], ACT.Gelu, bias=cols[0:n, 2 + k:3 + k]).then_inc(f_gelu, 1)

def kernel_attention(nc, x_all, ident, dram):
    M, EPS = 32, 1e-6
    with ExitStack() as ctx:
        def sb(name, shape, dt=F32):
            return ctx.enter_context(nc.sbuf_tensor("k_" + name, shape, dt))

        used = []

        def sem(name):
            used.append(ctx.enter_context(nc.semaphore("k_" + name)))
            return used[-1]

        bank = [ctx.enter_context(nc.psum_tensor(f"k_bank{i}", [128, 512], F32)) for i in range(6)]
        proj = sb("proj", [128, M])
        ctx_all = sb("ctx_all", [128, BATCH * CTX])
        ctx_rows = sb("ctx_rows", [CTX, BATCH, DIM])
        ctx_t = sb("ctx_t", [128, 2 * CTX])
        ctx_1 = sb("ctx_1", [CTX, 2, DIM + 1])
        work = (sb("stats", [128, PASS_TILES, 6]), sb("mv", [128, PASS_TILES, 2]), sb("var", [128, 3, PASS_TILES]))
        xn = sb("xn", [128, PASS_TOK])
        xn_t = sb("xn_t", [128, PASS_TOK])
        phi_q = sb("phi_q", [M, PASS_TOK])
        phi_k = sb("phi_k", [CTX, 2, M])
        kvz = sb("kvz", [M, 2, DIM + 1])
        den = sb("den", [128, 2, PASS_TILES])
        loaded, consts, own_v = sem("loaded"), sem("consts"), sem("own_vector")
        normed, x_turned, xn_t_made, ctx_taken = sem("normed"), sem("x_turned"), sem("xn_t_made"), sem("ctx_taken")
        k_done, k_exped, kv_done, kvz_made, q_done, q_exped = sem("k_done"), sem("k_exped"), sem("kv_done"), sem("kvz_made"), sem("q_done"), sem("q_exped")
        o_done, x_added = sem("o_done"), sem("x_added")
        ctx.callback(clear, nc, used)
        block = ctx.enter_context(nc.Block())

        @block.sync
        def _(sp):
            sp.dma_start(ctx_all[:, :], dram["ctx_t"]).then_inc(loaded, 16)
            sp.dma_start(ctx_rows[:, :, :], dram["ctx_rows"]).then_inc(loaded, 16)
            sp.dma_start(proj[:, :], dram["k_proj"]).then_inc(loaded, 16)

        @block.gpsimd
        def _(pool):
            nc.gpsimd.memset(ctx_1[:, :, :], 1.0).then_inc(consts, 1)
            pool.wait_ge(loaded, 48)
            pool.wait_ge(consts, 1)
            with pool.Fori(0, PASSES) as p:
                pool.wait_ge(kv_done, p)
                nc.gpsimd.tensor_copy(ctx_1[:, :, 0:DIM], ctx_rows[:, bass.ds(p * 2, 2), :]).then_inc(ctx_taken, 1)
                nc.gpsimd.tensor_copy(ctx_t[:, :], ctx_all[:, bass.ds(p * 2 * CTX, 2 * CTX)]).then_inc(ctx_taken, 1)

        @block.tensor
        def _(pe):
            pe.wait_ge(loaded, 48)
            with pe.Fori(0, PASSES) as p:
                pe.wait_ge(ctx_taken, p * 2 + 2)
                for b in range(2):
                    last = nc.tensor.matmul(bank[0][0:CTX, M * b:M * b + M], ctx_t[:, CTX * b:CTX * b + CTX], proj[:, :], start=True, stop=True)
                last.then_inc(k_done, 1)
                pe.wait_ge(k_exped, p + 1)
                alone(pe)
                for b in range(2):
                    last = nc.tensor.matmul(bank[1][0:M, 129 * b:129 * b + 129], phi_k[:, b, :], ctx_1[:, b, :], start=True, stop=True)
                last.then_inc(kv_done, 1)
                pe.wait_ge(normed, p + 1)
                for t in range(PASS_TILES):
                    last = nc.tensor.transpose(bank[2][:, 128 * t:128 * t + 128], xn[:, 128 * t:128 * t + 128], ident[:, :])
                last.then_inc(x_turned, 1)
                pe.wait_ge(xn_t_made, p + 1)
                nc.tensor.matmul(bank[3][0:M, :], proj[:, :], xn_t[:, :], start=True, stop=True).then_inc(q_done, 1)
                pe.wait_ge(q_exped, p + 1)
                pe.wait_ge(kvz_made, p + 1)
                for t in range(PASS_TILES):
                    last = nc.tensor.matmul(bank[4 + t // 2][:, 129 * (t % 2):129 * (t % 2) + 129], phi_q[:, 128 * t:128 * t + 128], kvz[:, t // 2, :], start=True, stop=True)
                last.then_inc(o_done, 1)

        @block.vector
        def _(dve):
            chain = Chain(dve, own_v)
            with dve.Fori(0, PASSES) as p:
                layer_norm_tiles(nc, dve, chain, lambda t: x_all[:, bass.ds(p * PASS_TOK + 128 * t, 128)],
                                 lambda t: xn[:, 128 * t:128 * t + 128], work).then_inc(normed, 1)
                dve.wait_ge(o_done, p + 1)
                for b in range(2):
                    sums = bank[4 + b][:, 0:258].rearrange("p (t n) -> p t n", n=129)[:, :, 128]
                    chain.mark(nc.vector.tensor_scalar(den[:, 0, 2 * b:2 * b + 2], sums, EPS, None, ALU.add))
                chain.wait()
                chain.link(nc.vector.reciprocal(den[:, 1, :], den[:, 0, :]))
                for t in range(PASS_TILES):
                    tile = x_all[:, bass.ds(p * PASS_TOK + 128 * t, 128)]
                    chain.mark(nc.vector.scalar_tensor_tensor(tile, bank[4 + t // 2][:, 129 * (t % 2):129 * (t % 2) + 128], den[:, 1, t:t + 1], tile, ALU.mult, ALU.add))
                chain.reset()

        @block.scalar
        def _(act):
            with act.Fori(0, PASSES) as p:
                act.wait_ge(k_done, p + 1)
                nc.scalar.activation(phi_k[:, :, :], bank[0][0:CTX, 0:2 * M].rearrange("p (b m) -> p b m", b=2), ACT.Exp, scale=DIM ** -0.5).then_inc(k_exped, 1)
                act.wait_ge(kv_done, p + 1)
                nc.scalar.activation(kvz[:, :, :], bank[1][0:M, 0:258].rearrange("p (b m) -> p b m", b=2), ACT.Copy, scale=M ** -0.5).then_inc(kvz_made, 1)
                act.wait_ge(x_turned, p + 1)
                nc.scalar.activation(xn_t[:, :], bank[2][:, :], ACT.Copy).then_inc(xn_t_made, 1)
                act.wait_ge(q_done, p + 1)
                nc.scalar.activation(phi_q[:, :], bank[3][0:M, :], ACT.Exp, scale=DIM ** -0.5).then_inc(q_exped, 1)


def quantise(nc, chain, out, value, work):
    chain.link(nc.vector.tensor_scalar(work, value, ROUND, None, ALU.add))
    chain.link(nc.vector.tensor_scalar(work, work, ROUND, -128.0, ALU.subtract, ALU.max))
    return nc.vector.tensor_scalar(out, work, 127.0, None, ALU.min)


def quantised_ffn(nc, x_all, s_all, ident, dram):
    QMAX = 127.0
    K = 3
    with ExitStack() as ctx:
        def sb(name, shape, dt=F32):
            return ctx.enter_context(nc.sbuf_tensor("q_" + name, shape, dt))

        used = []

        def sem(name):
            used.append(ctx.enter_context(nc.semaphore("q_" + name)))
            return used[-1]

        bank = [ctx.enter_context(nc.psum_tensor(f"q_bank{i}", [128, 512], F32)) for i in range(8)]
        w_gu = sb("w_gu", [128, 2 * K, DIM])
        w_d = sb("w_d", [128, K * 128])
        w_work = sb("w_work", [128, 2 * K * DIM])
        w_work2 = sb("w_work2", [128, 2 * K * DIM])
        w_gu_t = sb("w_gu_t", [128, 2 * K, 128], BF16)
        w_d_t = sb("w_d_t", [128, K, 128], BF16)
        clips = sb("clips", [128, 2])
        sig = sb("sig", [128, 2])
        top = sb("top", [128, 4])
        sc = sb("sc", [128, 2 * K + 1])
        inv = sb("inv", [128, 2 * K + 1])
        act_scale = sb("act_scale", [128, 4])
        gu_scale = sb("gu_scale", [128, 2 * K])
        diag = sb("diag", [128, 128])
        ones = sb("ones", [128, 128])
        out_scale = sb("out_scale", [128, 128])
        xi = sb("xi", [128, 2, PASS_TOK])
        xi_t = sb("xi_t", [128, PASS_TOK], BF16)
        gate = sb("gate", [128, K, PASS_TOK])
        h_all = sb("h_all", [128, K, TILES * 128])
        h_top = sb("h_top", [128, PASSES, K])
        h_work = sb("h_work", [128, K, PASS_TOK])
        h_int = sb("h_int", [128, K, PASS_TOK], BF16)
        y = sb("y", [128, PASS_TOK])

        loaded, own_v, own_p = sem("loaded"), sem("own_vector"), sem("own_pool")
        amax_made, amax_all, sig_made = sem("amax_made"), sem("amax_all"), sem("sig_made")
        w_rounded, w_turned, w_t_made, diag_made, d_spread = sem("w_rounded"), sem("w_turned"), sem("w_t_made"), sem("diag_made"), sem("d_spread")

        ctx.callback(clear, nc, used)
        with nc.Block() as block:

            @block.sync
            def _(sp):
                sp.dma_start(w_gu[:, :, :], dram["q_gu"]).then_inc(loaded, 16)
                sp.dma_start(w_d[:, :], dram["q_d"]).then_inc(loaded, 16)
                sp.dma_start(clips[:, :], dram["q_clips"]).then_inc(loaded, 16)

            @block.gpsimd
            def _(pool):
                nc.gpsimd.memset(ones[:, :], 1.0).then_inc(own_p, 1)
                pool.wait_ge(amax_made, 1)
                nc.gpsimd.partition_all_reduce(top[:, 1:2], top[:, 0:1], 128, bass.bass_isa.ReduceOp.max).then_inc(amax_all, 1)

            @block.scalar
            def _(act):
                act.wait_ge(loaded, 48)
                nc.scalar.activation(sig[:, :], clips[:, :], ACT.Sigmoid).then_inc(sig_made, 1)
                for k in range(2 * K):
                    act.wait_ge(w_turned, k + 1)
                    nc.scalar.activation(w_gu_t[:, k, :], bank[k][:, 0:128], ACT.Copy).then_inc(w_t_made, 1)
                for k in range(K):
                    act.wait_ge(w_turned, 2 * K + k + 1)
                    nc.scalar.activation(w_d_t[:, k, :], bank[6 + k % 2][:, 0:128], ACT.Copy).then_inc(w_t_made, 1)
                act.wait_ge(d_spread, 1)
                nc.scalar.activation(out_scale[:, :], bank[0][:, 0:128], ACT.Copy).then_inc(w_t_made, 1)

            @block.tensor
            def _(pe):
                pe.wait_ge(w_rounded, 1)
                for k in range(2 * K):
                    nc.tensor.transpose(bank[k][:, 0:128], w_work2[:, 128 * k:128 * k + 128], ident[:, :]).then_inc(w_turned, 1)
                pe.wait_ge(w_rounded, 2)
                for k in range(K):
                    if k == 2:
                        pe.wait_ge(w_t_made, 2 * K + 1)
                    nc.tensor.transpose(bank[6 + k % 2][:, 0:128], w_work[:, 128 * k:128 * k + 128], ident[:, :]).then_inc(w_turned, 1)
                pe.wait_ge(diag_made, 1)
                pe.wait_ge(own_p, 1)
                nc.tensor.matmul(bank[0][:, 0:128], ones[:, :], diag[:, :], start=True, stop=True).then_inc(d_spread, 1)

            @block.vector
            def _(dve):
                chain = Chain(dve, own_v)
                nc.vector.tensor_reduce(top[:, 0:1], s_all[:, :], AX_X, ALU.max, apply_absolute_value=True).then_inc(amax_made, 1)
                dve.wait_ge(loaded, 48)
                chain.mark(nc.vector.tensor_reduce(sc[:, 0:2 * K], w_gu[:, :, :], AX_X, ALU.max, apply_absolute_value=True))
                chain.link(nc.vector.tensor_reduce(sc[:, 2 * K:2 * K + 1], w_d[:, :], AX_X, ALU.max, apply_absolute_value=True))
                chain.link(nc.vector.tensor_scalar(sc[:, :], sc[:, :], 1 / QMAX, 1e-30, ALU.mult, ALU.max))
                chain.link(nc.vector.reciprocal(inv[:, :], sc[:, :]))
                shape = [128, 2 * K, DIM]
                chain.link(nc.vector.tensor_tensor(w_work[:, :].rearrange("p (k n) -> p k n", k=2 * K), w_gu[:, :, :], over(inv[:, 0:2 * K], shape), ALU.mult))
                quantise(nc, chain, w_work2[:, :], w_work[:, :], w_work[:, :]).then_inc(w_rounded, 1)
                dve.wait_ge(w_rounded, 1)
                chain.link(nc.vector.tensor_scalar(w_work[:, 0:K * 128], w_d[:, :], inv[:, 2 * K:2 * K + 1], None, ALU.mult))
                quantise(nc, chain, w_work[:, 0:K * 128], w_work[:, 0:K * 128], w_work[:, 0:K * 128]).then_inc(w_rounded, 1)
                nc.vector.tensor_scalar(diag[:, :], ident[:, :], sc[:, 2 * K:2 * K + 1], None, ALU.mult).then_inc(diag_made, 1)
                dve.wait_ge(sig_made, 1)
                dve.wait_ge(amax_all, 1)
                chain.link(nc.vector.tensor_tensor(act_scale[:, 0:1], sig[:, 0:1], top[:, 1:2], ALU.mult))
                chain.link(nc.vector.tensor_scalar(act_scale[:, 0:1], act_scale[:, 0:1], 1 / QMAX, None, ALU.mult))
                chain.link(nc.vector.reciprocal(act_scale[:, 1:2], act_scale[:, 0:1]))
                chain.link(nc.vector.tensor_scalar(gu_scale[:, :], sc[:, 0:2 * K], act_scale[:, 0:1], None, ALU.mult))

        with ExitStack() as loop:
            used_here = []

            def sem(name):
                used_here.append(loop.enter_context(nc.semaphore("qa_" + name)))
                return used_here[-1]

            own, x_rounded, x_turned, x_t_made, projected, silued, h_made = (
                sem("own"), sem("x_rounded"), sem("x_turned"), sem("x_t_made"), sem("projected"), sem("silued"), sem("h_made"))
            loop.callback(clear, nc, used_here)
            block = loop.enter_context(nc.Block())

            @block.vector
            def _(dve):
                chain = Chain(dve, own)
                with dve.Fori(0, PASSES) as p:
                    s = s_all[:, bass.ds(p * PASS_TOK, PASS_TOK)]
                    chain.link(nc.vector.tensor_scalar(xi[:, 1, :], s, act_scale[:, 1:2], None, ALU.mult))
                    quantise(nc, chain, xi[:, 0, :], xi[:, 1, :], xi[:, 1, :]).then_inc(x_rounded, 1)
                    for k in range(K):
                        dve.wait_ge(projected, p * (2 * K) + 2 * k + 2)
                        dve.wait_ge(silued, p * K + (k + 1))
                        h = h_all[:, k, bass.ds(p * PASS_TOK, PASS_TOK)]
                        nc.vector.scalar_tensor_tensor(h, bank[1 + 2 * k][:, :], gu_scale[:, K + k:K + k + 1], gate[:, k, :], ALU.mult, ALU.mult).then_inc(h_made, 1)
                        dve.wait_ge(h_made, p * K + (k + 1))
                        chain.link(nc.vector.tensor_reduce(h_top[:, bass.ds(p, 1), k], h, AX_X, ALU.max, apply_absolute_value=True))
                    chain.reset()

            @block.tensor
            def _(pe):
                with pe.Fori(0, PASSES) as p:
                    pe.wait_ge(x_rounded, p + 1)
                    for t in range(PASS_TILES):
                        last = nc.tensor.transpose(bank[7][:, 128 * t:128 * t + 128], xi[:, 0, 128 * t:128 * t + 128], ident[:, :])
                    last.then_inc(x_turned, 1)
                    pe.wait_ge(x_t_made, p + 1)
                    pe.wait_ge(h_made, p * K)
                    for k in range(K):
                        for n in range(2):
                            nc.tensor.matmul(bank[2 * k + n][:, :], w_gu_t[:, K * n + k, :], xi_t[:, :], start=True, stop=True).then_inc(projected, 1)

            @block.scalar
            def _(act):
                with act.Fori(0, PASSES) as p:
                    act.wait_ge(x_turned, p + 1)
                    nc.scalar.activation(xi_t[:, :], bank[7][:, :], ACT.Copy).then_inc(x_t_made, 1)
                    act.wait_ge(h_made, p * K)
                    for k in range(K):
                        act.wait_ge(projected, p * (2 * K) + 2 * k + 1)
                        nc.scalar.activation(gate[:, k, :], bank[2 * k][:, :], ACT.Silu, scale=gu_scale[:, k:k + 1]).then_inc(silued, 1)

        with ExitStack() as loop:
            used_here = []

            def sem(name):
                used_here.append(loop.enter_context(nc.semaphore("qb_" + name)))
                return used_here[-1]

            own, h_amax, h_all_max, h_rounded, downed, x_added = sem("own"), sem("h_amax"), sem("h_all_max"), sem("h_rounded"), sem("downed"), sem("x_added")
            loop.callback(clear, nc, used_here)
            block = loop.enter_context(nc.Block())

            @block.gpsimd
            def _(pool):
                pool.wait_ge(h_amax, 1)
                nc.gpsimd.partition_all_reduce(top[:, 3:4], top[:, 2:3], 128, bass.bass_isa.ReduceOp.max).then_inc(h_all_max, 1)

            @block.vector
            def _(dve):
                chain = Chain(dve, own)
                nc.vector.tensor_reduce(top[:, 2:3], h_top[:, :, :].rearrange("p a b -> p (a b)"), AX_X, ALU.max).then_inc(h_amax, 1)
                dve.wait_ge(h_all_max, 1)
                chain.link(nc.vector.tensor_tensor(act_scale[:, 2:3], sig[:, 1:2], top[:, 3:4], ALU.mult))
                chain.link(nc.vector.tensor_scalar(act_scale[:, 2:3], act_scale[:, 2:3], 1 / QMAX, None, ALU.mult))
                chain.link(nc.vector.reciprocal(act_scale[:, 3:4], act_scale[:, 2:3]))
                chain.link(nc.vector.tensor_scalar(out_scale[:, :], out_scale[:, :], act_scale[:, 2:3], None, ALU.mult))
                chain.reset()
                with dve.Fori(0, PASSES) as p:
                    dve.wait_ge(downed, p)
                    for k in range(K):
                        h = h_all[:, k, bass.ds(p * PASS_TOK, PASS_TOK)]
                        chain.link(nc.vector.tensor_scalar(h_work[:, k, :], h, act_scale[:, 3:4], None, ALU.mult))
                        quantise(nc, chain, h_int[:, k, :], h_work[:, k, :], h_work[:, k, :]).then_inc(h_rounded, 1)
                    dve.wait_ge(downed, p + 1)
                    chain.link(nc.vector.tensor_tensor(y[:, :].rearrange("p (t n) -> p t n", n=128), bank[0][:, :].rearrange("p (t n) -> p t n", n=128),
                                                       out_scale[:, :].unsqueeze(1).broadcast_to([128, PASS_TILES, 128]), ALU.mult))
                    x = x_all[:, bass.ds(p * PASS_TOK, PASS_TOK)]
                    nc.vector.tensor_tensor(x, x, y[:, :], ALU.add).then_inc(x_added, 1)
                    chain.reset()

            @block.tensor
            def _(pe):
                with pe.Fori(0, PASSES) as p:
                    pe.wait_ge(h_rounded, p * K + K)
                    pe.wait_ge(x_added, p)
                    for t in range(PASS_TILES):
                        for k in range(K):
                            last = nc.tensor.matmul(bank[0][:, 128 * t:128 * t + 128], h_int[:, k, 128 * t:128 * t + 128], w_d_t[:, k, :], start=(k == 0), stop=(k == K - 1))
                    last.then_inc(downed, 1)


def two_attentions(nc, x_all, ident, ident_bf, dram):
    EPS, LEAK = 1e-3, 0.2
    SELF_SCALE, CTX_SCALE = SEQ ** -0.5, CTX ** -0.5
    W_NAMES = ("a_Wk1", "a_Wq1", "a_Wv1", "a_Wk2", "a_Wq2", "a_Wv2", "a_W1", "a_W2")
    WK1, WQ1, WV1, WK2, WQ2, WV2, W1, W2 = range(8)
    with ExitStack() as ctx:
        def sb(name, shape, dt=F32):
            return ctx.enter_context(nc.sbuf_tensor("a_" + name, shape, dt))

        used = []

        def sem(name):
            used.append(ctx.enter_context(nc.semaphore("a_" + name)))
            return used[-1]

        bank = [ctx.enter_context(nc.psum_tensor(f"a_bank{i}", [128, 512], F32)) for i in range(8)]
        w = sb("w", [128, 8, DIM])
        rows = sb("rows", [128, 3, DIM])
        GAMMA, BETA, B2 = range(3)
        b1 = sb("b1", [128, 1])
        causal_in = sb("causal_in", [128, 128])
        causal = sb("causal", [128, 128], BF16)
        ctx_all = sb("ctx_all", [128, BATCH * CTX])
        ctx_t = sb("ctx_t", [128, 2 * CTX])
        work = (sb("stats", [128, PASS_TILES, 6]), sb("mv", [128, PASS_TILES, 2]), sb("var", [128, 3, PASS_TILES]))
        xn = sb("xn", [128, PASS_TOK])
        xn_t = sb("xn_t", [128, PASS_TOK])
        k1 = sb("k1", [128, PASS_TOK])
        q1 = sb("q1", [128, PASS_TOK])
        v1 = sb("v1", [128, PASS_TOK])
        k2 = sb("k2", [128, 2 * CTX])
        v2 = sb("v2", [CTX, 2, DIM])
        top = sb("top", [128, 2, PASS_TILES])
        total = sb("total", [128, 2, PASS_TILES])
        prob = sb("prob", [128, PASS_TILES, SEQ])
        prob_t = sb("prob_t", [128, 6, 128])
        att = sb("att", [128, PASS_TOK])
        att_t = sb("att_t", [128, PASS_TOK])
        q2 = sb("q2", [128, PASS_TOK])
        y = sb("y", [128, 3, PASS_TOK])
        n1 = sb("n1", [128, PASS_TOK])
        n2 = sb("n2", [128, PASS_TOK])
        n2_t = sb("n2_t", [128, PASS_TOK])
        s2 = sb("s2", [128, PASS_TILES, CTX])
        top2 = sb("top2", [128, 3, PASS_TILES])
        s2_t = sb("s2_t", [CTX, PASS_TOK])
        h = sb("h", [128, 2, PASS_TOK])

        loaded, causal_made, own_v = sem("loaded"), sem("causal_made"), sem("own_vector")
        normed, x_turned, xn_t_made, ctx_taken = sem("normed"), sem("x_turned"), sem("xn_t_made"), sem("ctx_taken")
        projected, kq_made, v1_made, kv2_made = sem("projected"), sem("kq_made"), sem("v1_made"), sem("kv2_made")
        s1_done, top_made, exp_made, p_turned, p_t_made, att_done, att_made = (
            sem("s1_done"), sem("top_made"), sem("exp_made"), sem("p_turned"), sem("p_t_made"), sem("att_done"), sem("att_made"))
        att_turned, att_t_made, q2_done, q2_made, s2_done, s2_sub, s2_exp, s2_turned, s2_t_made, att2_done = (
            sem("att_turned"), sem("att_t_made"), sem("q2_done"), sem("q2_made"), sem("s2_done"), sem("s2_sub"), sem("s2_exp"), sem("s2_turned"), sem("s2_t_made"), sem("att2_done"))
        n2_made, n2_turned, n2_t_made, h_done, h_made, ff_done = (
            sem("n2_made"), sem("n2_turned"), sem("n2_t_made"), sem("h_done"), sem("h_made"), sem("ff_done"))
        ctx.callback(clear, nc, used)
        block = ctx.enter_context(nc.Block())
        BLOCKS = [(t, b) for t in range(PASS_TILES) for b in range(t % 2 + 1)]
        SCORE_BANK = (5, 6, 7, 0)

        def tile(ap, t):
            return ap[:, 128 * t:128 * t + 128]

        @block.sync
        def _(sp):
            for n, name in enumerate(W_NAMES):
                sp.dma_start(w[:, n, :], dram[name]).then_inc(loaded, 16)
            sp.dma_start(rows[:, :, :], dram["a_rows"]).then_inc(loaded, 16)
            sp.dma_start(b1[:, :], dram["a_b1"]).then_inc(loaded, 16)
            sp.dma_start(causal_in[:, :], dram["causal"]).then_inc(loaded, 16)
            sp.dma_start(ctx_all[:, :], dram["ctx_t"]).then_inc(loaded, 16)

        @block.gpsimd
        def _(pool):
            pool.wait_ge(loaded, 192)
            with pool.Fori(0, PASSES) as p:
                pool.wait_ge(kv2_made, p)
                nc.gpsimd.tensor_copy(ctx_t[:, :], ctx_all[:, bass.ds(p * 2 * CTX, 2 * CTX)]).then_inc(ctx_taken, 1)

        @block.tensor
        def _(pe):
            pe.wait_ge(loaded, 192)
            pe.wait_ge(causal_made, 1)
            with pe.Fori(0, PASSES) as p:
                def turn(to, source, signal):
                    for t in range(PASS_TILES):
                        last = nc.tensor.transpose(tile(bank[to], t), tile(source, t), ident[:, :])
                    last.then_inc(signal, 1)

                pe.wait_ge(ctx_taken, p + 1)
                nc.tensor.matmul(bank[4][:, 0:128], w[:, WK2, :], ctx_t[:, :], start=True, stop=True)
                for b in range(2):
                    last = nc.tensor.matmul(bank[4][0:CTX, 128 + 128 * b:256 + 128 * b], ctx_t[:, CTX * b:CTX * b + CTX], w[:, WV2, :], start=True, stop=True)
                last.then_inc(projected, 1)
                pe.wait_ge(normed, p + 1)
                turn(0, xn, x_turned)
                pe.wait_ge(xn_t_made, p + 1)
                nc.tensor.matmul(bank[1][:, :], w[:, WK1, :], xn_t[:, :], start=True, stop=True).then_inc(projected, 1)
                nc.tensor.matmul(bank[2][:, :], w[:, WQ1, :], xn_t[:, :], start=True, stop=True).then_inc(projected, 1)
                for t in range(PASS_TILES):
                    last = nc.tensor.matmul(tile(bank[3], t), tile(xn_t, t), w[:, WV1, :], start=True, stop=True)
                last.then_inc(projected, 1)
                pe.wait_ge(kq_made, p * 2 + 2)
                for t in range(PASS_TILES):
                    to, n = bank[SCORE_BANK[t]], 128 * (t % 2 + 1)
                    nc.tensor.matmul(to[:, n - 128:n], ident_bf[:, :], causal[:, :], start=True, stop=True)
                    at = SEQ * (t // 2)
                    nc.tensor.matmul(to[:, 0:n], tile(q1, t), k1[:, at:at + n], start=False, stop=True, skip_group_check=True).then_inc(s1_done, 1)
                pe.wait_ge(exp_made, p * PASS_TILES + PASS_TILES)
                for n, (t, b) in enumerate(BLOCKS):
                    last = nc.tensor.transpose(bank[1 + n // 4][:, 128 * (n % 4):128 * (n % 4) + 128], prob[:, t, 128 * b:128 * b + 128], ident[:, :])
                last.then_inc(p_turned, 1)
                pe.wait_ge(v1_made, p + 1)
                pe.wait_ge(p_t_made, p * 2 + 2)
                for n, (t, b) in enumerate(BLOCKS):
                    last = nc.tensor.matmul(tile(bank[3], t), prob_t[:, n, :], tile(v1, t - t % 2 + b), start=(b == 0), stop=(b == t % 2))
                last.then_inc(att_done, 1)
                pe.wait_ge(att_made, p + 1)
                turn(0, att, att_turned)
                pe.wait_ge(att_t_made, p + 1)
                nc.tensor.matmul(bank[1][:, :], w[:, WQ2, :], att_t[:, :], start=True, stop=True).then_inc(q2_done, 1)
                pe.wait_ge(q2_made, p + 1)
                pe.wait_ge(kv2_made, p + 1)
                for t in range(PASS_TILES):
                    b = t // 2
                    last = nc.tensor.matmul(bank[2][:, CTX * t:CTX * t + CTX], tile(q2, t), k2[:, CTX * b:CTX * b + CTX], start=True, stop=True)
                last.then_inc(s2_done, 1)
                pe.wait_ge(s2_exp, p + 1)
                alone(pe)
                for t in range(PASS_TILES):
                    last = nc.tensor.transpose(bank[5][0:CTX, 128 * t:128 * t + 128], s2[:, t, :], ident[:, :])
                last.then_inc(s2_turned, 1)
                pe.wait_ge(s2_t_made, p + 1)
                for t in range(PASS_TILES):
                    last = nc.tensor.matmul(tile(bank[6], t), tile(s2_t, t), v2[:, t // 2, :], start=True, stop=True)
                last.then_inc(att2_done, 1)
                pe.wait_ge(n2_made, p + 1)
                turn(0, n2, n2_turned)
                pe.wait_ge(n2_t_made, p + 1)
                nc.tensor.matmul(bank[1][:, :], w[:, W1, :], n2_t[:, :], start=True, stop=True).then_inc(h_done, 1)
                pe.wait_ge(h_made, p + 1)
                for t in range(PASS_TILES):
                    last = nc.tensor.matmul(tile(bank[2], t), h[:, 1, 128 * t:128 * t + 128], w[:, W2, :], start=True, stop=True)
                last.then_inc(ff_done, 1)

        @block.vector
        def _(dve):
            chain = Chain(dve, own_v)
            dve.wait_ge(loaded, 192)
            nc.vector.tensor_copy(causal[:, :], causal_in[:, :]).then_inc(causal_made, 1)
            tiles = [128, PASS_TILES, 128]

            def row(n):
                return rows[:, n, :].unsqueeze(1).broadcast_to(tiles)

            def by_tile(ap):
                return ap.rearrange("p (t n) -> p t n", n=128)

            def affine_norm(source, out):
                chain.link(layer_norm_tiles(nc, dve, chain, lambda t: source[:, 128 * t:128 * t + 128], lambda t: y[:, 1, 128 * t:128 * t + 128], work, EPS))
                chain.link(nc.vector.tensor_tensor(by_tile(y[:, 2, :]), by_tile(y[:, 1, :]), row(GAMMA), ALU.mult))
                return nc.vector.tensor_tensor(by_tile(out), by_tile(y[:, 2, :]), row(BETA), ALU.add)

            with dve.Fori(0, PASSES) as p:
                layer_norm_tiles(nc, dve, chain, lambda t: x_all[:, bass.ds(p * PASS_TOK + 128 * t, 128)],
                                 lambda t: xn[:, 128 * t:128 * t + 128], work).then_inc(normed, 1)
                dve.wait_ge(projected, p * 4 + 1)
                chain.mark(nc.vector.tensor_copy(k2[:, :], bank[4][:, 0:128]))
                nc.vector.tensor_copy(v2[:, :, :], bank[4][0:CTX, 128:384].rearrange("p (b n) -> p b n", b=2)).then_inc(kv2_made, 1)
                dve.wait_ge(projected, p * 4 + 4)
                nc.vector.tensor_copy(v1[:, :], bank[3][:, :]).then_inc(v1_made, 1)
                for t in range(PASS_TILES):
                    dve.wait_ge(s1_done, p * PASS_TILES + (t + 1))
                    chain.link(nc.vector.tensor_reduce(top[:, 0, t:t + 1], bank[SCORE_BANK[t]][:, 0:128 * (t % 2 + 1)], AX_X, ALU.max))
                    nc.vector.tensor_scalar(top[:, 1, t:t + 1], top[:, 0, t:t + 1], -SELF_SCALE, None, ALU.mult).then_inc(top_made, 1)
                dve.wait_ge(exp_made, p * PASS_TILES + PASS_TILES)
                chain.link(nc.vector.reciprocal(total[:, 1, :], total[:, 0, :]))
                dve.wait_ge(att_done, p + 1)
                nc.vector.tensor_tensor(by_tile(att[:, :]), by_tile(bank[3][:, :]), over(total[:, 1, :], tiles), ALU.mult).then_inc(att_made, 1)
                dve.wait_ge(att_made, p + 1)
                chain.link(nc.vector.tensor_tensor(y[:, 0, :], att[:, :], xn[:, :], ALU.add))
                chain.link(affine_norm(y[:, 0, :], n1[:, :]))
                dve.wait_ge(s2_done, p + 1)
                scores = bank[2][:, 0:PASS_TILES * CTX].rearrange("p (t n) -> p t n", n=CTX)
                chain.link(nc.vector.tensor_reduce(top2[:, 0, :], scores, AX_X, ALU.max))
                nc.vector.tensor_tensor(s2[:, :, :], scores, over(top2[:, 0, :], [128, PASS_TILES, CTX]), ALU.subtract).then_inc(s2_sub, 1)
                dve.wait_ge(s2_exp, p + 1)
                chain.link(nc.vector.tensor_reduce(top2[:, 1, :], s2[:, :, :], AX_X, ALU.add))
                chain.link(nc.vector.reciprocal(top2[:, 2, :], top2[:, 1, :]))
                dve.wait_ge(att2_done, p + 1)
                chain.link(nc.vector.tensor_tensor(by_tile(y[:, 0, :]), by_tile(bank[6][:, :]), over(top2[:, 2, :], tiles), ALU.mult))
                chain.link(nc.vector.tensor_tensor(y[:, 0, :], y[:, 0, :], n1[:, :], ALU.add))
                affine_norm(y[:, 0, :], n2[:, :]).then_inc(n2_made, 1)
                dve.wait_ge(h_done, p + 1)
                chain.link(nc.vector.tensor_scalar(h[:, 0, :], bank[1][:, :], b1[:, :], None, ALU.add))
                nc.vector.scalar_tensor_tensor(h[:, 1, :], h[:, 0, :], LEAK, h[:, 0, :], ALU.mult, ALU.max).then_inc(h_made, 1)
                dve.wait_ge(ff_done, p + 1)
                chain.link(nc.vector.tensor_tensor(by_tile(y[:, 0, :]), by_tile(bank[2][:, :]), row(B2), ALU.add))
                chain.link(nc.vector.tensor_tensor(y[:, 0, :], y[:, 0, :], n2[:, :], ALU.add))
                chain.link(affine_norm(y[:, 0, :], n1[:, :]))
                x = x_all[:, bass.ds(p * PASS_TOK, PASS_TOK)]
                chain.link(nc.vector.scalar_tensor_tensor(x, n1[:, :], 0.0, x, ALU.max, ALU.add))
                chain.reset()

        @block.scalar
        def _(act):
            with act.Fori(0, PASSES) as p:
                def take(ready, count, to, source, signal):
                    act.wait_ge(ready, count)
                    nc.scalar.activation(to, source, ACT.Copy).then_inc(signal, 1)

                take(x_turned, p + 1, xn_t[:, :], bank[0][:, :], xn_t_made)
                take(projected, p * 4 + 2, k1[:, :], bank[1][:, :], kq_made)
                take(projected, p * 4 + 3, q1[:, :], bank[2][:, :], kq_made)
                for t in range(PASS_TILES):
                    act.wait_ge(top_made, p * PASS_TILES + (t + 1))
                    n = 128 * (t % 2 + 1)
                    nc.scalar.activation(prob[:, t, 0:n], bank[SCORE_BANK[t]][:, 0:n], ACT.Exp, bias=top[:, 1, t:t + 1], scale=SELF_SCALE,
                                         accum_out=total[:, 0, t:t + 1]).then_inc(exp_made, 1)
                take(p_turned, p + 1, prob_t[:, 0:4, :], bank[1][:, :].rearrange("p (b n) -> p b n", n=128), p_t_made)
                take(p_turned, p + 1, prob_t[:, 4:6, :], bank[2][:, 0:256].rearrange("p (b n) -> p b n", n=128), p_t_made)
                take(att_turned, p + 1, att_t[:, :], bank[0][:, :], att_t_made)
                take(q2_done, p + 1, q2[:, :], bank[1][:, :], q2_made)
                act.wait_ge(s2_sub, p + 1)
                nc.scalar.activation(s2[:, :, :], s2[:, :, :], ACT.Exp, scale=CTX_SCALE).then_inc(s2_exp, 1)
                take(s2_turned, p + 1, s2_t[:, :], bank[5][0:CTX, :], s2_t_made)
                take(n2_turned, p + 1, n2_t[:, :], bank[0][:, :], n2_t_made)


def ternary_ffn(nc, x_all, ident, dram):
    HID, K = 512, 4
    with ExitStack() as ctx:
        def sb(name, shape, dt=F32):
            return ctx.enter_context(nc.sbuf_tensor("g_" + name, shape, dt))

        used = []

        def sem(name):
            used.append(ctx.enter_context(nc.semaphore("g_" + name)))
            return used[-1]

        bank = [ctx.enter_context(nc.psum_tensor(f"g_bank{i}", [128, 512], F32)) for i in range(8)]
        w = sb("w", [128, 2, HID])
        w_cmp = sb("w_cmp", [128, 2, HID])
        w_tern = sb("w_tern", [128, 2, HID])
        size = sb("size", [128, 2, 4])
        affine = sb("affine", [128, 2, K])
        work = (sb("stats", [128, PASS_TILES, 6]), sb("mv", [128, PASS_TILES, 2]), sb("var", [128, 3, PASS_TILES]))
        xn = sb("xn", [128, PASS_TOK])
        xn_t = sb("xn_t", [128, PASS_TOK])
        h = sb("h", [128, PASS_TILES, HID])
        hn = sb("hn", [128, PASS_TILES, HID])
        hn_t = sb("hn_t", [128, K, PASS_TOK])
        loaded, own_v, own_w, sized, size_sum, tern_made = sem("loaded"), sem("own_vector"), sem("own_weights"), sem("sized"), sem("size_sum"), sem("tern_made")
        normed, x_turned, xn_t_made, h_done, gelued, h_normed, h_turned, hn_t_made, o_done, x_added = (
            sem("normed"), sem("x_turned"), sem("xn_t_made"), sem("h_done"), sem("gelued"), sem("h_normed"), sem("h_turned"), sem("hn_t_made"), sem("o_done"), sem("x_added"))
        ctx.callback(clear, nc, used)
        block = ctx.enter_context(nc.Block())

        @block.sync
        def _(sp):
            sp.dma_start(w[:, 0, :], dram["g_fc"]).then_inc(loaded, 16)
            sp.dma_start(w[:, 1, :], dram["g_proj"]).then_inc(loaded, 16)
            sp.dma_start(affine[:, :, :], dram["g_affine"]).then_inc(loaded, 16)

        @block.gpsimd
        def _(pool):
            pool.wait_ge(sized, 1)
            nc.gpsimd.partition_all_reduce(size[:, :, 1], size[:, :, 0], 128, bass.bass_isa.ReduceOp.add).then_inc(size_sum, 1)

        @block.tensor
        def _(pe):
            pe.wait_ge(tern_made, 1)
            with pe.Fori(0, PASSES) as p:
                pe.wait_ge(normed, p + 1)
                for t in range(PASS_TILES):
                    last = nc.tensor.transpose(bank[0][:, 128 * t:128 * t + 128], xn[:, 128 * t:128 * t + 128], ident[:, :])
                last.then_inc(x_turned, 1)
                pe.wait_ge(xn_t_made, p + 1)
                for t in range(PASS_TILES):
                    nc.tensor.matmul(bank[1 + t][:, :], xn_t[:, 128 * t:128 * t + 128], w_tern[:, 0, :], start=True, stop=True).then_inc(h_done, 1)
                pe.wait_ge(h_normed, p * PASS_TILES + PASS_TILES)
                for k in range(K):
                    to = bank[5 + k % 3]
                    if k == 3:
                        pe.wait_ge(hn_t_made, p * K + 1)
                    for t in range(PASS_TILES):
                        last = nc.tensor.transpose(to[:, 128 * t:128 * t + 128], hn[:, t, 128 * k:128 * k + 128], ident[:, :])
                    last.then_inc(h_turned, 1)
                pe.wait_ge(hn_t_made, p * K + K)
                for t in range(PASS_TILES):
                    for k in range(K):
                        last = nc.tensor.matmul(bank[0][:, 128 * t:128 * t + 128], hn_t[:, k, 128 * t:128 * t + 128], w_tern[:, 1, 128 * k:128 * k + 128],
                                                start=(k == 0), stop=(k == K - 1))
                last.then_inc(o_done, 1)

        @block.vector
        def _(dve):
            weights = Chain(dve, own_w)
            dve.wait_ge(loaded, 48)
            nc.vector.tensor_reduce(size[:, :, 0], w[:, :, :], AX_X, ALU.add, apply_absolute_value=True).then_inc(sized, 1)
            dve.wait_ge(size_sum, 1)
            weights.link(nc.vector.tensor_scalar(size[:, :, 2], size[:, :, 1], 1.0 / (HID * DIM), 1e-6, ALU.mult, ALU.add))
            weights.link(nc.vector.reciprocal(size[:, :, 3], size[:, :, 2]))
            for n in range(2):
                weights.mark(nc.vector.tensor_scalar(w_cmp[:, n, :], w[:, n, :], size[:, n, 3:4], -0.5, ALU.mult, ALU.is_lt))
                weights.link(nc.vector.tensor_scalar(w_tern[:, n, :], w[:, n, :], size[:, n, 3:4], 0.5, ALU.mult, ALU.is_gt))
            nc.vector.tensor_tensor(w_tern[:, :, :], w_tern[:, :, :], w_cmp[:, :, :], ALU.subtract).then_inc(tern_made, 1)
            chain = Chain(dve, own_v)
            with dve.Fori(0, PASSES) as p:
                layer_norm_tiles(nc, dve, chain, lambda t: x_all[:, bass.ds(p * PASS_TOK + 128 * t, 128)],
                                 lambda t: xn[:, 128 * t:128 * t + 128], work).then_inc(normed, 1)
                stats, mv, var = work
                dve.wait_ge(normed, p + 1)
                for t in range(PASS_TILES):
                    dve.wait_ge(gelued, p * PASS_TILES + (t + 1))
                    chain.mark(nc.vector.bn_stats(stats[:, t, :], h[:, t, :]))
                chain.wait()
                for t in range(PASS_TILES):
                    chain.mark(nc.vector.bn_aggr(mv[:, t, :], stats[:, t, :]))
                chain.wait()
                chain.link(nc.vector.tensor_scalar(var[:, 0, :], mv[:, :, 1], 1e-5, None, ALU.add))
                rsqrt(nc.vector, chain, var[:, 1, :], var[:, 0, :], var[:, 2, :])
                for t in range(PASS_TILES):
                    nc.vector.tensor_scalar(hn[:, t, :], h[:, t, :], mv[:, t, 0:1], var[:, 1, t:t + 1], ALU.subtract, ALU.mult).then_inc(h_normed, 1)
                dve.wait_ge(o_done, p + 1)
                x = x_all[:, bass.ds(p * PASS_TOK, PASS_TOK)]
                nc.vector.tensor_tensor(x, x, bank[0][:, :], ALU.add).then_inc(x_added, 1)
                dve.wait_ge(x_added, p + 1)
                alone(dve)
                chain.reset()

        @block.scalar
        def _(act):
            act.wait_ge(loaded, 48)
            with act.Fori(0, PASSES) as p:
                act.wait_ge(x_turned, p + 1)
                nc.scalar.activation(xn_t[:, :], bank[0][:, :], ACT.Copy).then_inc(xn_t_made, 1)
                for t in range(PASS_TILES):
                    act.wait_ge(h_done, p * PASS_TILES + (t + 1))
                    nc.scalar.activation(h[:, t, :], bank[1 + t][:, :], ACT.Gelu).then_inc(gelued, 1)
                for k in range(K):
                    act.wait_ge(h_turned, p * K + (k + 1))
                    nc.scalar.activation(hn_t[:, k, :], bank[5 + k % 3][:, :], ACT.Identity, scale=affine[:, 0, k:k + 1], bias=affine[:, 1, k:k + 1]).then_inc(hn_t_made, 1)


def context_attention(nc, x_all, ident, dram):
    with ExitStack() as ctx:
        def sb(name, shape, dt=F32):
            return ctx.enter_context(nc.sbuf_tensor("y_" + name, shape, dt))

        used = []

        def sem(name):
            used.append(ctx.enter_context(nc.semaphore("y_" + name)))
            return used[-1]

        bank = [ctx.enter_context(nc.psum_tensor(f"y_bank{i}", [128, 512], F32)) for i in range(5)]
        w = sb("w", [128, DIM])
        b = sb("b", [128, 1])
        ctx_t = sb("ctx_t", [128, BATCH * CTX])
        ctx_rows = sb("ctx_rows", [CTX, BATCH, DIM])
        work = (sb("stats", [128, PASS_TILES, 6]), sb("mv", [128, PASS_TILES, 2]), sb("var", [128, 3, PASS_TILES]))
        xn = sb("xn", [128, PASS_TOK])
        xn_t = sb("xn_t", [128, PASS_TOK])
        proj_t = sb("proj_t", [128, PASS_TOK])
        score = sb("score", [128, PASS_TILES, CTX])
        stat = sb("stat", [128, 3, PASS_TILES])
        score_t = sb("score_t", [CTX, PASS_TOK])
        loaded, own_v = sem("loaded"), sem("own_vector")
        normed, x_turned, xn_t_made, proj_done, proj_made, s_done, s_sub, s_exp, s_turned, s_t_made, o_done = (
            sem("normed"), sem("x_turned"), sem("xn_t_made"), sem("proj_done"), sem("proj_made"), sem("s_done"), sem("s_sub"), sem("s_exp"), sem("s_turned"), sem("s_t_made"), sem("o_done"))
        ctx.callback(clear, nc, used)
        block = ctx.enter_context(nc.Block())

        @block.sync
        def _(sp):
            sp.dma_start(w[:, :], dram["y_W"]).then_inc(loaded, 16)
            sp.dma_start(b[:, :], dram["y_b"]).then_inc(loaded, 16)
            sp.dma_start(ctx_t[:, :], dram["ctx_t"]).then_inc(loaded, 16)
            sp.dma_start(ctx_rows[:, :, :], dram["ctx_rows"]).then_inc(loaded, 16)

        @block.tensor
        def _(pe):
            pe.wait_ge(loaded, 64)
            with pe.Fori(0, PASSES) as p:
                pe.wait_ge(normed, p + 1)
                for t in range(PASS_TILES):
                    last = nc.tensor.transpose(bank[0][:, 128 * t:128 * t + 128], xn[:, 128 * t:128 * t + 128], ident[:, :])
                last.then_inc(x_turned, 1)
                pe.wait_ge(xn_t_made, p + 1)
                nc.tensor.matmul(bank[1][:, :], w[:, :], xn_t[:, :], start=True, stop=True).then_inc(proj_done, 1)
                pe.wait_ge(proj_made, p + 1)
                for t in range(PASS_TILES):
                    last = nc.tensor.matmul(bank[2][:, CTX * t:CTX * t + CTX], proj_t[:, 128 * t:128 * t + 128],
                                            ctx_t[:, bass.ds(p * (2 * CTX) + CTX * (t // 2), CTX)], start=True, stop=True)
                last.then_inc(s_done, 1)
                pe.wait_ge(s_exp, p + 1)
                alone(pe)
                for t in range(PASS_TILES):
                    last = nc.tensor.transpose(bank[3][0:CTX, 128 * t:128 * t + 128], score[:, t, :], ident[:, :])
                last.then_inc(s_turned, 1)
                pe.wait_ge(s_t_made, p + 1)
                for t in range(PASS_TILES):
                    last = nc.tensor.matmul(bank[4][:, 128 * t:128 * t + 128], score_t[:, 128 * t:128 * t + 128],
                                            ctx_rows[:, bass.ds(p * 2 + t // 2, 1), :].rearrange("p a n -> p (a n)"), start=True, stop=True)
                last.then_inc(o_done, 1)

        @block.vector
        def _(dve):
            chain = Chain(dve, own_v)
            with dve.Fori(0, PASSES) as p:
                layer_norm_tiles(nc, dve, chain, lambda t: x_all[:, bass.ds(p * PASS_TOK + 128 * t, 128)],
                                 lambda t: xn[:, 128 * t:128 * t + 128], work).then_inc(normed, 1)
                dve.wait_ge(s_done, p + 1)
                scores = bank[2][:, 0:PASS_TILES * CTX].rearrange("p (t n) -> p t n", n=CTX)
                chain.link(nc.vector.tensor_reduce(stat[:, 0, :], scores, AX_X, ALU.max))
                nc.vector.tensor_tensor(score[:, :, :], scores, over(stat[:, 0, :], [128, PASS_TILES, CTX]), ALU.subtract).then_inc(s_sub, 1)
                dve.wait_ge(s_exp, p + 1)
                chain.link(nc.vector.tensor_reduce(stat[:, 1, :], score[:, :, :], AX_X, ALU.add))
                chain.link(nc.vector.reciprocal(stat[:, 2, :], stat[:, 1, :]))
                dve.wait_ge(o_done, p + 1)
                for t in range(PASS_TILES):
                    x = x_all[:, bass.ds(p * PASS_TOK + 128 * t, 128)]
                    chain.mark(nc.vector.scalar_tensor_tensor(x, bank[4][:, 128 * t:128 * t + 128], stat[:, 2, t:t + 1], x, ALU.mult, ALU.add))
                chain.reset()

        @block.scalar
        def _(act):
            act.wait_ge(loaded, 64)
            with act.Fori(0, PASSES) as p:
                act.wait_ge(x_turned, p + 1)
                nc.scalar.activation(xn_t[:, :], bank[0][:, :], ACT.Copy).then_inc(xn_t_made, 1)
                act.wait_ge(proj_done, p + 1)
                nc.scalar.activation(proj_t[:, :], bank[1][:, :], ACT.Identity, bias=b[:, :]).then_inc(proj_made, 1)
                act.wait_ge(s_sub, p + 1)
                nc.scalar.activation(score[:, :, :], score[:, :, :], ACT.Exp).then_inc(s_exp, 1)
                act.wait_ge(s_turned, p + 1)
                nc.scalar.activation(score_t[:, :], bank[3][0:CTX, :], ACT.Copy).then_inc(s_t_made, 1)


EXPERTS = 8
FF = 512
CHUNKS = FF // 128
CAPACITY = BATCH * SEQ // EXPERTS
TOP_BIT = 29


def experts(nc, x_all, ident, dram):
    with ExitStack() as ctx:
        weight = ctx.enter_context(nc.sbuf_tensor("e_weight", [128, TILES * EXPERTS], F32))
        xn_t_all = ctx.enter_context(nc.sbuf_tensor("e_xn_t_all", [128, TILES * 128], F32))
        w1 = ctx.enter_context(nc.sbuf_tensor("e_w1", [128, EXPERTS, FF], F32))
        w2 = ctx.enter_context(nc.sbuf_tensor("e_w2", [128, EXPERTS, CHUNKS, DIM], F32))
        b1 = ctx.enter_context(nc.sbuf_tensor("e_b1", [128, EXPERTS * CHUNKS], F32))
        b2 = ctx.enter_context(nc.sbuf_tensor("e_b2", [EXPERTS, DIM], F32))
        w_in = ctx.enter_context(nc.semaphore("e_w_in"))
        ctx.callback(clear, nc, [w_in])
        route(nc, x_all, ident, dram, weight, xn_t_all, (w1, w2, b1, b2), w_in)
        choose(nc, weight)
        apply_experts(nc, x_all, ident, weight, xn_t_all, (w1, w2, b1, b2), w_in)


def route(nc, x_all, ident, dram, prob, xn_t_all, weights, w_in):
    with ExitStack() as ctx:
        def sb(name, shape, dt=F32):
            return ctx.enter_context(nc.sbuf_tensor("er_" + name, shape, dt))

        used = []

        def sem(name):
            used.append(ctx.enter_context(nc.semaphore("er_" + name)))
            return used[-1]

        bank = [ctx.enter_context(nc.psum_tensor(f"er_bank{i}", [128, 512], F32)) for i in range(2)]
        ws, bs, ones = sb("ws", [128, EXPERTS]), sb("bs", [1, EXPERTS]), sb("ones", [1, 128])
        work = (sb("stats", [128, PASS_TILES, 6]), sb("mv", [128, PASS_TILES, 2]), sb("var", [128, 3, PASS_TILES]))
        xn = sb("xn", [128, PASS_TOK])
        xn_t = sb("xn_t", [128, PASS_TOK])
        score = sb("score", [128, PASS_TILES, EXPERTS])
        stat = sb("stat", [128, 3, PASS_TILES])
        loaded, ones_set, own_v = sem("loaded"), sem("ones_set"), sem("own_vector")
        normed, x_turned, xn_t_made, xn_t_kept, s_done, s_sub, s_exp = (
            sem("normed"), sem("x_turned"), sem("xn_t_made"), sem("xn_t_kept"), sem("s_done"), sem("s_sub"), sem("s_exp"))
        ctx.callback(clear, nc, used)
        block = ctx.enter_context(nc.Block())

        @block.sync
        def _(sp):
            sp.dma_start(ws[:, :], dram["e_Ws"]).then_inc(loaded, 16)
            sp.dma_start(bs[:, :], dram["e_bs"]).then_inc(loaded, 16)
            for held, name in zip(weights, ("e_W1", "e_W2", "e_b1", "e_b2")):
                flat = held[:, :] if len(held.shape) == 2 else held[:, :, :] if len(held.shape) == 3 else held[:, :, :, :]
                sp.dma_start(flat, dram[name]).then_inc(w_in, 16)

        @block.gpsimd
        def _(pool):
            nc.gpsimd.memset(ones[:, :], 1.0).then_inc(ones_set, 1)
            with pool.Fori(0, PASSES) as p:
                pool.wait_ge(xn_t_made, p + 1)
                nc.gpsimd.tensor_copy(xn_t_all[:, bass.ds(p * PASS_TOK, PASS_TOK)], xn_t[:, :]).then_inc(xn_t_kept, 1)

        @block.tensor
        def _(pe):
            pe.wait_ge(loaded, 32)
            pe.wait_ge(ones_set, 1)
            with pe.Fori(0, PASSES) as p:
                pe.wait_ge(normed, p + 1)
                for t in range(PASS_TILES):
                    last = nc.tensor.transpose(bank[0][:, 128 * t:128 * t + 128], xn[:, 128 * t:128 * t + 128], ident[:, :])
                last.then_inc(x_turned, 1)
                pe.wait_ge(xn_t_made, p + 1)
                for t in range(PASS_TILES):
                    s = bank[1][:, EXPERTS * t:EXPERTS * t + EXPERTS]
                    nc.tensor.matmul(s, xn_t[:, 128 * t:128 * t + 128], ws[:, :], start=True, stop=False)
                    last = nc.tensor.matmul(s, ones[:, :], bs[:, :], start=False, stop=True)
                last.then_inc(s_done, 1)

        @block.vector
        def _(dve):
            chain = Chain(dve, own_v)
            with dve.Fori(0, PASSES) as p:
                layer_norm_tiles(nc, dve, chain, lambda t: x_all[:, bass.ds(p * PASS_TOK + 128 * t, 128)],
                                 lambda t: xn[:, 128 * t:128 * t + 128], work).then_inc(normed, 1)
                dve.wait_ge(s_done, p + 1)
                scores = bank[1][:, 0:PASS_TILES * EXPERTS].rearrange("p (t n) -> p t n", n=EXPERTS)
                chain.link(nc.vector.tensor_reduce(stat[:, 0, :], scores, AX_X, ALU.max))
                nc.vector.tensor_tensor(score[:, :, :], scores, over(stat[:, 0, :], [128, PASS_TILES, EXPERTS]), ALU.subtract).then_inc(s_sub, 1)
                dve.wait_ge(s_exp, p + 1)
                chain.link(nc.vector.tensor_reduce(stat[:, 1, :], score[:, :, :], AX_X, ALU.add))
                chain.link(nc.vector.reciprocal(stat[:, 2, :], stat[:, 1, :]))
                kept = prob[:, bass.ds(p * (PASS_TILES * EXPERTS), PASS_TILES * EXPERTS)].rearrange("p (t n) -> p t n", n=EXPERTS)
                chain.mark(nc.vector.tensor_tensor(kept, score[:, :, :], over(stat[:, 2, :], [128, PASS_TILES, EXPERTS]), ALU.mult))
                chain.reset()

        @block.scalar
        def _(act):
            with act.Fori(0, PASSES) as p:
                act.wait_ge(x_turned, p + 1)
                act.wait_ge(xn_t_kept, p)
                nc.scalar.activation(xn_t[:, :], bank[0][:, :], ACT.Copy).then_inc(xn_t_made, 1)
                act.wait_ge(s_sub, p + 1)
                nc.scalar.activation(score[:, :, :], score[:, :, :], ACT.Exp).then_inc(s_exp, 1)


def choose(nc, weight):
    with ExitStack() as ctx:
        def sb(name, shape, dt=F32):
            return ctx.enter_context(nc.sbuf_tensor("ec_" + name, shape, dt))

        used = []

        def sem(name):
            used.append(ctx.enter_context(nc.semaphore("ec_" + name)))
            return used[-1]

        bank = [ctx.enter_context(nc.psum_tensor(f"ec_bank{i}", [128, 512], F32)) for i in range(3)]
        ones, before = sb("ones", [128, 128]), sb("before", [128, 128])
        threshold, attempt, gain = sb("threshold", [128, EXPERTS], I32), sb("attempt", [128, EXPERTS], I32), sb("gain", [128, EXPERTS], I32)
        bit, bit_int = sb("bit", [128, 1]), sb("bit_int", [128, 1], I32)
        reached = sb("reached", [128, TILES, EXPERTS])
        equal = sb("equal", [128, TILES, EXPERTS])
        sums = [sb("sums0", [128, TILES, EXPERTS]), sb("sums1", [128, TILES, EXPERTS])]
        part = sb("part", [128, EXPERTS])
        left = sb("left", [128, EXPERTS])
        own_v, own_pool, tables, counted, total_done, above_counted, above_done, equal_marked, ranks_done = (
            sem("own_vector"), sem("own_pool"), sem("tables"), sem("counted"), sem("total_done"), sem("above_counted"), sem("above_done"),
            sem("equal_marked"), sem("ranks_done"))
        p3 = weight[:, :].rearrange("p (t n) -> p t n", n=EXPERTS)
        shape = [128, TILES, EXPERTS]

        def per_tile(ap):
            return ap.unsqueeze(1).broadcast_to(shape)

        ctx.callback(clear, nc, used)
        block = ctx.enter_context(nc.Block())

        @block.gpsimd
        def _(pool):
            nc.gpsimd.memset(ones[:, :], 1.0).then_inc(own_pool, 1)
            nc.gpsimd.memset(before[:, :], 0.0).then_inc(own_pool, 1)
            pool.wait_ge(own_pool, 2)
            nc.gpsimd.affine_select(out=before[:, :], in_=before[:, :], compare_op=ALU.is_ge, fill=1.0, base=0,
                                    pattern=[[-1, 128]], channel_multiplier=1).then_inc(tables, 1)

        @block.tensor
        def _(pe):
            pe.wait_ge(tables, 1)
            with pe.Fori(0, TOP_BIT + 1) as i:
                pe.wait_ge(counted, i + 1)
                nc.tensor.matmul(bank[0][:, 0:EXPERTS], ones[:, :], part[:, :], start=True, stop=True).then_inc(total_done, 1)
            pe.wait_ge(above_counted, 1)
            nc.tensor.matmul(bank[0][:, 0:EXPERTS], ones[:, :], part[:, :], start=True, stop=True).then_inc(above_done, 1)
            pe.wait_ge(equal_marked, 1)
            nc.tensor.matmul(bank[1][:, 0:TILES * EXPERTS], before[:, :], equal[:, :, :].rearrange("p t n -> p (t n)"), start=True, stop=True)
            nc.tensor.matmul(bank[2][:, 0:TILES * EXPERTS], ones[:, :], equal[:, :, :].rearrange("p t n -> p (t n)"), start=True, stop=True).then_inc(ranks_done, 1)

        @block.vector
        def _(dve):
            chain = Chain(dve, own_v)
            chain.mark(nc.vector.memset(threshold[:, :], 0))
            chain.link(nc.vector.memset(bit[:, :], float(2 ** TOP_BIT)))
            chain.reset()
            with dve.Fori(0, TOP_BIT + 1) as i:
                chain.link(nc.vector.tensor_copy(bit_int[:, :], bit[:, :]))
                chain.link(nc.vector.tensor_tensor(attempt[:, :], threshold[:, :], bit_int[:, :].broadcast_to([128, EXPERTS]), ALU.bitwise_or))
                chain.link(nc.vector.tensor_tensor(reached[:, :, :], p3, per_tile(attempt[:, :].bitcast(F32)), ALU.is_ge))
                nc.vector.tensor_reduce(part[:, :], reached[:, :, :].rearrange("p t n -> p n t"), AX_X, ALU.add).then_inc(counted, 1)
                dve.wait_ge(total_done, i + 1)
                chain.link(nc.vector.tensor_scalar(gain[:, :], bank[0][:, 0:EXPERTS], float(CAPACITY), bit[:, :], ALU.is_ge, ALU.mult))
                chain.mark(nc.vector.tensor_tensor(threshold[:, :], threshold[:, :], gain[:, :], ALU.bitwise_or))
                chain.mark(nc.vector.tensor_scalar(bit[:, :], bit[:, :], 0.5, None, ALU.mult))
                chain.reset()
            limit = per_tile(threshold[:, :].bitcast(F32))
            nc.vector.tensor_tensor(equal[:, :, :], p3, limit, ALU.is_equal).then_inc(equal_marked, 1)
            chain.link(nc.vector.tensor_tensor(reached[:, :, :], p3, limit, ALU.is_gt))
            nc.vector.tensor_reduce(part[:, :], reached[:, :, :].rearrange("p t n -> p n t"), AX_X, ALU.add).then_inc(above_counted, 1)
            dve.wait_ge(ranks_done, 1)
            chain.link(nc.vector.tensor_copy(sums[0][:, :, :].rearrange("p t n -> p (t n)"), bank[2][:, 0:TILES * EXPERTS]))
            step, now = 1, 0
            while step < TILES:
                a, b = sums[now], sums[1 - now]
                chain.mark(nc.vector.tensor_copy(b[:, 0:step, :], a[:, 0:step, :]))
                chain.link(nc.vector.tensor_tensor(b[:, step:, :], a[:, step:, :], a[:, 0:TILES - step, :], ALU.add))
                step, now = 2 * step, 1 - now
            a, b = sums[now], sums[1 - now]
            flat = [m[:, :, :].rearrange("p t n -> p (t n)") for m in (a, b)]
            chain.link(nc.vector.tensor_tensor(flat[1], flat[0], bank[2][:, 0:TILES * EXPERTS], ALU.subtract))
            chain.link(nc.vector.tensor_tensor(flat[1], flat[1], bank[1][:, 0:TILES * EXPERTS], ALU.add))
            dve.wait_ge(above_done, 1)
            chain.link(nc.vector.tensor_scalar(left[:, :], bank[0][:, 0:EXPERTS], -1.0, float(CAPACITY), ALU.mult, ALU.add))
            chain.link(nc.vector.tensor_tensor(b[:, :, :], b[:, :, :], per_tile(left[:, :]), ALU.is_lt))
            chain.link(nc.vector.tensor_tensor(b[:, :, :], b[:, :, :], equal[:, :, :], ALU.mult))
            chain.link(nc.vector.tensor_tensor(b[:, :, :], b[:, :, :], reached[:, :, :], ALU.add))
            nc.vector.tensor_tensor(p3, p3, b[:, :, :], ALU.mult)


def apply_experts(nc, x_all, ident, weight, xn_t_all, weights, w_in):
    w1, w2, b1, b2 = weights
    with ExitStack() as ctx:
        def sb(name, shape, dt=F32):
            return ctx.enter_context(nc.sbuf_tensor("ea_" + name, shape, dt))

        used = []

        def sem(name):
            used.append(ctx.enter_context(nc.semaphore("ea_" + name)))
            return used[-1]

        h_bank = [ctx.enter_context(nc.psum_tensor(f"ea_h_bank{i}", [128, 512], F32)) for i in range(CHUNKS)]
        o_bank = [ctx.enter_context(nc.psum_tensor(f"ea_o_bank{i}", [128, 512], F32)) for i in range(2)]
        b_bank = ctx.enter_context(nc.psum_tensor("ea_b_bank", [128, 512], F32))
        t_bank = ctx.enter_context(nc.psum_tensor("ea_t_bank", [128, 512], F32))
        h = sb("h", [128, 2, CHUNKS, PASS_TOK])
        w_now = sb("w_now", [128, PASS_TILES * EXPERTS])
        w_t = sb("w_t", [EXPERTS, PASS_TOK])
        acc = sb("acc", [128, PASS_TILES, DIM])
        own_v = sem("own_vector")
        w_ready, w_turned, w_t_made, bias_done, h_done, h_made, o_done, o_added = (
            sem("w_ready"), sem("w_turned"), sem("w_t_made"), sem("bias_done"), sem("h_done"), sem("h_made"), sem("o_done"), sem("o_added"))
        per_pass = EXPERTS * CHUNKS
        ctx.callback(clear, nc, used)
        block = ctx.enter_context(nc.Block())

        @block.tensor
        def _(pe):
            def first_product(p, e):
                for c in range(CHUNKS):
                    if e > 0:
                        pe.wait_ge(h_made, p * per_pass + (CHUNKS * (e - 1) + c + 1))
                    nc.tensor.matmul(h_bank[c][:, :], w1[:, e, 128 * c:128 * c + 128], xn_t_all[:, bass.ds(p * PASS_TOK, PASS_TOK)],
                                     start=True, stop=True).then_inc(h_done, 1)

            def second_product(p, e):
                pe.wait_ge(o_added, p * EXPERTS + max(e - 1, 0))
                pe.wait_ge(h_made, p * per_pass + CHUNKS * (e + 1))
                for t in range(PASS_TILES):
                    for c in range(CHUNKS):
                        last = nc.tensor.matmul(o_bank[e % 2][:, 128 * t:128 * t + 128], h[:, e % 2, c, 128 * t:128 * t + 128], w2[:, e, c, :],
                                                start=c == 0, stop=c == CHUNKS - 1)
                last.then_inc(o_done, 1)

            pe.wait_ge(w_in, 64)
            with pe.Fori(0, PASSES) as p:
                first_product(p, 0)
                pe.wait_ge(w_ready, p + 1)
                for t in range(PASS_TILES):
                    last = nc.tensor.transpose(t_bank[0:EXPERTS, 128 * t:128 * t + 128], w_now[:, EXPERTS * t:EXPERTS * t + EXPERTS], ident[:, :])
                last.then_inc(w_turned, 1)
                first_product(p, 1)
                pe.wait_ge(w_t_made, p + 1)
                for t in range(PASS_TILES):
                    last = nc.tensor.matmul(b_bank[:, 128 * t:128 * t + 128], w_t[:, 128 * t:128 * t + 128], b2[:, :], start=True, stop=True)
                last.then_inc(bias_done, 1)
                for e in range(1, EXPERTS):
                    second_product(p, e - 1)
                    if e + 1 < EXPERTS:
                        first_product(p, e + 1)
                second_product(p, EXPERTS - 1)

        @block.scalar
        def _(act):
            act.wait_ge(w_in, 64)
            with act.Fori(0, PASSES) as p:
                for e in range(EXPERTS):
                    for c in range(CHUNKS):
                        act.wait_ge(h_done, p * per_pass + (CHUNKS * e + c + 1))
                        at = CHUNKS * e + c
                        nc.scalar.activation(h[:, e % 2, c, :], h_bank[c][:, :], ACT.Gelu_apprx_tanh, bias=b1[:, at:at + 1]).then_inc(h_made, 1)
                    if e == 0:
                        act.wait_ge(w_turned, p + 1)
                        nc.scalar.activation(w_t[:, :], t_bank[0:EXPERTS, :], ACT.Copy).then_inc(w_t_made, 1)

        @block.vector
        def _(dve):
            chain = Chain(dve, own_v)
            with dve.Fori(0, PASSES) as p:
                nc.vector.tensor_copy(w_now[:, :], weight[:, bass.ds(p * (PASS_TILES * EXPERTS), PASS_TILES * EXPERTS)]).then_inc(w_ready, 1)
                dve.wait_ge(bias_done, p + 1)
                flat = acc[:, :, :].rearrange("p t n -> p (t n)")
                x = x_all[:, bass.ds(p * PASS_TOK, PASS_TOK)]
                chain.link(nc.vector.tensor_tensor(flat, b_bank[:, :], x, ALU.add))
                for e in range(EXPERTS):
                    if e > 0:
                        dve.wait_ge(o_added, p * EXPERTS + e)
                    dve.wait_ge(o_done, p * EXPERTS + (e + 1))
                    for t in range(PASS_TILES):
                        at = EXPERTS * t + e
                        last = nc.vector.scalar_tensor_tensor(acc[:, t, :], o_bank[e % 2][:, 128 * t:128 * t + 128], w_now[:, at:at + 1], acc[:, t, :], ALU.mult, ALU.add)
                    last.then_inc(o_added, 1)
                dve.wait_ge(o_added, p * EXPERTS + EXPERTS)
                alone(dve)
                chain.link(nc.vector.tensor_copy(x, flat))
                chain.reset()


def build(nc, arrays, out):
    with ExitStack() as ctx:
        x_all = ctx.enter_context(nc.sbuf_tensor("x_all", [128, TILES * DIM], F32))
        ident = ctx.enter_context(nc.sbuf_tensor("ident", [128, 128], F32))
        ident_bf = ctx.enter_context(nc.sbuf_tensor("ident_bf", [128, 128], BF16))
        x_in, ident_cleared, ident_made, x_out = (ctx.enter_context(nc.semaphore(n)) for n in ("x_in", "ident_cleared", "ident_made", "x_out"))
        with nc.Block() as block:

            @block.sync
            def _(sp):
                sp.dma_start(x_all[:, :], arrays["x"]).then_inc(x_in, 16)
                sp.wait_ge(x_in, 16)

            @block.gpsimd
            def _(pool):
                nc.gpsimd.memset(ident[:, :], 0.0).then_inc(ident_cleared, 1)
                nc.gpsimd.memset(ident_bf[:, :], 0.0).then_inc(ident_cleared, 1)
                pool.wait_ge(ident_cleared, 2)
                for m in (ident, ident_bf):
                    nc.gpsimd.affine_select(out=m[:, :], in_=m[:, :], compare_op=ALU.not_equal, fill=1.0, base=0,
                                            pattern=[[-1, 128]], channel_multiplier=1).then_inc(ident_made, 1)
                pool.wait_ge(ident_made, 2)

        cross_attention(nc, x_all, ident, ident_bf, arrays)
        with nc.sbuf_tensor("s_all", [128, TILES * DIM], F32) as s_all:
            norm_all(nc, x_all, s_all, "fn")
            shifted_layers(nc, s_all, ident, ident_bf, arrays)
            add_all(nc, x_all, s_all)
        kernel_attention(nc, x_all, ident, arrays)
        with nc.sbuf_tensor("s2_all", [128, TILES * DIM], F32) as s_all:
            norm_all(nc, x_all, s_all, "qn")
            quantised_ffn(nc, x_all, s_all, ident, arrays)
        two_attentions(nc, x_all, ident, ident_bf, arrays)
        ternary_ffn(nc, x_all, ident, arrays)
        context_attention(nc, x_all, ident, arrays)
        experts(nc, x_all, ident, arrays)
        with nc.Block() as block:

            @block.sync
            def _(sp):
                sp.dma_start(out, x_all[:, :]).then_inc(x_out, 16)
                sp.wait_ge(x_out, 16)


def constants():
    half = np.arange(0, HEAD_DIM, 2, dtype=np.float32)
    inv_freq = (np.float32(1.0) / np.power(np.float32(10000.0), half / np.float32(HEAD_DIM))).astype(np.float32)
    t = np.arange(SEQ, dtype=np.float32)
    freqs = t[:, None] * inv_freq[None, :]
    base = ((half + np.float32(0.4 * HEAD_DIM)) / np.float32(1.4 * HEAD_DIM)).astype(np.float32)
    power = (t - SEQ // 2) / np.float32(16)
    scale = np.power(base[None, :], power[:, None]).astype(np.float32)
    cos, sin = np.cos(freqs), np.sin(freqs)
    rot = np.zeros((SEQ, 4, HEAD_DIM), np.float32)
    for n, s in ((0, scale), (2, np.float32(1.0) / scale)):
        rot[:, n, :] = np.concatenate([cos * s, cos * s], -1)
        rot[:, n + 1, :] = np.concatenate([-sin * s, sin * s], -1)
    rot = rot.reshape(2, 128, 4, HEAD_DIM).transpose(1, 0, 2, 3)
    row, col = np.arange(128)[:, None], np.arange(64)[None, :]
    r = row % 32
    keep = (col >= r) & (col <= r + 32)
    first = keep & ((row >= 32) | (col >= 32))
    band = np.stack([np.where(k, 0.0, -1e25).astype(np.float32) for k in (first, keep)], 1)
    band = np.tile(band, (1, 1, 4))
    return {"rot": np.ascontiguousarray(rot), "band": band}


def lay_out(i):
    c = np.ascontiguousarray
    f = {n: np.asarray(i[n]) for n in i}
    d = dict(constants())
    d["x"] = c(f["x"].reshape(TILES, 128, DIM).transpose(1, 0, 2)).reshape(128, TILES * DIM)
    d["Wqkv"] = c(f["L0_ffn_Wqkv"])
    d["Wo"] = c(f["L0_ffn_Wo"].reshape(6, PAIRS, 128, DIM).transpose(0, 2, 1, 3))
    d["W1"] = c(f["L0_ffn_W1"])
    w2 = np.zeros((6, 3 * 128, DIM), np.float32)
    w2[:, 0:341] = f["L0_ffn_W2"]
    w2[:, 2 * 128 + 96] = f["L0_ffn_b2"]
    d["W2"] = c(w2.reshape(6, 3, 128, DIM).transpose(0, 2, 1, 3))
    cols = np.zeros((6, 8, 384), np.float32)
    cols[:, 0, 0:128] = f["L0_ffn_ln_g"]
    cols[:, 1, 0:128] = f["L0_ffn_ln_b"]
    for k, (at, n) in enumerate(((0, 128), (128, 128), (256, 85))):
        cols[:, 2 + k, 0:n] = f["L0_ffn_b1"][:, 341 + at:341 + at + n]
        cols[:, 5 + k, 0:n] = f["L0_ffn_b1"][:, at:at + n]
    d["cols"] = c(cols[:, :, 0:128].transpose(0, 2, 1))
    qs, ks = f["L0_ffn_q_scale"], f["L0_ffn_k_scale"]
    turn = np.concatenate([np.arange(32, 64), np.arange(0, 32)])
    four = np.stack([qs, qs[:, turn], ks, ks[:, turn]], 1)
    d["qk_scale"] = c(np.broadcast_to(four[:, None], (6, 128, 4, HEAD_DIM)))
    ctx = f["ctx_1024"]
    d["ctx_t"] = c(ctx.reshape(BATCH * CTX, DIM).T)
    d["ctx_rows"] = c(ctx.transpose(1, 0, 2))
    d["mask"] = c(f["mask_BxS2_bf1"].reshape(1, BATCH * CTX)).view(np.uint8)
    d["x_Wq"] = c(f["L0_xattn_Wq"].T)
    kv = f["L0_xattn_Wkv"].T
    odd_even = kv[:, INNER:].reshape(DIM, PAIRS, 2, HEAD_DIM).transpose(0, 2, 1, 3).reshape(DIM, INNER)
    d["x_Wkv"] = c(np.concatenate([kv[:, :INNER], odd_even], 1))
    d["x_Wout"] = c(f["L0_xattn_Wout"].T.reshape(PAIRS, 128, DIM).transpose(1, 0, 2))
    d["x_b"] = c(f["L0_xattn_b_out"].reshape(1, DIM))
    gu = np.zeros((2, 3 * 128, DIM), np.float32)
    gu[0, :352], gu[1, :352] = f["L1_ffn_w_gate"], f["L1_ffn_w_up"]
    d["q_gu"] = c(gu.reshape(6, 128, DIM).transpose(1, 0, 2))
    down = np.zeros((DIM, 3 * 128), np.float32)
    down[:, :352] = f["L1_ffn_w_down"]
    d["q_d"] = down
    d["q_clips"] = c(np.broadcast_to(np.concatenate([f["L1_ffn_clip_x"], f["L1_ffn_clip_down"]]), (128, 2)))
    for n in ("Wk1", "Wq1", "Wv1", "Wk2", "Wq2", "Wv2", "W1", "W2"):
        d["a_" + n] = c(f["L2_xattn_" + n])
    d["a_rows"] = c(np.broadcast_to(np.stack([f["L2_xattn_gamma"], f["L2_xattn_beta"], f["L2_xattn_b2"]]), (128, 3, DIM)))
    d["a_b1"] = c(f["L2_xattn_b1"].reshape(DIM, 1))
    d["causal"] = np.where(np.arange(128)[None, :] > np.arange(128)[:, None], -1e30, 0.0).astype(np.float32)
    d["g_fc"] = c(f["L2_ffn_W_fc"].T)
    d["g_proj"] = c(f["L2_ffn_W_proj"].T.reshape(4, 128, DIM).transpose(1, 0, 2)).reshape(128, 4 * DIM)
    d["g_affine"] = c(np.stack([f["L2_ffn_ln_w"], f["L2_ffn_ln_b"]]).reshape(2, 4, 128).transpose(2, 0, 1))
    d["y_W"] = c(f["L3_xattn_W"])
    d["y_b"] = c(f["L3_xattn_b"].reshape(DIM, 1))
    d["e_Ws"] = c(f["L3_ffn_Ws"])
    d["e_bs"] = c(f["L3_ffn_bs"].reshape(1, EXPERTS))
    d["e_W1"] = c(f["L3_ffn_W1"].transpose(1, 0, 2))
    d["e_W2"] = c(f["L3_ffn_W2"].reshape(EXPERTS, CHUNKS, 128, DIM).transpose(2, 0, 1, 3))
    d["e_b1"] = c(f["L3_ffn_b1"].reshape(EXPERTS * CHUNKS, 128).T)
    d["e_b2"] = c(f["L3_ffn_b2"])
    d["k_proj"] = c(f["L1_xattn_projection"].T)
    return d


def kernel(**inputs):
    import concourse.bacc as _bacc
    from concourse.bass_utils import run_bass_kernel_spmd as _run

    nc = _bacc.Bacc("TRN2", target_bir_lowering=False, num_devices=1)
    arrays = lay_out(inputs)
    aps = {n: nc.dram_tensor("in_" + n, a.shape, mybir.dt.from_np(a.dtype), kind="ExternalInput").ap() for n, a in arrays.items()}
    out = nc.dram_tensor("out", (128, TILES * DIM), F32, kind="ExternalOutput").ap()
    build(nc, aps, out)
    r = _run(nc, [{"in_" + n: a for n, a in arrays.items()}], core_ids=[0])
    y = np.asarray(r.results[0]["out"]).reshape(128, TILES, DIM)
    return np.ascontiguousarray(y.transpose(1, 0, 2)).reshape(BATCH, SEQ, DIM)
```

```python
from contextlib import ExitStack

import numpy as np

import concourse.bass as bass
from concourse import mybir

F32 = mybir.dt.float32
BF16 = mybir.dt.bfloat16
I32 = mybir.dt.int32
U8 = mybir.dt.uint8
ALU = mybir.AluOpType
ACT = mybir.ActivationFunctionType
AX_X = mybir.AxisListType.X

BATCH, SEQ, DIM = 16, 256, 128
CTX = 64
TILES = BATCH * SEQ // 128
PASS_TOK = 512
PASS_TILES = PASS_TOK // 128
PASSES = BATCH * SEQ // PASS_TOK
HEADS, HEAD_DIM = 16, 64
INNER = HEADS * HEAD_DIM
GROUP = 8
PAIRS = HEADS // 2
ROUND = 12582912.0
RSQRT_SEED = 1597463007.0


class Chain:

    def __init__(self, engine, semaphore):
        self.engine, self.semaphore, self.count = engine, semaphore, 0

    def link(self, instruction):
        instruction.then_inc(self.semaphore, 1)
        self.count += 1
        self.engine.wait_ge(self.semaphore, self.count)

    def mark(self, instruction):
        instruction.then_inc(self.semaphore, 1)
        self.count += 1

    def wait(self):
        self.engine.wait_ge(self.semaphore, self.count)

    def reset(self):
        self.engine.wait_ge(self.semaphore, self.count)
        self.engine.sem_clear(self.semaphore)
        self.count = 0


def clear(nc, semaphores):
    with nc.Block() as block:

        @block.sync
        def _(sp):
            for semaphore in semaphores:
                sp.sem_clear(semaphore)


def rsqrt(vector, chain, out, value, work):
    chain.link(vector.tensor_scalar(out.bitcast(I32), value.bitcast(I32), -0.5, RSQRT_SEED, ALU.mult, ALU.add))
    for step in range(3):
        chain.link(vector.tensor_tensor(work, out, out, ALU.mult))
        chain.link(vector.scalar_tensor_tensor(work, work, -0.5, value, ALU.mult, ALU.mult))
        last = vector.scalar_tensor_tensor(out, work, 1.5, out, ALU.add, ALU.mult)
        if step < 2:
            chain.link(last)
    return last


def alone(engine):
    engine.nop(nofuse=True)


def over(ap, shape):
    return ap.unsqueeze(len(ap.shape)).broadcast_to(shape)


def layer_norm_tiles(nc, dve, chain, source, out, work, eps=1e-5):
    stats, mv, var = work
    for t in range(PASS_TILES):
        chain.mark(nc.vector.bn_stats(stats[:, t, :], source(t)))
    chain.wait()
    for t in range(PASS_TILES):
        chain.mark(nc.vector.bn_aggr(mv[:, t, :], stats[:, t, :]))
    chain.wait()
    chain.link(nc.vector.tensor_scalar(var[:, 0, :], mv[:, :, 1], eps, None, ALU.add))
    chain.link(rsqrt(nc.vector, chain, var[:, 1, :], var[:, 0, :], var[:, 2, :]))
    for t in range(PASS_TILES):
        last = nc.vector.tensor_scalar(out(t), source(t), mv[:, t, 0:1], var[:, 1, t:t + 1], ALU.subtract, ALU.mult)
        if t < PASS_TILES - 1:
            chain.mark(last)
    return last


def norm_all(nc, x_all, s_all, name):
    with ExitStack() as ctx:
        stats = ctx.enter_context(nc.sbuf_tensor(name + "_stats", [128, PASS_TILES, 6], F32))
        mv = ctx.enter_context(nc.sbuf_tensor(name + "_mv", [128, PASS_TILES, 2], F32))
        var = ctx.enter_context(nc.sbuf_tensor(name + "_var", [128, 3, PASS_TILES], F32))
        own = ctx.enter_context(nc.semaphore(name + "_own_vector"))
        ctx.callback(clear, nc, [own])
        block = ctx.enter_context(nc.Block())

        @block.vector
        def _(dve):
            chain = Chain(dve, own)
            with dve.Fori(0, PASSES) as p:
                def tile(source):
                    return lambda t: source[:, bass.ds(p * PASS_TOK + 128 * t, 128)]
                chain.link(layer_norm_tiles(nc, dve, chain, tile(x_all), tile(s_all), (stats, mv, var)))
                chain.reset()


def add_all(nc, x_all, s_all):
    with nc.Block() as block:
        half = TILES * DIM // 2

        @block.vector
        def _(dve):
            nc.vector.tensor_tensor(x_all[:, 0:half], x_all[:, 0:half], s_all[:, 0:half], ALU.add)

        @block.gpsimd
        def _(pool):
            nc.gpsimd.tensor_tensor(x_all[:, half:], x_all[:, half:], s_all[:, half:], ALU.add)


def cross_attention(nc, x_all, ident, ident_bf, dram):
    SCALE = HEAD_DIM ** -0.5
    MASKED = 3e38
    CHUNKS = PASS_TILES * 2
    UNITS = 12
    UNIT_BANKS = (0, 1, 5, 6)
    with ExitStack() as ctx:
        def sb(name, shape, dt=F32):
            return ctx.enter_context(nc.sbuf_tensor("x_" + name, shape, dt))

        used = []

        def sem(name):
            used.append(ctx.enter_context(nc.semaphore("x_" + name)))
            return used[-1]

        bank = [ctx.enter_context(nc.psum_tensor(f"x_bank{i}", [128, 512], F32)) for i in range(8)]
        w_q = sb("w_q", [128, INNER])
        w_kv = sb("w_kv", [128, 2 * INNER])
        w_out = sb("w_out", [128, PAIRS, DIM])
        b_out = sb("b_out", [1, DIM])
        ctx_all = sb("ctx_all", [128, BATCH * CTX])
        mask_in = sb("mask_in", [1, BATCH * CTX], U8)
        mask_f = sb("mask_f", [1, BATCH * CTX])
        mask_b = sb("mask_b", [1, BATCH, CTX], BF16)
        mask_8 = sb("mask_8", [1, 2, GROUP, CTX], BF16)
        ones = sb("ones", [1, 128])
        ones_b = sb("ones_b", [1, 128], BF16)
        work = (sb("stats", [128, PASS_TILES, 6]), sb("mv", [128, PASS_TILES, 2]), sb("var", [128, 3, PASS_TILES]))
        xn = sb("xn", [128, PASS_TOK])
        xn_t = sb("xn_t", [128, PASS_TOK])
        ctx_t = sb("ctx_t", [128, 2 * CTX])
        k_t = sb("k_t", [128, 2, PAIRS, 2 * CTX])
        v = sb("v", [128, 2, PAIRS, 2, HEAD_DIM])
        q_t = sb("q_t", [128, PAIRS, PASS_TOK])
        score = sb("score", [128, 2, GROUP, CTX])
        stat = sb("stat", [128, 3, GROUP])
        prob = sb("prob", [128, GROUP, CTX])
        prob_t = sb("prob_t", [128, 4, 128])
        out_t = sb("out_t", [128, PAIRS, PASS_TOK])

        loaded, consts, mask_made, own_v = sem("loaded"), sem("consts"), sem("mask_made"), sem("own_vector")
        normed, x_turned, xn_t_made, ctx_taken = sem("normed"), sem("x_turned"), sem("xn_t_made"), sem("ctx_taken")
        unit_done, unit_made = sem("unit_done"), sem("unit_made")
        scores_done, score_banks_free, exped = sem("scores_done"), sem("score_banks_free"), sem("exped")
        prob_made, prob_turned, prob_t_made = sem("prob_made"), sem("prob_turned"), sem("prob_t_made")
        mixed, mix_out, o_done, o_added = sem("mixed"), sem("mix_out"), sem("o_done"), sem("o_added")

        ctx.callback(clear, nc, used)
        block = ctx.enter_context(nc.Block())

        @block.sync
        def _(sp):
            for to, name in ((ctx_all, "ctx_t"), (w_q, "x_Wq"), (w_kv, "x_Wkv"), (b_out, "x_b"), (mask_in, "mask")):
                sp.dma_start(to[:, :], dram[name]).then_inc(loaded, 16)
            sp.dma_start(w_out[:, :, :], dram["x_Wout"]).then_inc(loaded, 16)

        @block.gpsimd
        def _(pool):
            nc.gpsimd.memset(ones[:, :], 1.0).then_inc(consts, 1)
            nc.gpsimd.memset(ones_b[:, :], 1.0).then_inc(consts, 1)
            nc.gpsimd.memset(k_t[:, :, :, :], 0.0).then_inc(consts, 1)
            nc.gpsimd.memset(v[:, :, :, :, :], 0.0).then_inc(consts, 1)
            pool.wait_ge(loaded, 96)
            pool.wait_ge(mask_made, 3)
            with pool.Fori(0, PASSES) as p:
                pool.wait_ge(scores_done, p * CHUNKS)
                nc.gpsimd.tensor_copy(mask_8[:, :, :, :], mask_b[:, bass.ds(p * 2, 2), :].unsqueeze(2).broadcast_to([1, 2, GROUP, CTX])).then_inc(ctx_taken, 1)
                nc.gpsimd.tensor_copy(ctx_t[:, :], ctx_all[:, bass.ds(p * 2 * CTX, 2 * CTX)]).then_inc(ctx_taken, 1)

        @block.tensor
        def _(pe):
            pe.wait_ge(loaded, 96)
            pe.wait_ge(consts, 4)
            with pe.Fori(0, PASSES) as p:
                pe.wait_ge(normed, p + 1)
                for t in range(PASS_TILES):
                    last = nc.tensor.transpose(bank[3][:, 128 * t:128 * t + 128], xn[:, 128 * t:128 * t + 128], ident[:, :])
                last.then_inc(x_turned, 1)
                pe.wait_ge(ctx_taken, p * 2 + 2)
                for u in range(UNITS):
                    to = bank[UNIT_BANKS[u % 4]]
                    if u >= 4:
                        pe.wait_ge(unit_made, p * (UNITS + 4) + (u - 3 + min(u - 3, 4)))
                    if u < 2:
                        for b in range(4):
                            at = 128 * (4 * u + b)
                            last = nc.tensor.matmul(to[:, 128 * b:128 * b + 128], w_kv[:, at:at + 128], ctx_t[:, :], start=True, stop=True)
                    elif u < 4:
                        for n in range(2):
                            last = nc.tensor.matmul(to[64 * n:64 * n + 64, :], ctx_t[:, CTX * (u - 2):CTX * (u - 1)],
                                                    w_kv[:, INNER + 512 * n:INNER + 512 * n + 512], start=True, stop=True)
                    else:
                        if u == 4:
                            pe.wait_ge(xn_t_made, p + 1)
                        last = nc.tensor.matmul(to[:, :], w_q[:, 128 * (u - 4):128 * (u - 3)], xn_t[:, :], start=True, stop=True)
                    last.then_inc(unit_done, 1)
                pe.wait_ge(unit_made, p * (UNITS + 4) + (UNITS + 4))

                def scores(j):
                    t, g = j // 2, j % 2
                    pe.wait_ge(score_banks_free, p * CHUNKS + (j + 1))
                    to = bank[5 + j % 2]
                    nc.tensor.matmul(to[:, :], ones_b[:, :], mask_8[:, t // 2, :, :].rearrange("a b c -> a (b c)"), start=True, stop=True)
                    for b in range(4):
                        last = nc.tensor.matmul(to[:, 128 * b:128 * b + 128], q_t[:, 4 * g + b, 128 * t:128 * t + 128],
                                                k_t[:, :, 4 * g + b, CTX * (t // 2):CTX * (t // 2) + CTX],
                                                start=False, stop=True, skip_group_check=True)
                    last.then_inc(scores_done, 1)

                def turn_prob(j):
                    pe.wait_ge(prob_made, p * CHUNKS + (j + 1))
                    if j >= 1:
                        pe.wait_ge(prob_t_made, p * CHUNKS + j)
                    for b in range(4):
                        last = nc.tensor.transpose(bank[7][:, 128 * b:128 * b + 128], prob[:, 2 * b:2 * b + 2, :].rearrange("p a c -> p (a c)"), ident[:, :])
                    last.then_inc(prob_turned, 1)

                def mix(j):
                    t, g = j // 2, j % 2
                    pe.wait_ge(prob_t_made, p * CHUNKS + (j + 1))
                    if j >= 1:
                        pe.wait_ge(mix_out, p * CHUNKS + j)
                    alone(pe)
                    for b in range(4):
                        last = nc.tensor.matmul(bank[3][:, 128 * b:128 * b + 128], v[:, t // 2, 4 * g + b, :, :],
                                                prob_t[:, b, :], start=True, stop=True)
                    last.then_inc(mixed, 1)

                def project_out(t):
                    pe.wait_ge(mix_out, p * CHUNKS + 2 * (t + 1))
                    if t:
                        pe.wait_ge(o_added, p * PASS_TILES + t)
                    for b in range(PAIRS):
                        nc.tensor.matmul(bank[2][:, 0:128], out_t[:, b, 128 * t:128 * t + 128], w_out[:, b, :], start=(b == 0), stop=False)
                    nc.tensor.matmul(bank[2][:, 0:128], ones[:, :], b_out[:, :], start=False, stop=True).then_inc(o_done, 1)

                for i in range(CHUNKS + 4):
                    if i < CHUNKS:
                        scores(i)
                    if 2 <= i <= CHUNKS + 1:
                        turn_prob(i - 2)
                    if i >= 5 and i % 2:
                        project_out((i - 5) // 2)
                    if 3 <= i <= CHUNKS + 2:
                        mix(i - 3)

        @block.vector
        def _(dve):
            chain = Chain(dve, own_v)
            dve.sem_inc(score_banks_free, 2)
            dve.wait_ge(loaded, 96)
            nc.vector.tensor_copy(mask_f[:, :], mask_in[:, :]).then_inc(mask_made, 1)
            dve.wait_ge(mask_made, 1)
            nc.vector.tensor_scalar(mask_f[:, :], mask_f[:, :], 1.0, MASKED, ALU.subtract, ALU.mult).then_inc(mask_made, 1)
            dve.wait_ge(mask_made, 2)
            nc.vector.tensor_copy(mask_b[:, :, :], mask_f[:, :].rearrange("a (b c) -> a b c", c=CTX)).then_inc(mask_made, 1)

            def norm_pass(p):
                dve.wait_ge(x_turned, p)
                alone(dve)
                layer_norm_tiles(nc, dve, chain, lambda t: x_all[:, bass.ds(p * PASS_TOK + 128 * t, 128)],
                                 lambda t: xn[:, 128 * t:128 * t + 128], work).then_inc(normed, 1)

            def attention_pass(p, last_pass=False):
                def soften(j):
                    dve.wait_ge(scores_done, p * CHUNKS + (j + 1))
                    dve.wait_ge(score_banks_free, p * CHUNKS + (j + 2))
                    source = bank[5 + j % 2][:, :].rearrange("p (h c) -> p h c", c=CTX)
                    chain.link(nc.vector.tensor_reduce(stat[:, 0, :], source, AX_X, ALU.max))
                    nc.vector.tensor_tensor(score[:, j % 2, :, :], source, over(stat[:, 0, :], [128, GROUP, CTX]), ALU.subtract).then_inc(score_banks_free, 1)

                def normalise(j):
                    dve.wait_ge(exped, p * CHUNKS + (j + 1))
                    dve.wait_ge(prob_made, p * CHUNKS + j)
                    chain.link(nc.vector.tensor_reduce(stat[:, 1, :], score[:, j % 2, :, :], AX_X, ALU.add))
                    chain.link(nc.vector.reciprocal(stat[:, 2, :], stat[:, 1, :]))
                    if j >= 1:
                        dve.wait_ge(prob_turned, p * CHUNKS + j)
                    nc.vector.tensor_tensor(prob[:, :, :], score[:, j % 2, :, :], over(stat[:, 2, :], [128, GROUP, 64]), ALU.mult).then_inc(prob_made, 1)

                for i in range(CHUNKS + 4):
                    if i < CHUNKS:
                        soften(i)
                    if 1 <= i <= CHUNKS:
                        normalise(i - 1)
                    if i == CHUNKS + 1 and not last_pass:
                        norm_pass(p + 1)
                    if i >= 5 and i % 2:
                        t = (i - 5) // 2
                        dve.wait_ge(o_done, p * PASS_TILES + (t + 1))
                        tile = x_all[:, bass.ds(p * PASS_TOK + 128 * t, 128)]
                        nc.vector.tensor_tensor(tile, tile, bank[2][:, 0:128], ALU.add).then_inc(o_added, 1)
                chain.reset()

            norm_pass(0)
            chain.reset()
            with dve.Fori(0, PASSES - 1) as p:
                attention_pass(p)
            attention_pass(PASSES - 1, last_pass=True)

        @block.scalar
        def _(act):
            act.wait_ge(consts, 4)
            with act.Fori(0, PASSES) as p:
                for u in range(UNITS):
                    if u == 4:
                        act.wait_ge(x_turned, p + 1)
                        nc.scalar.activation(xn_t[:, :], bank[3][:, :], ACT.Copy).then_inc(xn_t_made, 1)
                    if u == 0:
                        act.wait_ge(mixed, p * CHUNKS)
                    act.wait_ge(unit_done, p * UNITS + (u + 1))
                    source = bank[UNIT_BANKS[u % 4]][:, :]
                    if u >= 4:
                        nc.scalar.activation(q_t[:, u - 4, :], source, ACT.Copy).then_inc(unit_made, 1)
                    for n in range(2 if u < 4 else 0):
                        half = slice(64 * n, 64 * n + 64)
                        if u < 2:
                            to, part = k_t[half, n, 4 * u:4 * u + 4, :], source[half, :].rearrange("p (b n) -> p b n", b=4)
                        else:
                            to, part = v[half, u - 2, :, n, :], source[half, :].rearrange("p (b d) -> p b d", d=HEAD_DIM)
                        nc.scalar.activation(to, part, ACT.Copy).then_inc(unit_made, 1)
                for i in range(CHUNKS + 3):
                    if i < CHUNKS:
                        act.wait_ge(score_banks_free, p * CHUNKS + (i + 3))
                        nc.scalar.activation(score[:, i % 2, :, :], score[:, i % 2, :, :], ACT.Exp, scale=SCALE).then_inc(exped, 1)
                    if 2 <= i <= CHUNKS + 1:
                        j = i - 2
                        act.wait_ge(prob_turned, p * CHUNKS + (j + 1))
                        if j >= 1:
                            act.wait_ge(mixed, p * CHUNKS + j)
                        nc.scalar.activation(prob_t[:, :, :], bank[7][:, :].rearrange("p (b n) -> p b n", b=4), ACT.Copy).then_inc(prob_t_made, 1)
                    if i >= 3:
                        j = i - 3
                        t, g = j // 2, j % 2
                        act.wait_ge(mixed, p * CHUNKS + (j + 1))
                        nc.scalar.activation(out_t[:, 4 * g:4 * g + 4, 128 * t:128 * t + 128], bank[3][:, :].rearrange("p (b n) -> p b n", b=4), ACT.Copy).then_inc(mix_out, 1)


def shifted_layers(nc, x_all, ident, ident_bf, dram):
    DEPTH, WINDOW, QK_SCALE = 6, 32, 8.0
    HALF = 341
    CHUNKS = PASS_TILES * 2
    FF = [(0, 128), (128, 128), (256, 85)]
    ONES_ROW = 96
    with ExitStack() as ctx:
        def sb(name, shape, dt=F32):
            return ctx.enter_context(nc.sbuf_tensor("f_" + name, shape, dt))

        used = []

        def sem(name):
            used.append(ctx.enter_context(nc.semaphore("f_" + name)))
            return used[-1]

        bank = [ctx.enter_context(nc.psum_tensor(f"f_bank{i}", [128, 512], F32)) for i in range(8)]
        w_qkv = sb("w_qkv", [128, 3 * INNER])
        w_o = sb("w_o", [128, PAIRS, DIM])
        w_1 = sb("w_1", [128, 2 * HALF])
        w_2 = sb("w_2", [128, 3, DIM])
        cols = sb("cols", [128, 8])
        rot_const = sb("rot_const", [128, 2, 4, HEAD_DIM])
        head_scale = sb("head_scale", [128, 4, HEAD_DIM])
        rot = sb("rot", [128, 2, 4, HEAD_DIM])
        band_in = sb("band_in", [128, 2, 512])
        band = sb("band", [128, 2, 512], BF16)
        xw = sb("xw", [128, PASS_TOK])
        xs_t = sb("xs_t", [128, 2, SEQ])
        squares = sb("squares", [128, 2, 2, 512])
        rot_a = sb("rot_a", [128, 2, 2, 512])
        rot_b = sb("rot_b", [128, 2, 2, 512])
        qk = sb("qk", [128, 2, 2, 512])
        norm = sb("norm", [128, 2, 16])
        norm_y = sb("norm_y", [128, 3, 16])
        q_t = sb("q_t", [128, 512])
        k_t = sb("k_t", [128, 2, PAIRS, WINDOW + SEQ])
        v = sb("v", [128, 4, 512])
        v_off = sb("v_off", [128, 4, 512])
        score = sb("score", [128, 2, GROUP, 64])
        prob = sb("prob", [128, GROUP, 64])
        stat = sb("stat", [128, 3, GROUP])
        prob_t = sb("prob_t", [128, 2, GROUP, 2, WINDOW])
        out_t = sb("out_t", [128, PAIRS, PASS_TOK])
        x_shifted = sb("x_shifted", [128, TILES, DIM])
        f_stats = sb("f_stats", [128, PASS_TILES, 6])
        f_mv = sb("f_mv", [128, PASS_TILES, 2])
        f_var = sb("f_var", [128, 3, PASS_TILES])
        f_n = sb("f_n", [128, PASS_TOK])
        f_nt = sb("f_nt", [128, PASS_TOK])
        gate = sb("gate", [128, 3, PASS_TOK])
        hidden = sb("hidden", [128, 3, PASS_TOK])

        const_in = sem("const_in")
        w_qkv_in, w_o_in, w_ff_in, scale_in = sem("w_qkv_in"), sem("w_o_in"), sem("w_ff_in"), sem("scale_in")
        zeroed = sem("zeroed")
        own_v = sem("own_vector")
        tables_made = sem("tables_made")
        x_taken, x_turned, xs_made = sem("x_taken"), sem("x_turned"), sem("xs_made")
        x_shifted_in = sem("x_shifted_in")
        qk_proj, v_proj = sem("qk_proj"), sem("v_proj")
        squared = sem("squared")
        qk_free = sem("qk_free")
        v_made = sem("v_made")
        v_moved = [sem(f"v_moved{i}") for i in range(4)]
        v_carried = [sem(f"v_carried{i}") for i in range(2)]
        scaled = sem("scaled")
        norms_made = sem("norms_made")
        rot_free, q_rotated, k_rotated = sem("rot_free"), sem("q_rotated"), sem("k_rotated")
        qk_turned, qk_t_made = sem("qk_turned"), sem("qk_t_made")
        scores_done, maxed, shifted, exped = sem("scores_done"), sem("maxed"), sem("shifted"), sem("exped")
        score_banks_free = sem("score_banks_free")
        prob_made, prob_turned, prob_t_made = sem("prob_made"), sem("prob_turned"), sem("prob_t_made")
        mixed, mix_out = sem("mixed"), sem("mix_out")
        o_done, o_added = sem("o_done"), sem("o_added")
        f_normed, f_again, f_affine = sem("f_normed"), sem("f_again"), sem("f_affine")
        f_gate, f_up, f_gelu, f_hidden, f_done, x_stored = (
            sem("f_gate"), sem("f_up"), sem("f_gelu"), sem("f_hidden"), sem("f_done"), sem("x_stored"))

        def flat(i):
            return bank[i][:, :]

        ctx.callback(clear, nc, used)
        block = ctx.enter_context(nc.Block())

        def layer_passes(engine, layer, attention_pass):
            attention_pass(layer * PASSES, 0, first=True)
            with engine.Fori(0, PASSES - 2) as middle:
                attention_pass(layer * PASSES + middle + 1, middle + 1)
            attention_pass(layer * PASSES + (PASSES - 1), PASSES - 1, last=True)

        def steps(first, last):
            return range(CHUNKS + 3 if last else CHUNKS)

        def in_pass(j, first, last):
            return (j >= 0 or not first) and j < CHUNKS

        def out_tile(i, first, last):
            if i % 2 or (first and i < 4):
                return None
            return (i - 4) // 2

        @block.sync
        def _(sp):
            sp.dma_start(rot_const[:, :, :, :], dram["rot"]).then_inc(const_in, 16)
            sp.dma_start(band_in[:, :, :], dram["band"]).then_inc(const_in, 16)
            sp.wait_ge(zeroed, 6)

            def shift_out(p, pair):
                sp.wait_ge(o_added, p * PASS_TILES + PASS_TILES)
                alone(sp)
                sp.wait_ge(x_shifted_in, p * 48)
                to = x_shifted[:, bass.ds(pair * PASS_TILES, PASS_TILES), :]
                source = x_all[:, bass.ds(pair * PASS_TOK, PASS_TOK)].rearrange("p (t n) -> p t n", n=DIM)
                sp.dma_start(to[:, :, 0:64], source[:, :, 0:64]).then_inc(x_shifted_in, 16)
                sp.dma_start(to[1:128, :, 64:128], source[0:127, :, 64:128]).then_inc(x_shifted_in, 16)
                sp.dma_start(to[0:1, 1::2, 64:128], source[127:128, 0::2, 64:128]).then_inc(x_shifted_in, 16)

            with sp.Fori(0, DEPTH) as layer:
                sp.wait_ge(v_proj, layer * (PASSES * CHUNKS))
                sp.dma_start(w_qkv[:, :], dram["Wqkv"][bass.ds(layer, 1)].rearrange("a p n -> (a p) n")).then_inc(w_qkv_in, 16)
                sp.wait_ge(tables_made, layer)
                sp.dma_start(head_scale[:, :, :], dram["qk_scale"][bass.ds(layer, 1)].rearrange("a p n d -> (a p) n d")).then_inc(scale_in, 16)
                sp.wait_ge(o_done, layer * (PASSES * PASS_TILES))
                sp.dma_start(w_o[:, :, :], dram["Wo"][bass.ds(layer, 1)].rearrange("a p n d -> (a p) n d")).then_inc(w_o_in, 16)
                sp.wait_ge(x_stored, layer * PASSES)
                sp.dma_start(w_1[:, :], dram["W1"][bass.ds(layer, 1)].rearrange("a p n -> (a p) n")).then_inc(w_ff_in, 16)
                sp.dma_start(w_2[:, :, :], dram["W2"][bass.ds(layer, 1)].rearrange("a p n d -> (a p) n d")).then_inc(w_ff_in, 16)
                sp.dma_start(cols[:, :], dram["cols"][bass.ds(layer, 1)].rearrange("a p n -> (a p) n")).then_inc(w_ff_in, 16)

                def attention_pass(p, pair, first=False, last=False):
                    for c in range(CHUNKS):
                        sp.wait_ge(v_made, p * CHUNKS + (c + 1))
                        sp.dma_start(v_off[32:128, c % 4, :], v[0:96, c % 4, :]).then_inc(v_moved[c % 4], 16)
                        if c % 4 < 2:
                            if c >= 2 or not first:
                                sp.wait_ge(mixed, p * CHUNKS + (c - 1))
                            sp.dma_start(v_off[0:32, c % 4 + 2, :], v[96:128, c % 4, :]).then_inc(v_carried[c % 2], 16)
                        if c == 3 and not first:
                            shift_out(p - 1, pair - 1)
                    if last:
                        shift_out(p, pair)

                layer_passes(sp, layer, attention_pass)

        @block.tensor
        def _(pe):
            pe.wait_ge(const_in, 32)
            pe.wait_ge(zeroed, 6)
            with pe.Fori(0, DEPTH) as layer:
                pe.wait_ge(w_qkv_in, layer * 16 + 16)
                pe.wait_ge(w_o_in, layer * 16 + 16)
                pe.wait_ge(w_ff_in, layer * 48 + 48)
                pe.wait_ge(x_taken, layer * PASSES + 1)
                for t in range(PASS_TILES):
                    turned = nc.tensor.transpose(bank[6][:, 128 * t:128 * t + 128], xw[:, 128 * t:128 * t + 128], ident[:, :])
                turned.then_inc(x_turned, 1)

                def attention_pass(p, pair, first=False, last=False):

                    def turn_next_x():
                        pe.wait_ge(x_taken, p + 2)
                        pe.wait_ge(o_added, p * PASS_TILES + 2)
                        for t in range(PASS_TILES):
                            turned = nc.tensor.transpose(bank[6][:, 128 * t:128 * t + 128], xw[:, 128 * t:128 * t + 128], ident[:, :])
                        turned.then_inc(x_turned, 1)

                    def proj(i, n):
                        t, g = (i // 2) % PASS_TILES, i % 2
                        x_tile = xs_t[:, t // 2, 128 * (t % 2):128 * (t % 2) + 128]
                        pe.wait_ge(qk_free, p * (2 * CHUNKS) + (2 * i + n + 1))
                        nc.tensor.matmul(flat(n), x_tile, w_qkv[:, n * INNER + 512 * g:n * INNER + 512 * g + 512],
                                         start=True, stop=True).then_inc(qk_proj, 1)

                    def proj_v(i):
                        t, g = i // 2, i % 2
                        x_tile = xs_t[:, t // 2, 128 * (t % 2):128 * (t % 2) + 128]
                        pe.wait_ge(v_made, p * CHUNKS + i)
                        nc.tensor.matmul(flat(2), x_tile, w_qkv[:, 2 * INNER + 512 * g:2 * INNER + 512 * g + 512],
                                         start=True, stop=True).then_inc(v_proj, 1)

                    def turn_qk(j):
                        for n, ready in enumerate((q_rotated, k_rotated)):
                            pe.wait_ge(ready, p * CHUNKS + (j + 1))
                            if n == 0 and (j >= 2 or not first):
                                pe.wait_ge(mix_out, p * (4 * CHUNKS) + 4 * (j - 1))
                            for b in range(4):
                                turned = nc.tensor.transpose(bank[3 + n][:, 128 * b:128 * b + 128], qk[:, j % 2, n, 128 * b:128 * b + 128], ident[:, :])
                            turned.then_inc(qk_turned, 1)

                    def turn_prob(j):
                        pe.wait_ge(prob_made, p * CHUNKS + (j + 1))
                        pe.wait_ge(prob_t_made, p * (2 * CHUNKS) + 2 * j)
                        alone(pe)
                        for h in range(GROUP):
                            for b in range(2):
                                r = 64 * b
                                turned = nc.tensor.matmul(bank[7][r:r + 64, 64 * h:64 * h + 64], prob[r:r + 64, h, :], ident[r:r + 64, r:r + 64], start=True, stop=True)
                        turned.then_inc(prob_turned, 1)

                    def scores(j):
                        t, g = j // 2, j % 2
                        pe.wait_ge(score_banks_free, p * CHUNKS + (j + 1))
                        pe.wait_ge(qk_t_made, p * (3 * CHUNKS) + (3 * j + 3))
                        nc.tensor.matmul(flat(5), ident_bf[:, :], band[:, t % 2, :], start=True, stop=True)
                        for b in range(4):
                            for w in range(4):
                                at = WINDOW * (4 * (t % 2) + w)
                                done = nc.tensor.matmul(
                                    bank[5][32 * w:32 * w + 32, 128 * b:128 * b + 128],
                                    q_t[:, 128 * b + 32 * w:128 * b + 32 * w + 32],
                                    k_t[:, :, 4 * g + b, at:at + 64],
                                    start=False, stop=True, skip_group_check=True)
                        done.then_inc(scores_done, 1)

                    def mix(j):
                        t, g = j // 2, j % 2
                        pe.wait_ge(prob_t_made, p * (2 * CHUNKS) + (2 * j + 2))
                        pe.wait_ge(v_moved[j % 4], p * 32 + 16 * (j // 4 + 1))
                        if t % 2:
                            pe.wait_ge(v_carried[g], p * 32 + 16 * (j // 4 + 1))
                        if not (last and j == CHUNKS - 1):
                            pe.wait_ge(qk_t_made, p * (3 * CHUNKS) + (3 * j + 6))
                        alone(pe)
                        for u in range(2):
                            for b in range(4):
                                done = nc.tensor.matmul(
                                    bank[3 + u][:, 128 * b:128 * b + 128],
                                    (v if u else v_off)[:, j % 4, 128 * b:128 * b + 128],
                                    prob_t[:, u, 2 * b:2 * b + 2, :, :], start=True, stop=True)
                        done.then_inc(mixed, 1)

                    def project_out(t):
                        pe.wait_ge(mix_out, p * (4 * CHUNKS) + 8 * (t + 1))
                        pe.wait_ge(o_added, p * PASS_TILES + t)
                        at = 128 * (t % PASS_TILES)
                        for b in range(PAIRS):
                            done = nc.tensor.matmul(bank[6][:, 0:128], out_t[:, b, at:at + 128], w_o[:, b, :],
                                                    start=(b == 0), stop=(b == PAIRS - 1))
                        done.then_inc(o_done, 1)

                    if first:
                        pe.wait_ge(xs_made, p * 2 + 2)
                        proj(0, 0)
                        proj(0, 1)
                    for i in steps(first, last):
                        ahead = i + 1 < CHUNKS or not last
                        if in_pass(i - 1, first, last):
                            turn_qk(i - 1)
                        if i < CHUNKS:
                            proj_v(i)
                        if i == CHUNKS - 1 and not last:
                            turn_next_x()
                        if in_pass(i - 1, first, last):
                            scores(i - 1)
                        if in_pass(i - 2, first, last):
                            turn_prob(i - 2)
                        if ahead:
                            if i == CHUNKS - 1:
                                pe.wait_ge(xs_made, p * 2 + 4)
                            proj(i + 1, 0)
                        if (t := out_tile(i, first, last)) is not None:
                            project_out(t)
                        if in_pass(i - 2, first, last):
                            mix(i - 2)
                        if ahead:
                            proj(i + 1, 1)

                layer_passes(pe, layer, attention_pass)

                def turn_normed(p):
                    pe.wait_ge(f_normed, p + 1)
                    for t in range(PASS_TILES):
                        turned = nc.tensor.transpose(bank[3][:, 128 * t:128 * t + 128], f_n[:, 128 * t:128 * t + 128], ident[:, :])
                    turned.then_inc(f_again, 1)

                def feed_forward(p, last=False):
                    pe.wait_ge(f_affine, p + 1)
                    for k, (at, n) in enumerate(FF):
                        nc.tensor.matmul(bank[k][0:n, :], w_1[:, HALF + at:HALF + at + n], f_nt[:, :], start=True, stop=True).then_inc(f_gate, 1)
                    for k, (at, n) in enumerate(FF):
                        nc.tensor.matmul(bank[5 + k][0:n, :], w_1[:, at:at + n], f_nt[:, :], start=True, stop=True).then_inc(f_up, 1)
                    if not last:
                        turn_normed(p + 1)
                    pe.wait_ge(f_hidden, p * 3 + 3)
                    pe.wait_ge(x_stored, p)
                    for t in range(PASS_TILES):
                        for k, rows in enumerate((128, 128, ONES_ROW + 1)):
                            done = nc.tensor.matmul(bank[4][:, 128 * t:128 * t + 128], hidden[0:rows, k, 128 * t:128 * t + 128], w_2[0:rows, k, :],
                                                    start=(k == 0), stop=(k == 2))
                    done.then_inc(f_done, 1)

                turn_normed(layer * PASSES)
                pe.wait_ge(o_added, layer * (PASSES * PASS_TILES) + PASSES * PASS_TILES)
                alone(pe)
                with pe.Fori(0, PASSES - 1) as pair:
                    feed_forward(layer * PASSES + pair)
                feed_forward(layer * PASSES + (PASSES - 1), last=True)

        @block.vector
        def _(dve):
            chain = Chain(dve, own_v)
            chain.link(nc.vector.memset(xs_t[:, :, :], 0.0))
            chain.link(nc.vector.memset(hidden[:, :, :], 0.0))
            nc.vector.memset(k_t[:, :, :, :], 0.0).then_inc(zeroed, 1)
            nc.vector.memset(prob_t[:, :, :, :, :], 0.0).then_inc(zeroed, 1)
            nc.vector.memset(v_off[:, :, :], 0.0).then_inc(zeroed, 1)
            nc.vector.memset(x_shifted[:, :, :], 0.0).then_inc(zeroed, 1)
            nc.vector.memset(hidden[ONES_ROW:ONES_ROW + 1, 2, :], 1.0).then_inc(zeroed, 1)
            dve.wait_ge(const_in, 32)
            nc.vector.tensor_copy(band[:, :, :], band_in[:, :, :]).then_inc(zeroed, 1)
            dve.wait_ge(zeroed, 6)
            dve.sem_inc(qk_free, 2)
            dve.sem_inc(score_banks_free, 1)
            chain.reset()
            with dve.Fori(0, DEPTH) as layer:
                dve.wait_ge(scale_in, layer * 16 + 16)
                nc.vector.tensor_tensor(rot[:, :, :, :], rot_const[:, :, :, :], head_scale[:, :, :].unsqueeze(1).broadcast_to([128, 2, 4, HEAD_DIM]), ALU.mult).then_inc(tables_made, 1)
                dve.wait_ge(tables_made, layer + 1)
                alone(dve)

                def norm_pass(p, pair):
                    dve.wait_ge(x_shifted_in, p * 48 + 48)
                    alone(dve)
                    layer_norm_tiles(nc, dve, chain, lambda t: x_shifted[:, bass.ds(pair * PASS_TILES + t, 1), :].rearrange("p a n -> p (a n)"),
                                     lambda t: f_n[:, 128 * t:128 * t + 128], (f_stats, f_mv, f_var)).then_inc(f_normed, 1)

                def attention_pass(p, pair, first=False, last=False):

                    def rotate(i):
                        half = (i // 2) % 2
                        dve.wait_ge(rot_free, p * CHUNKS + (i + 1))
                        for n in range(2):
                            dve.wait_ge(squared, p * (2 * CHUNKS) + (2 * i + n + 1))
                            source = flat(n).rearrange("p (h d) -> p h d", h=GROUP)
                            swapped = flat(n).rearrange("p (h s d) -> p h s d", h=GROUP, s=2)[:, :, ::-1, :]
                            c_tab = rot[:, half, 2 * n, :].unsqueeze(1).broadcast_to([128, GROUP, HEAD_DIM])
                            s_tab = rot[:, half, 2 * n + 1, :].rearrange("p (s d) -> p s d", s=2).unsqueeze(1).broadcast_to([128, GROUP, 2, 32])
                            chain.mark(nc.vector.tensor_tensor(rot_a[:, i % 2, n, :].rearrange("p (h d) -> p h d", h=GROUP), source, c_tab, ALU.mult))
                            nc.vector.tensor_tensor(rot_b[:, i % 2, n, :].rearrange("p (h s d) -> p h s d", h=GROUP, s=2), swapped, s_tab, ALU.mult).then_inc(qk_free, 1)

                    def lengths_of(i):
                        y = norm[:, i % 2, :]
                        if i >= 2 or not first:
                            dve.wait_ge(k_rotated, p * CHUNKS + (i - 1))
                        dve.wait_ge(norms_made, p * CHUNKS + i)
                        chain.link(nc.vector.tensor_reduce(norm_y[:, 0, :], squares[:, i % 2, :, :].rearrange("p n (h d) -> p (n h) d", h=GROUP), AX_X, ALU.add))
                        chain.link(nc.vector.tensor_scalar(norm_y[:, 1, :], norm_y[:, 0, :], 1e-24, None, ALU.max))
                        rsqrt(nc.vector, chain, y, norm_y[:, 1, :], norm_y[:, 2, :]).then_inc(norms_made, 1)

                    def soften(j):
                        dve.wait_ge(scores_done, p * CHUNKS + (j + 1))
                        dve.wait_ge(norms_made, p * CHUNKS + (j + 1))
                        nc.vector.tensor_tensor(score[:, j % 2, :, :], flat(5).rearrange("p (h c) -> p h c", c=64),
                                                over(norm[:, j % 2, 0:GROUP], [128, GROUP, 64]), ALU.mult).then_inc(score_banks_free, 1)
                        dve.wait_ge(score_banks_free, p * CHUNKS + (j + 2))
                        nc.vector.tensor_reduce(stat[:, 0, :], score[:, j % 2, :, :], AX_X, ALU.max).then_inc(maxed, 1)

                    def normalise(j):
                        dve.wait_ge(exped, p * CHUNKS + (j + 1))
                        chain.link(nc.vector.tensor_reduce(stat[:, 1, :], score[:, j % 2, :, :], AX_X, ALU.add))
                        chain.link(nc.vector.reciprocal(stat[:, 2, :], stat[:, 1, :]))
                        dve.wait_ge(prob_turned, p * CHUNKS + j)
                        nc.vector.tensor_tensor(prob[:, :, :], score[:, j % 2, :, :], over(stat[:, 2, :], [128, GROUP, 64]), ALU.mult).then_inc(prob_made, 1)

                    for i in steps(first, last):
                        if i < CHUNKS:
                            rotate(i)
                        if in_pass(i - 2, first, last):
                            normalise(i - 2)
                        if i < CHUNKS:
                            lengths_of(i)
                        if in_pass(i - 1, first, last):
                            soften(i - 1)
                        if i == CHUNKS:
                            norm_pass(layer * PASSES, 0)
                        if (t := out_tile(i, first, last)) is not None:
                            dve.wait_ge(o_done, p * PASS_TILES + (t + 1))
                            x = x_all[:, bass.ds(pair * PASS_TOK + 128 * t, 128)]
                            nc.vector.tensor_tensor(x, x, bank[6][:, 0:128], ALU.add).then_inc(o_added, 1)
                    chain.reset()

                def feed_forward(p, pair, last=False):
                    if not last:
                        dve.wait_ge(f_again, p + 1)
                        norm_pass(p + 1, pair + 1)
                    for k, (at, n) in enumerate(FF):
                        dve.wait_ge(f_up, p * 3 + (k + 1))
                        dve.wait_ge(f_gelu, p * 3 + (k + 1))
                        nc.vector.scalar_tensor_tensor(hidden[0:n, k, :], bank[5 + k][0:n, :], cols[0:n, 5 + k:6 + k], gate[0:n, k, :],
                                                       ALU.add, ALU.mult).then_inc(f_hidden, 1)
                    dve.wait_ge(f_done, p + 1)
                    x = x_all[:, bass.ds(pair * PASS_TOK, PASS_TOK)]
                    nc.vector.tensor_tensor(x, x, flat(4), ALU.add).then_inc(x_stored, 1)
                    chain.reset()

                layer_passes(dve, layer, attention_pass)
                with dve.Fori(0, PASSES - 1) as pair:
                    feed_forward(layer * PASSES + pair, pair)
                feed_forward(layer * PASSES + (PASSES - 1), PASSES - 1, last=True)

        @block.gpsimd
        def _(pool):
            pool.sem_inc(rot_free, 2)
            nc.gpsimd.tensor_copy(xw[:, :], x_all[:, 0:PASS_TOK]).then_inc(x_taken, 1)
            with pool.Fori(0, DEPTH) as layer:

                def attention_pass(p, pair, first=False, last=False):

                    def take_next_x():
                        pool.wait_ge(x_turned, p + 1)
                        alone(pool)
                        nc.gpsimd.tensor_copy(xw[:, :], x_all[:, bass.ds((pair + 1) * PASS_TOK, PASS_TOK)]).then_inc(x_taken, 1)

                    def sub_max(j):
                        pool.wait_ge(maxed, p * CHUNKS + (j + 1))
                        nc.gpsimd.tensor_tensor(score[:, j % 2, :, :], score[:, j % 2, :, :], over(stat[:, 0, :], [128, GROUP, 64]), ALU.subtract).then_inc(shifted, 1)

                    def add_up(i):
                        pool.wait_ge(qk_free, p * (2 * CHUNKS) + (2 * i + 3))
                        if i >= 2 or not first:
                            pool.wait_ge(qk_turned, p * (2 * CHUNKS) + (2 * i - 2))
                        nc.gpsimd.tensor_tensor(qk[:, i % 2, 0, :], rot_a[:, i % 2, 0, :], rot_b[:, i % 2, 0, :], ALU.add).then_inc(q_rotated, 1)
                        pool.wait_ge(qk_free, p * (2 * CHUNKS) + (2 * i + 4))
                        nc.gpsimd.tensor_tensor(qk[:, i % 2, 1, :], rot_a[:, i % 2, 1, :], rot_b[:, i % 2, 1, :], ALU.add).then_inc(rot_free, 1)
                        pool.wait_ge(rot_free, p * CHUNKS + (i + 3))
                        pool.wait_ge(norms_made, p * CHUNKS + (i + 1))
                        k_heads = qk[:, i % 2, 1, :].rearrange("p (h d) -> p h d", h=GROUP)
                        nc.gpsimd.tensor_tensor(k_heads, k_heads, over(norm[:, i % 2, GROUP:2 * GROUP], [128, GROUP, HEAD_DIM]), ALU.mult).then_inc(k_rotated, 1)

                    for i in steps(first, last):
                        if i < CHUNKS:
                            add_up(i)
                        if i == CHUNKS - 3 and not last:
                            take_next_x()
                        if in_pass(i - 1, first, last):
                            sub_max(i - 1)

                layer_passes(pool, layer, attention_pass)
                pool.wait_ge(x_turned, layer * PASSES + PASSES)
                pool.wait_ge(x_stored, layer * PASSES + 1)
                alone(pool)
                nc.gpsimd.tensor_copy(xw[:, :], x_all[:, 0:PASS_TOK]).then_inc(x_taken, 1)

        @block.scalar
        def _(act):
            act.wait_ge(zeroed, 6)
            with act.Fori(0, DEPTH) as layer:
                act.wait_ge(w_ff_in, layer * 48 + 48)

                def shift_in(p):
                    act.wait_ge(x_turned, p + 1)
                    source = flat(6).rearrange("p (s n) -> p s n", s=2)
                    nc.scalar.activation(xs_t[0:64, :, :], source[0:64, :, :], ACT.Copy).then_inc(xs_made, 1)
                    nc.scalar.activation(xs_t[64:128, :, 1:SEQ], source[64:128, :, 0:SEQ - 1], ACT.Copy).then_inc(xs_made, 1)

                shift_in(layer * PASSES)

                def attention_pass(p, pair, first=False, last=False):

                    def square(i, n):
                        if i >= 1 or not first:
                            act.wait_ge(norms_made, p * CHUNKS + (i - 1))
                        act.wait_ge(qk_proj, p * (2 * CHUNKS) + (2 * i + n + 1))
                        nc.scalar.activation(squares[:, i % 2, n, :], flat(n), ACT.Square).then_inc(squared, 1)

                    def copy_values(i):
                        act.wait_ge(v_proj, p * CHUNKS + (i + 1))
                        act.wait_ge(v_moved[i % 4], p * 32 + 16 * (i // 4))
                        if i % 4 < 2:
                            act.wait_ge(v_carried[i % 2], p * 32 + 16 * (i // 4))
                        if i >= 4 or not first:
                            act.wait_ge(mixed, p * CHUNKS + (i - 3))
                        nc.scalar.activation(v[:, i % 4, :], flat(2), ACT.Copy).then_inc(v_made, 1)

                    def copy_turned_qk(j):
                        t, g = j // 2, j % 2
                        act.wait_ge(qk_turned, p * (2 * CHUNKS) + (2 * j + 1))
                        act.wait_ge(scores_done, p * CHUNKS + j)
                        nc.scalar.activation(q_t[:, :], flat(3), ACT.Copy).then_inc(qk_t_made, 1)
                        act.wait_ge(qk_turned, p * (2 * CHUNKS) + (2 * j + 2))
                        at = WINDOW + 128 * (t % 2)
                        for n in range(2):
                            r = 64 * n
                            nc.scalar.activation(k_t[r:r + 64, n, 4 * g:4 * g + 4, at:at + 128], flat(4)[r:r + 64, :].rearrange("p (b n) -> p b n", b=4), ACT.Copy).then_inc(qk_t_made, 1)

                    def copy_turned_prob(j):
                        act.wait_ge(prob_turned, p * CHUNKS + (j + 1))
                        act.wait_ge(mixed, p * CHUNKS + j)
                        for s in range(2):
                            r = 64 * s
                            source = flat(7)[r:r + 64, :].rearrange("p (h u q) -> p u h q", h=GROUP, u=2)
                            nc.scalar.activation(prob_t[r:r + 64, :, :, s, :], source, ACT.Copy).then_inc(prob_t_made, 1)

                    def exponential(j):
                        act.wait_ge(shifted, p * CHUNKS + (j + 1))
                        nc.scalar.activation(score[:, j % 2, :, :], score[:, j % 2, :, :], ACT.Exp, scale=QK_SCALE).then_inc(exped, 1)

                    def copy_mixed(j):
                        t, g = j // 2, j % 2
                        act.wait_ge(mixed, p * CHUNKS + (j + 1))
                        at = 128 * (t % PASS_TILES)
                        for u in range(2):
                            for n in range(2):
                                r = 64 * n
                                source = flat(3 + u)[r:r + 64, :].rearrange("p (b n s q) -> p b n s q", b=4, n=2, s=2)[:, :, n, :, :]
                                to = out_t[r:r + 64, 4 * g:4 * g + 4, at:at + 128].rearrange("p b (s u q) -> p b s u q", s=2, u=2)[:, :, :, u, :]
                                nc.scalar.activation(to, source, ACT.Copy).then_inc(mix_out, 1)

                    if first:
                        square(0, 0)
                        square(0, 1)
                    for i in steps(first, last):
                        ahead = i + 1 < CHUNKS or not last
                        if in_pass(i - 1, first, last):
                            copy_turned_qk(i - 1)
                        if i < CHUNKS:
                            copy_values(i)
                        if i == CHUNKS - 1 and not last:
                            shift_in(p + 1)
                        if in_pass(i - 2, first, last):
                            copy_turned_prob(i - 2)
                        if ahead:
                            square(i + 1, 0)
                        if in_pass(i - 2, first, last):
                            copy_mixed(i - 2)
                        if in_pass(i - 1, first, last):
                            exponential(i - 1)
                        if ahead:
                            square(i + 1, 1)

                layer_passes(act, layer, attention_pass)

                def affine(p):
                    act.wait_ge(f_again, p + 1)
                    nc.scalar.activation(f_nt[:, :], flat(3), ACT.Identity, scale=cols[:, 0:1], bias=cols[:, 1:2]).then_inc(f_affine, 1)

                def feed_forward(p, last=False):
                    act.wait_ge(f_hidden, p * 3)
                    for k, (at, n) in enumerate(FF):
                        act.wait_ge(f_gate, p * 3 + (k + 1))
                        nc.scalar.activation(gate[0:n, k, :], bank[k][0:n, :], ACT.Gelu, bias=cols[0:n, 2 + k:3 + k]).then_inc(f_gelu, 1)
                    if not last:
                        affine(p + 1)

                affine(layer * PASSES)
                with act.Fori(0, PASSES - 1) as pair:
                    feed_forward(layer * PASSES + pair)
                feed_forward(layer * PASSES + (PASSES - 1), last=True)

def kernel_attention(nc, x_all, ident, dram):
    M, EPS = 32, 1e-6
    with ExitStack() as ctx:
        def sb(name, shape, dt=F32):
            return ctx.enter_context(nc.sbuf_tensor("k_" + name, shape, dt))

        used = []

        def sem(name):
            used.append(ctx.enter_context(nc.semaphore("k_" + name)))
            return used[-1]

        bank = [ctx.enter_context(nc.psum_tensor(f"k_bank{i}", [128, 512], F32)) for i in range(6)]
        proj = sb("proj", [128, M])
        ctx_all = sb("ctx_all", [128, BATCH * CTX])
        ctx_rows = sb("ctx_rows", [CTX, BATCH, DIM])
        ctx_t = sb("ctx_t", [128, 2 * CTX])
        ctx_1 = sb("ctx_1", [CTX, 2, DIM + 1])
        work = (sb("stats", [128, PASS_TILES, 6]), sb("mv", [128, PASS_TILES, 2]), sb("var", [128, 3, PASS_TILES]))
        xn = sb("xn", [128, PASS_TOK])
        xn_t = sb("xn_t", [128, PASS_TOK])
        phi_q = sb("phi_q", [M, PASS_TOK])
        phi_k = sb("phi_k", [CTX, 2, M])
        kvz = sb("kvz", [M, 2, DIM + 1])
        den = sb("den", [128, 2, PASS_TILES])
        loaded, consts, own_v = sem("loaded"), sem("consts"), sem("own_vector")
        normed, x_turned, xn_t_made, ctx_taken = sem("normed"), sem("x_turned"), sem("xn_t_made"), sem("ctx_taken")
        k_done, k_exped, kv_done, kvz_made, q_done, q_exped = sem("k_done"), sem("k_exped"), sem("kv_done"), sem("kvz_made"), sem("q_done"), sem("q_exped")
        o_done, x_added = sem("o_done"), sem("x_added")
        ctx.callback(clear, nc, used)
        block = ctx.enter_context(nc.Block())

        @block.sync
        def _(sp):
            sp.dma_start(ctx_all[:, :], dram["ctx_t"]).then_inc(loaded, 16)
            sp.dma_start(ctx_rows[:, :, :], dram["ctx_rows"]).then_inc(loaded, 16)
            sp.dma_start(proj[:, :], dram["k_proj"]).then_inc(loaded, 16)

        @block.gpsimd
        def _(pool):
            nc.gpsimd.memset(ctx_1[:, :, :], 1.0).then_inc(consts, 1)
            pool.wait_ge(loaded, 48)
            pool.wait_ge(consts, 1)
            with pool.Fori(0, PASSES) as p:
                pool.wait_ge(kv_done, p)
                nc.gpsimd.tensor_copy(ctx_1[:, :, 0:DIM], ctx_rows[:, bass.ds(p * 2, 2), :]).then_inc(ctx_taken, 1)
                nc.gpsimd.tensor_copy(ctx_t[:, :], ctx_all[:, bass.ds(p * 2 * CTX, 2 * CTX)]).then_inc(ctx_taken, 1)

        @block.tensor
        def _(pe):
            pe.wait_ge(loaded, 48)
            with pe.Fori(0, PASSES) as p:
                pe.wait_ge(ctx_taken, p * 2 + 2)
                for b in range(2):
                    last = nc.tensor.matmul(bank[0][0:CTX, M * b:M * b + M], ctx_t[:, CTX * b:CTX * b + CTX], proj[:, :], start=True, stop=True)
                last.then_inc(k_done, 1)
                pe.wait_ge(k_exped, p + 1)
                alone(pe)
                for b in range(2):
                    last = nc.tensor.matmul(bank[1][0:M, 129 * b:129 * b + 129], phi_k[:, b, :], ctx_1[:, b, :], start=True, stop=True)
                last.then_inc(kv_done, 1)
                pe.wait_ge(normed, p + 1)
                for t in range(PASS_TILES):
                    last = nc.tensor.transpose(bank[2][:, 128 * t:128 * t + 128], xn[:, 128 * t:128 * t + 128], ident[:, :])
                last.then_inc(x_turned, 1)
                pe.wait_ge(xn_t_made, p + 1)
                nc.tensor.matmul(bank[3][0:M, :], proj[:, :], xn_t[:, :], start=True, stop=True).then_inc(q_done, 1)
                pe.wait_ge(q_exped, p + 1)
                pe.wait_ge(kvz_made, p + 1)
                pe.wait_ge(x_added, p * PASS_TILES)
                for t in range(PASS_TILES):
                    last = nc.tensor.matmul(bank[4 + t // 2][:, 129 * (t % 2):129 * (t % 2) + 129], phi_q[:, 128 * t:128 * t + 128], kvz[:, t // 2, :], start=True, stop=True)
                last.then_inc(o_done, 1)

        @block.vector
        def _(dve):
            chain = Chain(dve, own_v)

            def norm_pass(p):
                dve.wait_ge(x_turned, p)
                alone(dve)
                layer_norm_tiles(nc, dve, chain, lambda t: x_all[:, bass.ds(p * PASS_TOK + 128 * t, 128)],
                                 lambda t: xn[:, 128 * t:128 * t + 128], work).then_inc(normed, 1)

            def one_pass(p, last_pass=False):
                if not last_pass:
                    norm_pass(p + 1)
                dve.wait_ge(o_done, p + 1)
                dve.wait_ge(x_added, p * PASS_TILES)
                for b in range(2):
                    sums = bank[4 + b][:, 0:258].rearrange("p (t n) -> p t n", n=129)[:, :, 128]
                    chain.mark(nc.vector.tensor_scalar(den[:, 0, 2 * b:2 * b + 2], sums, EPS, None, ALU.add))
                chain.wait()
                chain.link(nc.vector.reciprocal(den[:, 1, :], den[:, 0, :]))
                for t in range(PASS_TILES):
                    tile = x_all[:, bass.ds(p * PASS_TOK + 128 * t, 128)]
                    nc.vector.scalar_tensor_tensor(tile, bank[4 + t // 2][:, 129 * (t % 2):129 * (t % 2) + 128], den[:, 1, t:t + 1], tile, ALU.mult, ALU.add).then_inc(x_added, 1)
                chain.reset()

            norm_pass(0)
            chain.reset()
            with dve.Fori(0, PASSES - 1) as p:
                one_pass(p)
            one_pass(PASSES - 1, last_pass=True)

        @block.scalar
        def _(act):
            with act.Fori(0, PASSES) as p:
                act.wait_ge(k_done, p + 1)
                nc.scalar.activation(phi_k[:, :, :], bank[0][0:CTX, 0:2 * M].rearrange("p (b m) -> p b m", b=2), ACT.Exp, scale=DIM ** -0.5).then_inc(k_exped, 1)
                act.wait_ge(kv_done, p + 1)
                nc.scalar.activation(kvz[:, :, :], bank[1][0:M, 0:258].rearrange("p (b m) -> p b m", b=2), ACT.Copy, scale=M ** -0.5).then_inc(kvz_made, 1)
                act.wait_ge(x_turned, p + 1)
                nc.scalar.activation(xn_t[:, :], bank[2][:, :], ACT.Copy).then_inc(xn_t_made, 1)
                act.wait_ge(q_done, p + 1)
                nc.scalar.activation(phi_q[:, :], bank[3][0:M, :], ACT.Exp, scale=DIM ** -0.5).then_inc(q_exped, 1)


def quantise(nc, chain, out, value, work):
    chain.link(nc.vector.tensor_scalar(work, value, ROUND, None, ALU.add))
    chain.link(nc.vector.tensor_scalar(work, work, ROUND, -128.0, ALU.subtract, ALU.max))
    return nc.vector.tensor_scalar(out, work, 127.0, None, ALU.min)


def quantised_ffn(nc, x_all, s_all, ident, dram):
    QMAX = 127.0
    K = 3
    with ExitStack() as ctx:
        def sb(name, shape, dt=F32):
            return ctx.enter_context(nc.sbuf_tensor("q_" + name, shape, dt))

        used = []

        def sem(name):
            used.append(ctx.enter_context(nc.semaphore("q_" + name)))
            return used[-1]

        bank = [ctx.enter_context(nc.psum_tensor(f"q_bank{i}", [128, 512], F32)) for i in range(8)]
        w_gu = sb("w_gu", [128, 2 * K, DIM])
        w_d = sb("w_d", [128, K * 128])
        w_work = sb("w_work", [128, 2 * K * DIM])
        w_work2 = sb("w_work2", [128, 2 * K * DIM])
        w_gu_t = sb("w_gu_t", [128, 2 * K, 128], BF16)
        w_d_t = sb("w_d_t", [128, K, 128], BF16)
        clips = sb("clips", [128, 2])
        sig = sb("sig", [128, 2])
        top = sb("top", [128, 4])
        sc = sb("sc", [128, 2 * K + 1])
        inv = sb("inv", [128, 2 * K + 1])
        act_scale = sb("act_scale", [128, 4])
        gu_scale = sb("gu_scale", [128, 2 * K])
        diag = sb("diag", [128, 128])
        ones = sb("ones", [128, 128])
        out_scale = sb("out_scale", [128, 128])
        xi = sb("xi", [128, 2, PASS_TOK])
        xi_t = sb("xi_t", [128, PASS_TOK], BF16)
        gate = sb("gate", [128, K, PASS_TOK])
        h_all = sb("h_all", [128, K, TILES * 128])
        h_top = sb("h_top", [128, PASSES, K])
        h_work = sb("h_work", [128, K, PASS_TOK])
        h_int = sb("h_int", [128, K, PASS_TOK], BF16)
        y = sb("y", [128, PASS_TOK])

        loaded, own_v, own_p = sem("loaded"), sem("own_vector"), sem("own_pool")
        amax_made, amax_all, sig_made = sem("amax_made"), sem("amax_all"), sem("sig_made")
        w_rounded, w_turned, w_t_made, diag_made, d_spread = sem("w_rounded"), sem("w_turned"), sem("w_t_made"), sem("diag_made"), sem("d_spread")

        ctx.callback(clear, nc, used)
        with nc.Block() as block:

            @block.sync
            def _(sp):
                sp.dma_start(w_gu[:, :, :], dram["q_gu"]).then_inc(loaded, 16)
                sp.dma_start(w_d[:, :], dram["q_d"]).then_inc(loaded, 16)
                sp.dma_start(clips[:, :], dram["q_clips"]).then_inc(loaded, 16)

            @block.gpsimd
            def _(pool):
                nc.gpsimd.memset(ones[:, :], 1.0).then_inc(own_p, 1)
                pool.wait_ge(amax_made, 1)
                nc.gpsimd.partition_all_reduce(top[:, 1:2], top[:, 0:1], 128, bass.bass_isa.ReduceOp.max).then_inc(amax_all, 1)

            @block.scalar
            def _(act):
                act.wait_ge(loaded, 48)
                nc.scalar.activation(sig[:, :], clips[:, :], ACT.Sigmoid).then_inc(sig_made, 1)
                for k in range(2 * K):
                    act.wait_ge(w_turned, k + 1)
                    nc.scalar.activation(w_gu_t[:, k, :], bank[k][:, 0:128], ACT.Copy).then_inc(w_t_made, 1)
                for k in range(K):
                    act.wait_ge(w_turned, 2 * K + k + 1)
                    nc.scalar.activation(w_d_t[:, k, :], bank[6 + k % 2][:, 0:128], ACT.Copy).then_inc(w_t_made, 1)
                act.wait_ge(d_spread, 1)
                nc.scalar.activation(out_scale[:, :], bank[0][:, 0:128], ACT.Copy).then_inc(w_t_made, 1)

            @block.tensor
            def _(pe):
                pe.wait_ge(w_rounded, 1)
                for k in range(2 * K):
                    nc.tensor.transpose(bank[k][:, 0:128], w_work2[:, 128 * k:128 * k + 128], ident[:, :]).then_inc(w_turned, 1)
                pe.wait_ge(w_rounded, 2)
                for k in range(K):
                    if k == 2:
                        pe.wait_ge(w_t_made, 2 * K + 1)
                    nc.tensor.transpose(bank[6 + k % 2][:, 0:128], w_work[:, 128 * k:128 * k + 128], ident[:, :]).then_inc(w_turned, 1)
                pe.wait_ge(diag_made, 1)
                pe.wait_ge(own_p, 1)
                nc.tensor.matmul(bank[0][:, 0:128], ones[:, :], diag[:, :], start=True, stop=True).then_inc(d_spread, 1)

            @block.vector
            def _(dve):
                chain = Chain(dve, own_v)
                nc.vector.tensor_reduce(top[:, 0:1], s_all[:, :], AX_X, ALU.max, apply_absolute_value=True).then_inc(amax_made, 1)
                dve.wait_ge(loaded, 48)
                chain.mark(nc.vector.tensor_reduce(sc[:, 0:2 * K], w_gu[:, :, :], AX_X, ALU.max, apply_absolute_value=True))
                chain.link(nc.vector.tensor_reduce(sc[:, 2 * K:2 * K + 1], w_d[:, :], AX_X, ALU.max, apply_absolute_value=True))
                chain.link(nc.vector.tensor_scalar(sc[:, :], sc[:, :], 1 / QMAX, 1e-30, ALU.mult, ALU.max))
                chain.link(nc.vector.reciprocal(inv[:, :], sc[:, :]))
                shape = [128, 2 * K, DIM]
                chain.link(nc.vector.tensor_tensor(w_work[:, :].rearrange("p (k n) -> p k n", k=2 * K), w_gu[:, :, :], over(inv[:, 0:2 * K], shape), ALU.mult))
                quantise(nc, chain, w_work2[:, :], w_work[:, :], w_work[:, :]).then_inc(w_rounded, 1)
                dve.wait_ge(w_rounded, 1)
                chain.link(nc.vector.tensor_scalar(w_work[:, 0:K * 128], w_d[:, :], inv[:, 2 * K:2 * K + 1], None, ALU.mult))
                quantise(nc, chain, w_work[:, 0:K * 128], w_work[:, 0:K * 128], w_work[:, 0:K * 128]).then_inc(w_rounded, 1)
                nc.vector.tensor_scalar(diag[:, :], ident[:, :], sc[:, 2 * K:2 * K + 1], None, ALU.mult).then_inc(diag_made, 1)
                dve.wait_ge(sig_made, 1)
                dve.wait_ge(amax_all, 1)
                chain.link(nc.vector.tensor_tensor(act_scale[:, 0:1], sig[:, 0:1], top[:, 1:2], ALU.mult))
                chain.link(nc.vector.tensor_scalar(act_scale[:, 0:1], act_scale[:, 0:1], 1 / QMAX, None, ALU.mult))
                chain.link(nc.vector.reciprocal(act_scale[:, 1:2], act_scale[:, 0:1]))
                chain.link(nc.vector.tensor_scalar(gu_scale[:, :], sc[:, 0:2 * K], act_scale[:, 0:1], None, ALU.mult))

        with ExitStack() as loop:
            used_here = []

            def sem(name):
                used_here.append(loop.enter_context(nc.semaphore("qa_" + name)))
                return used_here[-1]

            own, x_rounded, x_turned, x_t_made, projected, silued, h_made = (
                sem("own"), sem("x_rounded"), sem("x_turned"), sem("x_t_made"), sem("projected"), sem("silued"), sem("h_made"))
            loop.callback(clear, nc, used_here)
            block = loop.enter_context(nc.Block())

            @block.vector
            def _(dve):
                chain = Chain(dve, own)
                with dve.Fori(0, PASSES) as p:
                    s = s_all[:, bass.ds(p * PASS_TOK, PASS_TOK)]
                    chain.link(nc.vector.tensor_scalar(xi[:, 1, :], s, act_scale[:, 1:2], None, ALU.mult))
                    quantise(nc, chain, xi[:, 0, :], xi[:, 1, :], xi[:, 1, :]).then_inc(x_rounded, 1)
                    for k in range(K):
                        dve.wait_ge(projected, p * (2 * K) + 2 * k + 2)
                        dve.wait_ge(silued, p * K + (k + 1))
                        h = h_all[:, k, bass.ds(p * PASS_TOK, PASS_TOK)]
                        nc.vector.scalar_tensor_tensor(h, bank[1 + 2 * k][:, :], gu_scale[:, K + k:K + k + 1], gate[:, k, :], ALU.mult, ALU.mult).then_inc(h_made, 1)
                        dve.wait_ge(h_made, p * K + (k + 1))
                        chain.link(nc.vector.tensor_reduce(h_top[:, bass.ds(p, 1), k], h, AX_X, ALU.max, apply_absolute_value=True))
                    chain.reset()

            @block.tensor
            def _(pe):
                with pe.Fori(0, PASSES) as p:
                    pe.wait_ge(x_rounded, p + 1)
                    for t in range(PASS_TILES):
                        last = nc.tensor.transpose(bank[7][:, 128 * t:128 * t + 128], xi[:, 0, 128 * t:128 * t + 128], ident[:, :])
                    last.then_inc(x_turned, 1)
                    pe.wait_ge(x_t_made, p + 1)
                    pe.wait_ge(h_made, p * K)
                    for k in range(K):
                        for n in range(2):
                            nc.tensor.matmul(bank[2 * k + n][:, :], w_gu_t[:, K * n + k, :], xi_t[:, :], start=True, stop=True).then_inc(projected, 1)

            @block.scalar
            def _(act):
                with act.Fori(0, PASSES) as p:
                    act.wait_ge(x_turned, p + 1)
                    nc.scalar.activation(xi_t[:, :], bank[7][:, :], ACT.Copy).then_inc(x_t_made, 1)
                    act.wait_ge(h_made, p * K)
                    for k in range(K):
                        act.wait_ge(projected, p * (2 * K) + 2 * k + 1)
                        nc.scalar.activation(gate[:, k, :], bank[2 * k][:, :], ACT.Silu, scale=gu_scale[:, k:k + 1]).then_inc(silued, 1)

        with ExitStack() as loop:
            used_here = []

            def sem(name):
                used_here.append(loop.enter_context(nc.semaphore("qb_" + name)))
                return used_here[-1]

            own, h_amax, h_all_max, h_rounded, downed, x_added = sem("own"), sem("h_amax"), sem("h_all_max"), sem("h_rounded"), sem("downed"), sem("x_added")
            loop.callback(clear, nc, used_here)
            block = loop.enter_context(nc.Block())

            @block.gpsimd
            def _(pool):
                pool.wait_ge(h_amax, 1)
                nc.gpsimd.partition_all_reduce(top[:, 3:4], top[:, 2:3], 128, bass.bass_isa.ReduceOp.max).then_inc(h_all_max, 1)

            @block.vector
            def _(dve):
                chain = Chain(dve, own)
                nc.vector.tensor_reduce(top[:, 2:3], h_top[:, :, :].rearrange("p a b -> p (a b)"), AX_X, ALU.max).then_inc(h_amax, 1)
                dve.wait_ge(h_all_max, 1)
                chain.link(nc.vector.tensor_tensor(act_scale[:, 2:3], sig[:, 1:2], top[:, 3:4], ALU.mult))
                chain.link(nc.vector.tensor_scalar(act_scale[:, 2:3], act_scale[:, 2:3], 1 / QMAX, None, ALU.mult))
                chain.link(nc.vector.reciprocal(act_scale[:, 3:4], act_scale[:, 2:3]))
                chain.link(nc.vector.tensor_scalar(out_scale[:, :], out_scale[:, :], act_scale[:, 2:3], None, ALU.mult))
                chain.reset()
                with dve.Fori(0, PASSES) as p:
                    dve.wait_ge(downed, p)
                    for k in range(K):
                        h = h_all[:, k, bass.ds(p * PASS_TOK, PASS_TOK)]
                        chain.link(nc.vector.tensor_scalar(h_work[:, k, :], h, act_scale[:, 3:4], None, ALU.mult))
                        quantise(nc, chain, h_int[:, k, :], h_work[:, k, :], h_work[:, k, :]).then_inc(h_rounded, 1)
                    dve.wait_ge(downed, p + 1)
                    chain.link(nc.vector.tensor_tensor(y[:, :].rearrange("p (t n) -> p t n", n=128), bank[0][:, :].rearrange("p (t n) -> p t n", n=128),
                                                       out_scale[:, :].unsqueeze(1).broadcast_to([128, PASS_TILES, 128]), ALU.mult))
                    x = x_all[:, bass.ds(p * PASS_TOK, PASS_TOK)]
                    nc.vector.tensor_tensor(x, x, y[:, :], ALU.add).then_inc(x_added, 1)
                    chain.reset()

            @block.tensor
            def _(pe):
                with pe.Fori(0, PASSES) as p:
                    pe.wait_ge(h_rounded, p * K + K)
                    pe.wait_ge(x_added, p)
                    for t in range(PASS_TILES):
                        for k in range(K):
                            last = nc.tensor.matmul(bank[0][:, 128 * t:128 * t + 128], h_int[:, k, 128 * t:128 * t + 128], w_d_t[:, k, :], start=(k == 0), stop=(k == K - 1))
                    last.then_inc(downed, 1)


def two_attentions(nc, x_all, ident, ident_bf, dram):
    EPS, LEAK = 1e-3, 0.2
    SELF_SCALE, CTX_SCALE = SEQ ** -0.5, CTX ** -0.5
    W_NAMES = ("a_Wk1", "a_Wq1", "a_Wv1", "a_Wk2", "a_Wq2", "a_Wv2", "a_W1", "a_W2")
    WK1, WQ1, WV1, WK2, WQ2, WV2, W1, W2 = range(8)
    with ExitStack() as ctx:
        def sb(name, shape, dt=F32):
            return ctx.enter_context(nc.sbuf_tensor("a_" + name, shape, dt))

        used = []

        def sem(name):
            used.append(ctx.enter_context(nc.semaphore("a_" + name)))
            return used[-1]

        bank = [ctx.enter_context(nc.psum_tensor(f"a_bank{i}", [128, 512], F32)) for i in range(8)]
        w = sb("w", [128, 8, DIM])
        rows = sb("rows", [128, 3, DIM])
        GAMMA, BETA, B2 = range(3)
        b1 = sb("b1", [128, 1])
        causal_in = sb("causal_in", [128, 128])
        causal = sb("causal", [128, 128], BF16)
        ctx_all = sb("ctx_all", [128, BATCH * CTX])
        ctx_t = sb("ctx_t", [128, 2 * CTX])
        work = (sb("stats", [128, PASS_TILES, 6]), sb("mv", [128, PASS_TILES, 2]), sb("var", [128, 3, PASS_TILES]))
        xn = sb("xn", [128, PASS_TOK])
        xn_t = sb("xn_t", [128, PASS_TOK])
        k1 = sb("k1", [128, PASS_TOK])
        q1 = sb("q1", [128, PASS_TOK])
        v1 = sb("v1", [128, PASS_TOK])
        k2 = sb("k2", [128, 2 * CTX])
        v2 = sb("v2", [CTX, 2, DIM])
        top = sb("top", [128, 2, PASS_TILES])
        total = sb("total", [128, 2, PASS_TILES])
        prob = sb("prob", [128, PASS_TILES, SEQ])
        prob_t = sb("prob_t", [128, 6, 128])
        att = sb("att", [128, PASS_TOK])
        att_t = sb("att_t", [128, PASS_TOK])
        q2 = sb("q2", [128, PASS_TOK])
        y = sb("y", [128, 3, PASS_TOK])
        n1 = sb("n1", [128, PASS_TOK])
        n2 = sb("n2", [128, PASS_TOK])
        n2_t = sb("n2_t", [128, PASS_TOK])
        s2 = sb("s2", [128, PASS_TILES, CTX])
        top2 = sb("top2", [128, 3, PASS_TILES])
        s2_t = sb("s2_t", [CTX, PASS_TOK])
        h = sb("h", [128, 2, PASS_TOK])

        loaded, causal_made, own_v = sem("loaded"), sem("causal_made"), sem("own_vector")
        normed, x_turned, xn_t_made, ctx_taken = sem("normed"), sem("x_turned"), sem("xn_t_made"), sem("ctx_taken")
        projected, kq_made, v1_made, kv2_made = sem("projected"), sem("kq_made"), sem("v1_made"), sem("kv2_made")
        s1_done, top_made, exp_made, p_turned, p_t_made, att_done, att_made = (
            sem("s1_done"), sem("top_made"), sem("exp_made"), sem("p_turned"), sem("p_t_made"), sem("att_done"), sem("att_made"))
        att_turned, att_t_made, q2_done, q2_made, s2_done, s2_sub, s2_exp, s2_turned, s2_t_made, att2_done = (
            sem("att_turned"), sem("att_t_made"), sem("q2_done"), sem("q2_made"), sem("s2_done"), sem("s2_sub"), sem("s2_exp"), sem("s2_turned"), sem("s2_t_made"), sem("att2_done"))
        n2_made, n2_turned, n2_t_made, h_done, h_made, ff_done = (
            sem("n2_made"), sem("n2_turned"), sem("n2_t_made"), sem("h_done"), sem("h_made"), sem("ff_done"))
        ctx.callback(clear, nc, used)
        block = ctx.enter_context(nc.Block())
        BLOCKS = [(t, b) for t in range(PASS_TILES) for b in range(t % 2 + 1)]
        SCORE_BANK = (5, 6, 7, 0)

        def tile(ap, t):
            return ap[:, 128 * t:128 * t + 128]

        @block.sync
        def _(sp):
            for n, name in enumerate(W_NAMES):
                sp.dma_start(w[:, n, :], dram[name]).then_inc(loaded, 16)
            sp.dma_start(rows[:, :, :], dram["a_rows"]).then_inc(loaded, 16)
            sp.dma_start(b1[:, :], dram["a_b1"]).then_inc(loaded, 16)
            sp.dma_start(causal_in[:, :], dram["causal"]).then_inc(loaded, 16)
            sp.dma_start(ctx_all[:, :], dram["ctx_t"]).then_inc(loaded, 16)

        @block.gpsimd
        def _(pool):
            pool.wait_ge(loaded, 192)
            with pool.Fori(0, PASSES) as p:
                pool.wait_ge(kv2_made, p)
                nc.gpsimd.tensor_copy(ctx_t[:, :], ctx_all[:, bass.ds(p * 2 * CTX, 2 * CTX)]).then_inc(ctx_taken, 1)

        @block.tensor
        def _(pe):
            pe.wait_ge(loaded, 192)
            pe.wait_ge(causal_made, 1)
            with pe.Fori(0, PASSES) as p:
                def turn(to, source, signal):
                    for t in range(PASS_TILES):
                        last = nc.tensor.transpose(tile(bank[to], t), tile(source, t), ident[:, :])
                    last.then_inc(signal, 1)

                pe.wait_ge(ctx_taken, p + 1)
                nc.tensor.matmul(bank[4][:, 0:128], w[:, WK2, :], ctx_t[:, :], start=True, stop=True)
                for b in range(2):
                    last = nc.tensor.matmul(bank[4][0:CTX, 128 + 128 * b:256 + 128 * b], ctx_t[:, CTX * b:CTX * b + CTX], w[:, WV2, :], start=True, stop=True)
                last.then_inc(projected, 1)
                pe.wait_ge(normed, p + 1)
                turn(0, xn, x_turned)
                pe.wait_ge(xn_t_made, p + 1)
                nc.tensor.matmul(bank[1][:, :], w[:, WK1, :], xn_t[:, :], start=True, stop=True).then_inc(projected, 1)
                nc.tensor.matmul(bank[2][:, :], w[:, WQ1, :], xn_t[:, :], start=True, stop=True).then_inc(projected, 1)
                for t in range(PASS_TILES):
                    last = nc.tensor.matmul(tile(bank[3], t), tile(xn_t, t), w[:, WV1, :], start=True, stop=True)
                last.then_inc(projected, 1)
                pe.wait_ge(kq_made, p * 2 + 2)
                for t in range(PASS_TILES):
                    to, n = bank[SCORE_BANK[t]], 128 * (t % 2 + 1)
                    nc.tensor.matmul(to[:, n - 128:n], ident_bf[:, :], causal[:, :], start=True, stop=True)
                    at = SEQ * (t // 2)
                    nc.tensor.matmul(to[:, 0:n], tile(q1, t), k1[:, at:at + n], start=False, stop=True, skip_group_check=True).then_inc(s1_done, 1)
                pe.wait_ge(exp_made, p * PASS_TILES + PASS_TILES)
                for n, (t, b) in enumerate(BLOCKS):
                    last = nc.tensor.transpose(bank[1 + n // 4][:, 128 * (n % 4):128 * (n % 4) + 128], prob[:, t, 128 * b:128 * b + 128], ident[:, :])
                last.then_inc(p_turned, 1)
                pe.wait_ge(v1_made, p + 1)
                pe.wait_ge(p_t_made, p * 2 + 2)
                for n, (t, b) in enumerate(BLOCKS):
                    last = nc.tensor.matmul(tile(bank[3], t), prob_t[:, n, :], tile(v1, t - t % 2 + b), start=(b == 0), stop=(b == t % 2))
                last.then_inc(att_done, 1)
                pe.wait_ge(att_made, p + 1)
                turn(0, att, att_turned)
                pe.wait_ge(att_t_made, p + 1)
                nc.tensor.matmul(bank[1][:, :], w[:, WQ2, :], att_t[:, :], start=True, stop=True).then_inc(q2_done, 1)
                pe.wait_ge(q2_made, p + 1)
                pe.wait_ge(kv2_made, p + 1)
                for t in range(PASS_TILES):
                    b = t // 2
                    last = nc.tensor.matmul(bank[2][:, CTX * t:CTX * t + CTX], tile(q2, t), k2[:, CTX * b:CTX * b + CTX], start=True, stop=True)
                last.then_inc(s2_done, 1)
                pe.wait_ge(s2_exp, p + 1)
                alone(pe)
                for t in range(PASS_TILES):
                    last = nc.tensor.transpose(bank[5][0:CTX, 128 * t:128 * t + 128], s2[:, t, :], ident[:, :])
                last.then_inc(s2_turned, 1)
                pe.wait_ge(s2_t_made, p + 1)
                for t in range(PASS_TILES):
                    last = nc.tensor.matmul(tile(bank[6], t), tile(s2_t, t), v2[:, t // 2, :], start=True, stop=True)
                last.then_inc(att2_done, 1)
                pe.wait_ge(n2_made, p + 1)
                turn(0, n2, n2_turned)
                pe.wait_ge(n2_t_made, p + 1)
                nc.tensor.matmul(bank[1][:, :], w[:, W1, :], n2_t[:, :], start=True, stop=True).then_inc(h_done, 1)
                pe.wait_ge(h_made, p + 1)
                for t in range(PASS_TILES):
                    last = nc.tensor.matmul(tile(bank[2], t), h[:, 1, 128 * t:128 * t + 128], w[:, W2, :], start=True, stop=True)
                last.then_inc(ff_done, 1)

        @block.vector
        def _(dve):
            chain = Chain(dve, own_v)
            dve.wait_ge(loaded, 192)
            nc.vector.tensor_copy(causal[:, :], causal_in[:, :]).then_inc(causal_made, 1)
            tiles = [128, PASS_TILES, 128]

            def row(n):
                return rows[:, n, :].unsqueeze(1).broadcast_to(tiles)

            def by_tile(ap):
                return ap.rearrange("p (t n) -> p t n", n=128)

            def affine_norm(source, out):
                chain.link(layer_norm_tiles(nc, dve, chain, lambda t: source[:, 128 * t:128 * t + 128], lambda t: y[:, 1, 128 * t:128 * t + 128], work, EPS))
                chain.link(nc.vector.tensor_tensor(by_tile(y[:, 2, :]), by_tile(y[:, 1, :]), row(GAMMA), ALU.mult))
                return nc.vector.tensor_tensor(by_tile(out), by_tile(y[:, 2, :]), row(BETA), ALU.add)

            with dve.Fori(0, PASSES) as p:
                layer_norm_tiles(nc, dve, chain, lambda t: x_all[:, bass.ds(p * PASS_TOK + 128 * t, 128)],
                                 lambda t: xn[:, 128 * t:128 * t + 128], work).then_inc(normed, 1)
                dve.wait_ge(projected, p * 4 + 1)
                chain.mark(nc.vector.tensor_copy(k2[:, :], bank[4][:, 0:128]))
                nc.vector.tensor_copy(v2[:, :, :], bank[4][0:CTX, 128:384].rearrange("p (b n) -> p b n", b=2)).then_inc(kv2_made, 1)
                dve.wait_ge(projected, p * 4 + 4)
                nc.vector.tensor_copy(v1[:, :], bank[3][:, :]).then_inc(v1_made, 1)
                for t in range(PASS_TILES):
                    dve.wait_ge(s1_done, p * PASS_TILES + (t + 1))
                    chain.link(nc.vector.tensor_reduce(top[:, 0, t:t + 1], bank[SCORE_BANK[t]][:, 0:128 * (t % 2 + 1)], AX_X, ALU.max))
                    nc.vector.tensor_scalar(top[:, 1, t:t + 1], top[:, 0, t:t + 1], -SELF_SCALE, None, ALU.mult).then_inc(top_made, 1)
                dve.wait_ge(exp_made, p * PASS_TILES + PASS_TILES)
                chain.link(nc.vector.reciprocal(total[:, 1, :], total[:, 0, :]))
                dve.wait_ge(att_done, p + 1)
                nc.vector.tensor_tensor(by_tile(att[:, :]), by_tile(bank[3][:, :]), over(total[:, 1, :], tiles), ALU.mult).then_inc(att_made, 1)
                dve.wait_ge(att_made, p + 1)
                chain.link(nc.vector.tensor_tensor(y[:, 0, :], att[:, :], xn[:, :], ALU.add))
                chain.link(affine_norm(y[:, 0, :], n1[:, :]))
                dve.wait_ge(s2_done, p + 1)
                scores = bank[2][:, 0:PASS_TILES * CTX].rearrange("p (t n) -> p t n", n=CTX)
                chain.link(nc.vector.tensor_reduce(top2[:, 0, :], scores, AX_X, ALU.max))
                nc.vector.tensor_tensor(s2[:, :, :], scores, over(top2[:, 0, :], [128, PASS_TILES, CTX]), ALU.subtract).then_inc(s2_sub, 1)
                dve.wait_ge(s2_exp, p + 1)
                chain.link(nc.vector.tensor_reduce(top2[:, 1, :], s2[:, :, :], AX_X, ALU.add))
                chain.link(nc.vector.reciprocal(top2[:, 2, :], top2[:, 1, :]))
                dve.wait_ge(att2_done, p + 1)
                chain.link(nc.vector.tensor_tensor(by_tile(y[:, 0, :]), by_tile(bank[6][:, :]), over(top2[:, 2, :], tiles), ALU.mult))
                chain.link(nc.vector.tensor_tensor(y[:, 0, :], y[:, 0, :], n1[:, :], ALU.add))
                affine_norm(y[:, 0, :], n2[:, :]).then_inc(n2_made, 1)
                dve.wait_ge(h_done, p + 1)
                chain.link(nc.vector.tensor_scalar(h[:, 0, :], bank[1][:, :], b1[:, :], None, ALU.add))
                nc.vector.scalar_tensor_tensor(h[:, 1, :], h[:, 0, :], LEAK, h[:, 0, :], ALU.mult, ALU.max).then_inc(h_made, 1)
                dve.wait_ge(ff_done, p + 1)
                chain.link(nc.vector.tensor_tensor(by_tile(y[:, 0, :]), by_tile(bank[2][:, :]), row(B2), ALU.add))
                chain.link(nc.vector.tensor_tensor(y[:, 0, :], y[:, 0, :], n2[:, :], ALU.add))
                chain.link(affine_norm(y[:, 0, :], n1[:, :]))
                x = x_all[:, bass.ds(p * PASS_TOK, PASS_TOK)]
                chain.link(nc.vector.scalar_tensor_tensor(x, n1[:, :], 0.0, x, ALU.max, ALU.add))
                chain.reset()

        @block.scalar
        def _(act):
            with act.Fori(0, PASSES) as p:
                def take(ready, count, to, source, signal):
                    act.wait_ge(ready, count)
                    nc.scalar.activation(to, source, ACT.Copy).then_inc(signal, 1)

                take(x_turned, p + 1, xn_t[:, :], bank[0][:, :], xn_t_made)
                take(projected, p * 4 + 2, k1[:, :], bank[1][:, :], kq_made)
                take(projected, p * 4 + 3, q1[:, :], bank[2][:, :], kq_made)
                for t in range(PASS_TILES):
                    act.wait_ge(top_made, p * PASS_TILES + (t + 1))
                    n = 128 * (t % 2 + 1)
                    nc.scalar.activation(prob[:, t, 0:n], bank[SCORE_BANK[t]][:, 0:n], ACT.Exp, bias=top[:, 1, t:t + 1], scale=SELF_SCALE,
                                         accum_out=total[:, 0, t:t + 1]).then_inc(exp_made, 1)
                take(p_turned, p + 1, prob_t[:, 0:4, :], bank[1][:, :].rearrange("p (b n) -> p b n", n=128), p_t_made)
                take(p_turned, p + 1, prob_t[:, 4:6, :], bank[2][:, 0:256].rearrange("p (b n) -> p b n", n=128), p_t_made)
                take(att_turned, p + 1, att_t[:, :], bank[0][:, :], att_t_made)
                take(q2_done, p + 1, q2[:, :], bank[1][:, :], q2_made)
                act.wait_ge(s2_sub, p + 1)
                nc.scalar.activation(s2[:, :, :], s2[:, :, :], ACT.Exp, scale=CTX_SCALE).then_inc(s2_exp, 1)
                take(s2_turned, p + 1, s2_t[:, :], bank[5][0:CTX, :], s2_t_made)
                take(n2_turned, p + 1, n2_t[:, :], bank[0][:, :], n2_t_made)


def ternary_ffn(nc, x_all, ident, dram):
    HID, K = 512, 4
    with ExitStack() as ctx:
        def sb(name, shape, dt=F32):
            return ctx.enter_context(nc.sbuf_tensor("g_" + name, shape, dt))

        used = []

        def sem(name):
            used.append(ctx.enter_context(nc.semaphore("g_" + name)))
            return used[-1]

        bank = [ctx.enter_context(nc.psum_tensor(f"g_bank{i}", [128, 512], F32)) for i in range(8)]
        w = sb("w", [128, 2, HID])
        w_cmp = sb("w_cmp", [128, 2, HID])
        w_tern = sb("w_tern", [128, 2, HID])
        size = sb("size", [128, 2, 4])
        affine = sb("affine", [128, 2, K])
        work = (sb("stats", [128, PASS_TILES, 6]), sb("mv", [128, PASS_TILES, 2]), sb("var", [128, 3, PASS_TILES]))
        xn = sb("xn", [128, PASS_TOK])
        xn_t = sb("xn_t", [128, PASS_TOK])
        h = sb("h", [128, PASS_TILES, HID])
        hn = sb("hn", [128, PASS_TILES, HID])
        hn_t = sb("hn_t", [128, K, PASS_TOK])
        loaded, own_v, own_w, sized, size_sum, tern_made = sem("loaded"), sem("own_vector"), sem("own_weights"), sem("sized"), sem("size_sum"), sem("tern_made")
        normed, x_turned, xn_t_made, h_done, gelued, h_normed, h_turned, hn_t_made, o_done, x_added = (
            sem("normed"), sem("x_turned"), sem("xn_t_made"), sem("h_done"), sem("gelued"), sem("h_normed"), sem("h_turned"), sem("hn_t_made"), sem("o_done"), sem("x_added"))
        ctx.callback(clear, nc, used)
        block = ctx.enter_context(nc.Block())

        @block.sync
        def _(sp):
            sp.dma_start(w[:, 0, :], dram["g_fc"]).then_inc(loaded, 16)
            sp.dma_start(w[:, 1, :], dram["g_proj"]).then_inc(loaded, 16)
            sp.dma_start(affine[:, :, :], dram["g_affine"]).then_inc(loaded, 16)

        @block.gpsimd
        def _(pool):
            pool.wait_ge(sized, 1)
            nc.gpsimd.partition_all_reduce(size[:, :, 1], size[:, :, 0], 128, bass.bass_isa.ReduceOp.add).then_inc(size_sum, 1)

        @block.tensor
        def _(pe):
            pe.wait_ge(tern_made, 1)
            with pe.Fori(0, PASSES) as p:
                pe.wait_ge(normed, p + 1)
                pe.wait_ge(x_added, p)
                for t in range(PASS_TILES):
                    last = nc.tensor.transpose(bank[0][:, 128 * t:128 * t + 128], xn[:, 128 * t:128 * t + 128], ident[:, :])
                last.then_inc(x_turned, 1)
                pe.wait_ge(xn_t_made, p + 1)
                for t in range(PASS_TILES):
                    nc.tensor.matmul(bank[1 + t][:, :], xn_t[:, 128 * t:128 * t + 128], w_tern[:, 0, :], start=True, stop=True).then_inc(h_done, 1)
                pe.wait_ge(h_normed, p * PASS_TILES + PASS_TILES)
                for k in range(K):
                    to = bank[5 + k % 3]
                    if k == 3:
                        pe.wait_ge(hn_t_made, p * K + 1)
                    for t in range(PASS_TILES):
                        last = nc.tensor.transpose(to[:, 128 * t:128 * t + 128], hn[:, t, 128 * k:128 * k + 128], ident[:, :])
                    last.then_inc(h_turned, 1)
                pe.wait_ge(hn_t_made, p * K + K)
                for t in range(PASS_TILES):
                    for k in range(K):
                        last = nc.tensor.matmul(bank[0][:, 128 * t:128 * t + 128], hn_t[:, k, 128 * t:128 * t + 128], w_tern[:, 1, 128 * k:128 * k + 128],
                                                start=(k == 0), stop=(k == K - 1))
                last.then_inc(o_done, 1)

        @block.vector
        def _(dve):
            weights = Chain(dve, own_w)
            dve.wait_ge(loaded, 48)
            nc.vector.tensor_reduce(size[:, :, 0], w[:, :, :], AX_X, ALU.add, apply_absolute_value=True).then_inc(sized, 1)
            dve.wait_ge(size_sum, 1)
            weights.link(nc.vector.tensor_scalar(size[:, :, 2], size[:, :, 1], 1.0 / (HID * DIM), 1e-6, ALU.mult, ALU.add))
            weights.link(nc.vector.reciprocal(size[:, :, 3], size[:, :, 2]))
            for n in range(2):
                weights.mark(nc.vector.tensor_scalar(w_cmp[:, n, :], w[:, n, :], size[:, n, 3:4], -0.5, ALU.mult, ALU.is_lt))
                weights.link(nc.vector.tensor_scalar(w_tern[:, n, :], w[:, n, :], size[:, n, 3:4], 0.5, ALU.mult, ALU.is_gt))
            nc.vector.tensor_tensor(w_tern[:, :, :], w_tern[:, :, :], w_cmp[:, :, :], ALU.subtract).then_inc(tern_made, 1)
            chain = Chain(dve, own_v)

            def norm_pass(p):
                dve.wait_ge(x_turned, p)
                alone(dve)
                layer_norm_tiles(nc, dve, chain, lambda t: x_all[:, bass.ds(p * PASS_TOK + 128 * t, 128)],
                                 lambda t: xn[:, 128 * t:128 * t + 128], work).then_inc(normed, 1)

            def one_pass(p, last_pass=False):
                stats, mv, var = work
                dve.wait_ge(normed, p + 1)
                for t in range(PASS_TILES):
                    dve.wait_ge(gelued, p * PASS_TILES + (t + 1))
                    chain.mark(nc.vector.bn_stats(stats[:, t, :], h[:, t, :]))
                chain.wait()
                for t in range(PASS_TILES):
                    chain.mark(nc.vector.bn_aggr(mv[:, t, :], stats[:, t, :]))
                chain.wait()
                chain.link(nc.vector.tensor_scalar(var[:, 0, :], mv[:, :, 1], 1e-5, None, ALU.add))
                chain.link(rsqrt(nc.vector, chain, var[:, 1, :], var[:, 0, :], var[:, 2, :]))
                for t in range(PASS_TILES):
                    nc.vector.tensor_scalar(hn[:, t, :], h[:, t, :], mv[:, t, 0:1], var[:, 1, t:t + 1], ALU.subtract, ALU.mult).then_inc(h_normed, 1)
                dve.wait_ge(h_normed, p * PASS_TILES + PASS_TILES)
                if not last_pass:
                    norm_pass(p + 1)
                dve.wait_ge(o_done, p + 1)
                x = x_all[:, bass.ds(p * PASS_TOK, PASS_TOK)]
                nc.vector.tensor_tensor(x, x, bank[0][:, :], ALU.add).then_inc(x_added, 1)
                dve.wait_ge(x_added, p + 1)
                alone(dve)
                chain.reset()

            norm_pass(0)
            chain.reset()
            with dve.Fori(0, PASSES - 1) as p:
                one_pass(p)
            one_pass(PASSES - 1, last_pass=True)

        @block.scalar
        def _(act):
            act.wait_ge(loaded, 48)
            with act.Fori(0, PASSES) as p:
                act.wait_ge(x_turned, p + 1)
                nc.scalar.activation(xn_t[:, :], bank[0][:, :], ACT.Copy).then_inc(xn_t_made, 1)
                for t in range(PASS_TILES):
                    act.wait_ge(h_done, p * PASS_TILES + (t + 1))
                    nc.scalar.activation(h[:, t, :], bank[1 + t][:, :], ACT.Gelu).then_inc(gelued, 1)
                for k in range(K):
                    act.wait_ge(h_turned, p * K + (k + 1))
                    nc.scalar.activation(hn_t[:, k, :], bank[5 + k % 3][:, :], ACT.Identity, scale=affine[:, 0, k:k + 1], bias=affine[:, 1, k:k + 1]).then_inc(hn_t_made, 1)


def context_attention(nc, x_all, ident, dram):
    with ExitStack() as ctx:
        def sb(name, shape, dt=F32):
            return ctx.enter_context(nc.sbuf_tensor("y_" + name, shape, dt))

        used = []

        def sem(name):
            used.append(ctx.enter_context(nc.semaphore("y_" + name)))
            return used[-1]

        bank = [ctx.enter_context(nc.psum_tensor(f"y_bank{i}", [128, 512], F32)) for i in range(5)]
        w = sb("w", [128, DIM])
        b = sb("b", [128, 1])
        ctx_t = sb("ctx_t", [128, BATCH * CTX])
        ctx_rows = sb("ctx_rows", [CTX, BATCH, DIM])
        work = (sb("stats", [128, PASS_TILES, 6]), sb("mv", [128, PASS_TILES, 2]), sb("var", [128, 3, PASS_TILES]))
        xn = sb("xn", [128, PASS_TOK])
        xn_t = sb("xn_t", [128, PASS_TOK])
        proj_t = sb("proj_t", [128, PASS_TOK])
        score = sb("score", [128, PASS_TILES, CTX])
        stat = sb("stat", [128, 3, PASS_TILES])
        score_t = sb("score_t", [CTX, PASS_TOK])
        loaded, own_v = sem("loaded"), sem("own_vector")
        normed, x_turned, xn_t_made, proj_done, proj_made, s_done, s_sub, s_exp, s_turned, s_t_made, o_done = (
            sem("normed"), sem("x_turned"), sem("xn_t_made"), sem("proj_done"), sem("proj_made"), sem("s_done"), sem("s_sub"), sem("s_exp"), sem("s_turned"), sem("s_t_made"), sem("o_done"))
        ctx.callback(clear, nc, used)
        block = ctx.enter_context(nc.Block())

        @block.sync
        def _(sp):
            sp.dma_start(w[:, :], dram["y_W"]).then_inc(loaded, 16)
            sp.dma_start(b[:, :], dram["y_b"]).then_inc(loaded, 16)
            sp.dma_start(ctx_t[:, :], dram["ctx_t"]).then_inc(loaded, 16)
            sp.dma_start(ctx_rows[:, :, :], dram["ctx_rows"]).then_inc(loaded, 16)

        @block.tensor
        def _(pe):
            pe.wait_ge(loaded, 64)
            with pe.Fori(0, PASSES) as p:
                pe.wait_ge(normed, p + 1)
                for t in range(PASS_TILES):
                    last = nc.tensor.transpose(bank[0][:, 128 * t:128 * t + 128], xn[:, 128 * t:128 * t + 128], ident[:, :])
                last.then_inc(x_turned, 1)
                pe.wait_ge(xn_t_made, p + 1)
                nc.tensor.matmul(bank[1][:, :], w[:, :], xn_t[:, :], start=True, stop=True).then_inc(proj_done, 1)
                pe.wait_ge(proj_made, p + 1)
                for t in range(PASS_TILES):
                    last = nc.tensor.matmul(bank[2][:, CTX * t:CTX * t + CTX], proj_t[:, 128 * t:128 * t + 128],
                                            ctx_t[:, bass.ds(p * (2 * CTX) + CTX * (t // 2), CTX)], start=True, stop=True)
                last.then_inc(s_done, 1)
                pe.wait_ge(s_exp, p + 1)
                alone(pe)
                for t in range(PASS_TILES):
                    last = nc.tensor.transpose(bank[3][0:CTX, 128 * t:128 * t + 128], score[:, t, :], ident[:, :])
                last.then_inc(s_turned, 1)
                pe.wait_ge(s_t_made, p + 1)
                for t in range(PASS_TILES):
                    last = nc.tensor.matmul(bank[4][:, 128 * t:128 * t + 128], score_t[:, 128 * t:128 * t + 128],
                                            ctx_rows[:, bass.ds(p * 2 + t // 2, 1), :].rearrange("p a n -> p (a n)"), start=True, stop=True)
                last.then_inc(o_done, 1)

        @block.vector
        def _(dve):
            chain = Chain(dve, own_v)

            def norm_pass(p):
                dve.wait_ge(x_turned, p)
                alone(dve)
                layer_norm_tiles(nc, dve, chain, lambda t: x_all[:, bass.ds(p * PASS_TOK + 128 * t, 128)],
                                 lambda t: xn[:, 128 * t:128 * t + 128], work).then_inc(normed, 1)

            def one_pass(p, last_pass=False):
                dve.wait_ge(s_done, p + 1)
                scores = bank[2][:, 0:PASS_TILES * CTX].rearrange("p (t n) -> p t n", n=CTX)
                chain.link(nc.vector.tensor_reduce(stat[:, 0, :], scores, AX_X, ALU.max))
                nc.vector.tensor_tensor(score[:, :, :], scores, over(stat[:, 0, :], [128, PASS_TILES, CTX]), ALU.subtract).then_inc(s_sub, 1)
                if not last_pass:
                    norm_pass(p + 1)
                dve.wait_ge(s_exp, p + 1)
                chain.link(nc.vector.tensor_reduce(stat[:, 1, :], score[:, :, :], AX_X, ALU.add))
                chain.link(nc.vector.reciprocal(stat[:, 2, :], stat[:, 1, :]))
                dve.wait_ge(o_done, p + 1)
                for t in range(PASS_TILES):
                    x = x_all[:, bass.ds(p * PASS_TOK + 128 * t, 128)]
                    chain.mark(nc.vector.scalar_tensor_tensor(x, bank[4][:, 128 * t:128 * t + 128], stat[:, 2, t:t + 1], x, ALU.mult, ALU.add))
                chain.reset()

            norm_pass(0)
            chain.reset()
            with dve.Fori(0, PASSES - 1) as p:
                one_pass(p)
            one_pass(PASSES - 1, last_pass=True)

        @block.scalar
        def _(act):
            act.wait_ge(loaded, 64)
            with act.Fori(0, PASSES) as p:
                act.wait_ge(x_turned, p + 1)
                nc.scalar.activation(xn_t[:, :], bank[0][:, :], ACT.Copy).then_inc(xn_t_made, 1)
                act.wait_ge(proj_done, p + 1)
                nc.scalar.activation(proj_t[:, :], bank[1][:, :], ACT.Identity, bias=b[:, :]).then_inc(proj_made, 1)
                act.wait_ge(s_sub, p + 1)
                nc.scalar.activation(score[:, :, :], score[:, :, :], ACT.Exp).then_inc(s_exp, 1)
                act.wait_ge(s_turned, p + 1)
                nc.scalar.activation(score_t[:, :], bank[3][0:CTX, :], ACT.Copy).then_inc(s_t_made, 1)


EXPERTS = 8
FF = 512
CHUNKS = FF // 128
CAPACITY = BATCH * SEQ // EXPERTS
TOP_BIT = 29


def experts(nc, x_all, ident, dram):
    with ExitStack() as ctx:
        weight = ctx.enter_context(nc.sbuf_tensor("e_weight", [128, TILES * EXPERTS], F32))
        xn_t_all = ctx.enter_context(nc.sbuf_tensor("e_xn_t_all", [128, TILES * 128], F32))
        w1 = ctx.enter_context(nc.sbuf_tensor("e_w1", [128, EXPERTS, FF], F32))
        w2 = ctx.enter_context(nc.sbuf_tensor("e_w2", [128, EXPERTS, CHUNKS, DIM], F32))
        b1 = ctx.enter_context(nc.sbuf_tensor("e_b1", [128, EXPERTS * CHUNKS], F32))
        b2 = ctx.enter_context(nc.sbuf_tensor("e_b2", [EXPERTS, DIM], F32))
        w_in = ctx.enter_context(nc.semaphore("e_w_in"))
        ctx.callback(clear, nc, [w_in])
        route(nc, x_all, ident, dram, weight, xn_t_all, (w1, w2, b1, b2), w_in)
        choose(nc, weight)
        apply_experts(nc, x_all, ident, weight, xn_t_all, (w1, w2, b1, b2), w_in)


def route(nc, x_all, ident, dram, prob, xn_t_all, weights, w_in):
    with ExitStack() as ctx:
        def sb(name, shape, dt=F32):
            return ctx.enter_context(nc.sbuf_tensor("er_" + name, shape, dt))

        used = []

        def sem(name):
            used.append(ctx.enter_context(nc.semaphore("er_" + name)))
            return used[-1]

        bank = [ctx.enter_context(nc.psum_tensor(f"er_bank{i}", [128, 512], F32)) for i in range(2)]
        ws, bs, ones = sb("ws", [128, EXPERTS]), sb("bs", [1, EXPERTS]), sb("ones", [1, 128])
        work = (sb("stats", [128, PASS_TILES, 6]), sb("mv", [128, PASS_TILES, 2]), sb("var", [128, 3, PASS_TILES]))
        xn = sb("xn", [128, PASS_TOK])
        xn_t = sb("xn_t", [128, PASS_TOK])
        score = sb("score", [128, PASS_TILES, EXPERTS])
        stat = sb("stat", [128, 3, PASS_TILES])
        loaded, ones_set, own_v = sem("loaded"), sem("ones_set"), sem("own_vector")
        normed, x_turned, xn_t_made, xn_t_kept, s_done, s_sub, s_exp = (
            sem("normed"), sem("x_turned"), sem("xn_t_made"), sem("xn_t_kept"), sem("s_done"), sem("s_sub"), sem("s_exp"))
        ctx.callback(clear, nc, used)
        block = ctx.enter_context(nc.Block())

        @block.sync
        def _(sp):
            sp.dma_start(ws[:, :], dram["e_Ws"]).then_inc(loaded, 16)
            sp.dma_start(bs[:, :], dram["e_bs"]).then_inc(loaded, 16)
            for held, name in zip(weights, ("e_W1", "e_W2", "e_b1", "e_b2")):
                flat = held[:, :] if len(held.shape) == 2 else held[:, :, :] if len(held.shape) == 3 else held[:, :, :, :]
                sp.dma_start(flat, dram[name]).then_inc(w_in, 16)

        @block.gpsimd
        def _(pool):
            nc.gpsimd.memset(ones[:, :], 1.0).then_inc(ones_set, 1)
            with pool.Fori(0, PASSES) as p:
                pool.wait_ge(xn_t_made, p + 1)
                nc.gpsimd.tensor_copy(xn_t_all[:, bass.ds(p * PASS_TOK, PASS_TOK)], xn_t[:, :]).then_inc(xn_t_kept, 1)

        @block.tensor
        def _(pe):
            pe.wait_ge(loaded, 32)
            pe.wait_ge(ones_set, 1)
            with pe.Fori(0, PASSES) as p:
                pe.wait_ge(normed, p + 1)
                for t in range(PASS_TILES):
                    last = nc.tensor.transpose(bank[0][:, 128 * t:128 * t + 128], xn[:, 128 * t:128 * t + 128], ident[:, :])
                last.then_inc(x_turned, 1)
                pe.wait_ge(xn_t_made, p + 1)
                for t in range(PASS_TILES):
                    s = bank[1][:, EXPERTS * t:EXPERTS * t + EXPERTS]
                    nc.tensor.matmul(s, xn_t[:, 128 * t:128 * t + 128], ws[:, :], start=True, stop=False)
                    last = nc.tensor.matmul(s, ones[:, :], bs[:, :], start=False, stop=True)
                last.then_inc(s_done, 1)

        @block.vector
        def _(dve):
            chain = Chain(dve, own_v)

            def norm_pass(p):
                dve.wait_ge(x_turned, p)
                alone(dve)
                layer_norm_tiles(nc, dve, chain, lambda t: x_all[:, bass.ds(p * PASS_TOK + 128 * t, 128)],
                                 lambda t: xn[:, 128 * t:128 * t + 128], work).then_inc(normed, 1)

            def one_pass(p, last_pass=False):
                dve.wait_ge(s_done, p + 1)
                scores = bank[1][:, 0:PASS_TILES * EXPERTS].rearrange("p (t n) -> p t n", n=EXPERTS)
                chain.link(nc.vector.tensor_reduce(stat[:, 0, :], scores, AX_X, ALU.max))
                nc.vector.tensor_tensor(score[:, :, :], scores, over(stat[:, 0, :], [128, PASS_TILES, EXPERTS]), ALU.subtract).then_inc(s_sub, 1)
                if not last_pass:
                    norm_pass(p + 1)
                dve.wait_ge(s_exp, p + 1)
                chain.link(nc.vector.tensor_reduce(stat[:, 1, :], score[:, :, :], AX_X, ALU.add))
                chain.link(nc.vector.reciprocal(stat[:, 2, :], stat[:, 1, :]))
                kept = prob[:, bass.ds(p * (PASS_TILES * EXPERTS), PASS_TILES * EXPERTS)].rearrange("p (t n) -> p t n", n=EXPERTS)
                chain.mark(nc.vector.tensor_tensor(kept, score[:, :, :], over(stat[:, 2, :], [128, PASS_TILES, EXPERTS]), ALU.mult))
                chain.reset()

            norm_pass(0)
            chain.reset()
            with dve.Fori(0, PASSES - 1) as p:
                one_pass(p)
            one_pass(PASSES - 1, last_pass=True)

        @block.scalar
        def _(act):
            with act.Fori(0, PASSES) as p:
                act.wait_ge(x_turned, p + 1)
                act.wait_ge(xn_t_kept, p)
                nc.scalar.activation(xn_t[:, :], bank[0][:, :], ACT.Copy).then_inc(xn_t_made, 1)
                act.wait_ge(s_sub, p + 1)
                nc.scalar.activation(score[:, :, :], score[:, :, :], ACT.Exp).then_inc(s_exp, 1)


def choose(nc, weight):
    with ExitStack() as ctx:
        def sb(name, shape, dt=F32):
            return ctx.enter_context(nc.sbuf_tensor("ec_" + name, shape, dt))

        used = []

        def sem(name):
            used.append(ctx.enter_context(nc.semaphore("ec_" + name)))
            return used[-1]

        bank = [ctx.enter_context(nc.psum_tensor(f"ec_bank{i}", [128, 512], F32)) for i in range(3)]
        ones, before = sb("ones", [128, 128]), sb("before", [128, 128])
        threshold, attempt, gain = sb("threshold", [128, EXPERTS], I32), sb("attempt", [128, EXPERTS], I32), sb("gain", [128, EXPERTS], I32)
        bit, bit_int = sb("bit", [128, 1]), sb("bit_int", [128, 1], I32)
        reached = sb("reached", [128, TILES, EXPERTS])
        equal = sb("equal", [128, TILES, EXPERTS])
        sums = [sb("sums0", [128, TILES, EXPERTS]), sb("sums1", [128, TILES, EXPERTS])]
        part = sb("part", [128, EXPERTS])
        left = sb("left", [128, EXPERTS])
        own_v, own_pool, tables, counted, total_done, above_counted, above_done, equal_marked, ranks_done = (
            sem("own_vector"), sem("own_pool"), sem("tables"), sem("counted"), sem("total_done"), sem("above_counted"), sem("above_done"),
            sem("equal_marked"), sem("ranks_done"))
        p3 = weight[:, :].rearrange("p (t n) -> p t n", n=EXPERTS)
        shape = [128, TILES, EXPERTS]

        def per_tile(ap):
            return ap.unsqueeze(1).broadcast_to(shape)

        ctx.callback(clear, nc, used)
        block = ctx.enter_context(nc.Block())

        @block.gpsimd
        def _(pool):
            nc.gpsimd.memset(ones[:, :], 1.0).then_inc(own_pool, 1)
            nc.gpsimd.memset(before[:, :], 0.0).then_inc(own_pool, 1)
            pool.wait_ge(own_pool, 2)
            nc.gpsimd.affine_select(out=before[:, :], in_=before[:, :], compare_op=ALU.is_ge, fill=1.0, base=0,
                                    pattern=[[-1, 128]], channel_multiplier=1).then_inc(tables, 1)

        @block.tensor
        def _(pe):
            pe.wait_ge(tables, 1)
            with pe.Fori(0, TOP_BIT + 1) as i:
                pe.wait_ge(counted, i + 1)
                nc.tensor.matmul(bank[0][:, 0:EXPERTS], ones[:, :], part[:, :], start=True, stop=True).then_inc(total_done, 1)
            pe.wait_ge(above_counted, 1)
            nc.tensor.matmul(bank[0][:, 0:EXPERTS], ones[:, :], part[:, :], start=True, stop=True).then_inc(above_done, 1)
            pe.wait_ge(equal_marked, 1)
            nc.tensor.matmul(bank[1][:, 0:TILES * EXPERTS], before[:, :], equal[:, :, :].rearrange("p t n -> p (t n)"), start=True, stop=True)
            nc.tensor.matmul(bank[2][:, 0:TILES * EXPERTS], ones[:, :], equal[:, :, :].rearrange("p t n -> p (t n)"), start=True, stop=True).then_inc(ranks_done, 1)

        @block.vector
        def _(dve):
            chain = Chain(dve, own_v)
            chain.mark(nc.vector.memset(threshold[:, :], 0))
            chain.link(nc.vector.memset(bit[:, :], float(2 ** TOP_BIT)))
            chain.reset()
            with dve.Fori(0, TOP_BIT + 1) as i:
                chain.link(nc.vector.tensor_copy(bit_int[:, :], bit[:, :]))
                chain.link(nc.vector.tensor_tensor(attempt[:, :], threshold[:, :], bit_int[:, :].broadcast_to([128, EXPERTS]), ALU.bitwise_or))
                chain.link(nc.vector.tensor_tensor(reached[:, :, :], p3, per_tile(attempt[:, :].bitcast(F32)), ALU.is_ge))
                nc.vector.tensor_reduce(part[:, :], reached[:, :, :].rearrange("p t n -> p n t"), AX_X, ALU.add).then_inc(counted, 1)
                dve.wait_ge(total_done, i + 1)
                chain.link(nc.vector.tensor_scalar(gain[:, :], bank[0][:, 0:EXPERTS], float(CAPACITY), bit[:, :], ALU.is_ge, ALU.mult))
                chain.mark(nc.vector.tensor_tensor(threshold[:, :], threshold[:, :], gain[:, :], ALU.bitwise_or))
                chain.mark(nc.vector.tensor_scalar(bit[:, :], bit[:, :], 0.5, None, ALU.mult))
                chain.reset()
            limit = per_tile(threshold[:, :].bitcast(F32))
            nc.vector.tensor_tensor(equal[:, :, :], p3, limit, ALU.is_equal).then_inc(equal_marked, 1)
            chain.link(nc.vector.tensor_tensor(reached[:, :, :], p3, limit, ALU.is_gt))
            nc.vector.tensor_reduce(part[:, :], reached[:, :, :].rearrange("p t n -> p n t"), AX_X, ALU.add).then_inc(above_counted, 1)
            dve.wait_ge(ranks_done, 1)
            chain.link(nc.vector.tensor_copy(sums[0][:, :, :].rearrange("p t n -> p (t n)"), bank[2][:, 0:TILES * EXPERTS]))
            step, now = 1, 0
            while step < TILES:
                a, b = sums[now], sums[1 - now]
                chain.mark(nc.vector.tensor_copy(b[:, 0:step, :], a[:, 0:step, :]))
                chain.link(nc.vector.tensor_tensor(b[:, step:, :], a[:, step:, :], a[:, 0:TILES - step, :], ALU.add))
                step, now = 2 * step, 1 - now
            a, b = sums[now], sums[1 - now]
            flat = [m[:, :, :].rearrange("p t n -> p (t n)") for m in (a, b)]
            chain.link(nc.vector.tensor_tensor(flat[1], flat[0], bank[2][:, 0:TILES * EXPERTS], ALU.subtract))
            chain.link(nc.vector.tensor_tensor(flat[1], flat[1], bank[1][:, 0:TILES * EXPERTS], ALU.add))
            dve.wait_ge(above_done, 1)
            chain.link(nc.vector.tensor_scalar(left[:, :], bank[0][:, 0:EXPERTS], -1.0, float(CAPACITY), ALU.mult, ALU.add))
            chain.link(nc.vector.tensor_tensor(b[:, :, :], b[:, :, :], per_tile(left[:, :]), ALU.is_lt))
            chain.link(nc.vector.tensor_tensor(b[:, :, :], b[:, :, :], equal[:, :, :], ALU.mult))
            chain.link(nc.vector.tensor_tensor(b[:, :, :], b[:, :, :], reached[:, :, :], ALU.add))
            nc.vector.tensor_tensor(p3, p3, b[:, :, :], ALU.mult)


def apply_experts(nc, x_all, ident, weight, xn_t_all, weights, w_in):
    w1, w2, b1, b2 = weights
    with ExitStack() as ctx:
        def sb(name, shape, dt=F32):
            return ctx.enter_context(nc.sbuf_tensor("ea_" + name, shape, dt))

        used = []

        def sem(name):
            used.append(ctx.enter_context(nc.semaphore("ea_" + name)))
            return used[-1]

        h_bank = [ctx.enter_context(nc.psum_tensor(f"ea_h_bank{i}", [128, 512], F32)) for i in range(CHUNKS)]
        o_bank = [ctx.enter_context(nc.psum_tensor(f"ea_o_bank{i}", [128, 512], F32)) for i in range(2)]
        b_bank = ctx.enter_context(nc.psum_tensor("ea_b_bank", [128, 512], F32))
        t_bank = ctx.enter_context(nc.psum_tensor("ea_t_bank", [128, 512], F32))
        h = sb("h", [128, 2, CHUNKS, PASS_TOK])
        w_now = sb("w_now", [128, PASS_TILES * EXPERTS])
        w_t = sb("w_t", [EXPERTS, PASS_TOK])
        acc = sb("acc", [128, PASS_TILES, DIM])
        own_v = sem("own_vector")
        w_ready, w_turned, w_t_made, bias_done, h_done, h_made, o_done, o_added = (
            sem("w_ready"), sem("w_turned"), sem("w_t_made"), sem("bias_done"), sem("h_done"), sem("h_made"), sem("o_done"), sem("o_added"))
        per_pass = EXPERTS * CHUNKS
        ctx.callback(clear, nc, used)
        block = ctx.enter_context(nc.Block())

        @block.tensor
        def _(pe):
            def first_product(p, e):
                for c in range(CHUNKS):
                    if e > 0:
                        pe.wait_ge(h_made, p * per_pass + (CHUNKS * (e - 1) + c + 1))
                    nc.tensor.matmul(h_bank[c][:, :], w1[:, e, 128 * c:128 * c + 128], xn_t_all[:, bass.ds(p * PASS_TOK, PASS_TOK)],
                                     start=True, stop=True).then_inc(h_done, 1)

            def second_product(p, e):
                pe.wait_ge(o_added, p * EXPERTS + max(e - 1, 0))
                pe.wait_ge(h_made, p * per_pass + CHUNKS * (e + 1))
                for t in range(PASS_TILES):
                    for c in range(CHUNKS):
                        last = nc.tensor.matmul(o_bank[e % 2][:, 128 * t:128 * t + 128], h[:, e % 2, c, 128 * t:128 * t + 128], w2[:, e, c, :],
                                                start=c == 0, stop=c == CHUNKS - 1)
                last.then_inc(o_done, 1)

            pe.wait_ge(w_in, 64)
            with pe.Fori(0, PASSES) as p:
                first_product(p, 0)
                pe.wait_ge(w_ready, p + 1)
                for t in range(PASS_TILES):
                    last = nc.tensor.transpose(t_bank[0:EXPERTS, 128 * t:128 * t + 128], w_now[:, EXPERTS * t:EXPERTS * t + EXPERTS], ident[:, :])
                last.then_inc(w_turned, 1)
                first_product(p, 1)
                pe.wait_ge(w_t_made, p + 1)
                for t in range(PASS_TILES):
                    last = nc.tensor.matmul(b_bank[:, 128 * t:128 * t + 128], w_t[:, 128 * t:128 * t + 128], b2[:, :], start=True, stop=True)
                last.then_inc(bias_done, 1)
                for e in range(1, EXPERTS):
                    second_product(p, e - 1)
                    if e + 1 < EXPERTS:
                        first_product(p, e + 1)
                second_product(p, EXPERTS - 1)

        @block.scalar
        def _(act):
            act.wait_ge(w_in, 64)
            with act.Fori(0, PASSES) as p:
                for e in range(EXPERTS):
                    for c in range(CHUNKS):
                        act.wait_ge(h_done, p * per_pass + (CHUNKS * e + c + 1))
                        at = CHUNKS * e + c
                        nc.scalar.activation(h[:, e % 2, c, :], h_bank[c][:, :], ACT.Gelu_apprx_tanh, bias=b1[:, at:at + 1]).then_inc(h_made, 1)
                    if e == 0:
                        act.wait_ge(w_turned, p + 1)
                        nc.scalar.activation(w_t[:, :], t_bank[0:EXPERTS, :], ACT.Copy).then_inc(w_t_made, 1)

        @block.vector
        def _(dve):
            chain = Chain(dve, own_v)
            with dve.Fori(0, PASSES) as p:
                nc.vector.tensor_copy(w_now[:, :], weight[:, bass.ds(p * (PASS_TILES * EXPERTS), PASS_TILES * EXPERTS)]).then_inc(w_ready, 1)
                dve.wait_ge(bias_done, p + 1)
                flat = acc[:, :, :].rearrange("p t n -> p (t n)")
                x = x_all[:, bass.ds(p * PASS_TOK, PASS_TOK)]
                chain.link(nc.vector.tensor_tensor(flat, b_bank[:, :], x, ALU.add))
                for e in range(EXPERTS):
                    if e > 0:
                        dve.wait_ge(o_added, p * EXPERTS + e)
                    dve.wait_ge(o_done, p * EXPERTS + (e + 1))
                    for t in range(PASS_TILES):
                        at = EXPERTS * t + e
                        last = nc.vector.scalar_tensor_tensor(acc[:, t, :], o_bank[e % 2][:, 128 * t:128 * t + 128], w_now[:, at:at + 1], acc[:, t, :], ALU.mult, ALU.add)
                    last.then_inc(o_added, 1)
                dve.wait_ge(o_added, p * EXPERTS + EXPERTS)
                alone(dve)
                chain.link(nc.vector.tensor_copy(x, flat))
                chain.reset()


def build(nc, arrays, out):
    with ExitStack() as ctx:
        x_all = ctx.enter_context(nc.sbuf_tensor("x_all", [128, TILES * DIM], F32))
        ident = ctx.enter_context(nc.sbuf_tensor("ident", [128, 128], F32))
        ident_bf = ctx.enter_context(nc.sbuf_tensor("ident_bf", [128, 128], BF16))
        x_in, ident_cleared, ident_made, x_out = (ctx.enter_context(nc.semaphore(n)) for n in ("x_in", "ident_cleared", "ident_made", "x_out"))
        with nc.Block() as block:

            @block.sync
            def _(sp):
                sp.dma_start(x_all[:, :], arrays["x"]).then_inc(x_in, 16)
                sp.wait_ge(x_in, 16)

            @block.gpsimd
            def _(pool):
                nc.gpsimd.memset(ident[:, :], 0.0).then_inc(ident_cleared, 1)
                nc.gpsimd.memset(ident_bf[:, :], 0.0).then_inc(ident_cleared, 1)
                pool.wait_ge(ident_cleared, 2)
                for m in (ident, ident_bf):
                    nc.gpsimd.affine_select(out=m[:, :], in_=m[:, :], compare_op=ALU.not_equal, fill=1.0, base=0,
                                            pattern=[[-1, 128]], channel_multiplier=1).then_inc(ident_made, 1)
                pool.wait_ge(ident_made, 2)

        cross_attention(nc, x_all, ident, ident_bf, arrays)
        with nc.sbuf_tensor("s_all", [128, TILES * DIM], F32) as s_all:
            norm_all(nc, x_all, s_all, "fn")
            shifted_layers(nc, s_all, ident, ident_bf, arrays)
            add_all(nc, x_all, s_all)
        kernel_attention(nc, x_all, ident, arrays)
        with nc.sbuf_tensor("s2_all", [128, TILES * DIM], F32) as s_all:
            norm_all(nc, x_all, s_all, "qn")
            quantised_ffn(nc, x_all, s_all, ident, arrays)
        two_attentions(nc, x_all, ident, ident_bf, arrays)
        ternary_ffn(nc, x_all, ident, arrays)
        context_attention(nc, x_all, ident, arrays)
        experts(nc, x_all, ident, arrays)
        with nc.Block() as block:

            @block.sync
            def _(sp):
                sp.dma_start(out, x_all[:, :]).then_inc(x_out, 16)
                sp.wait_ge(x_out, 16)


def constants():
    half = np.arange(0, HEAD_DIM, 2, dtype=np.float32)
    inv_freq = (np.float32(1.0) / np.power(np.float32(10000.0), half / np.float32(HEAD_DIM))).astype(np.float32)
    t = np.arange(SEQ, dtype=np.float32)
    freqs = t[:, None] * inv_freq[None, :]
    base = ((half + np.float32(0.4 * HEAD_DIM)) / np.float32(1.4 * HEAD_DIM)).astype(np.float32)
    power = (t - SEQ // 2) / np.float32(16)
    scale = np.power(base[None, :], power[:, None]).astype(np.float32)
    cos, sin = np.cos(freqs), np.sin(freqs)
    rot = np.zeros((SEQ, 4, HEAD_DIM), np.float32)
    for n, s in ((0, scale), (2, np.float32(1.0) / scale)):
        rot[:, n, :] = np.concatenate([cos * s, cos * s], -1)
        rot[:, n + 1, :] = np.concatenate([-sin * s, sin * s], -1)
    rot = rot.reshape(2, 128, 4, HEAD_DIM).transpose(1, 0, 2, 3)
    row, col = np.arange(128)[:, None], np.arange(64)[None, :]
    r = row % 32
    keep = (col >= r) & (col <= r + 32)
    first = keep & ((row >= 32) | (col >= 32))
    band = np.stack([np.where(k, 0.0, -1e25).astype(np.float32) for k in (first, keep)], 1)
    band = np.tile(band, (1, 1, GROUP))
    return {"rot": np.ascontiguousarray(rot), "band": band}


def lay_out(i):
    c = np.ascontiguousarray
    f = {n: np.asarray(i[n]) for n in i}
    d = dict(constants())
    d["x"] = c(f["x"].reshape(TILES, 128, DIM).transpose(1, 0, 2)).reshape(128, TILES * DIM)
    d["Wqkv"] = c(f["L0_ffn_Wqkv"])
    d["Wo"] = c(f["L0_ffn_Wo"].reshape(6, PAIRS, 128, DIM).transpose(0, 2, 1, 3))
    d["W1"] = c(f["L0_ffn_W1"])
    w2 = np.zeros((6, 3 * 128, DIM), np.float32)
    w2[:, 0:341] = f["L0_ffn_W2"]
    w2[:, 2 * 128 + 96] = f["L0_ffn_b2"]
    d["W2"] = c(w2.reshape(6, 3, 128, DIM).transpose(0, 2, 1, 3))
    cols = np.zeros((6, 8, 384), np.float32)
    cols[:, 0, 0:128] = f["L0_ffn_ln_g"]
    cols[:, 1, 0:128] = f["L0_ffn_ln_b"]
    for k, (at, n) in enumerate(((0, 128), (128, 128), (256, 85))):
        cols[:, 2 + k, 0:n] = f["L0_ffn_b1"][:, 341 + at:341 + at + n]
        cols[:, 5 + k, 0:n] = f["L0_ffn_b1"][:, at:at + n]
    d["cols"] = c(cols[:, :, 0:128].transpose(0, 2, 1))
    qs, ks = f["L0_ffn_q_scale"], f["L0_ffn_k_scale"]
    turn = np.concatenate([np.arange(32, 64), np.arange(0, 32)])
    four = np.stack([qs, qs[:, turn], ks, ks[:, turn]], 1)
    d["qk_scale"] = c(np.broadcast_to(four[:, None], (6, 128, 4, HEAD_DIM)))
    ctx = f["ctx_1024"]
    d["ctx_t"] = c(ctx.reshape(BATCH * CTX, DIM).T)
    d["ctx_rows"] = c(ctx.transpose(1, 0, 2))
    d["mask"] = c(f["mask_BxS2_bf1"].reshape(1, BATCH * CTX)).view(np.uint8)
    d["x_Wq"] = c(f["L0_xattn_Wq"].T)
    kv = f["L0_xattn_Wkv"].T
    odd_even = kv[:, INNER:].reshape(DIM, PAIRS, 2, HEAD_DIM).transpose(0, 2, 1, 3).reshape(DIM, INNER)
    d["x_Wkv"] = c(np.concatenate([kv[:, :INNER], odd_even], 1))
    d["x_Wout"] = c(f["L0_xattn_Wout"].T.reshape(PAIRS, 128, DIM).transpose(1, 0, 2))
    d["x_b"] = c(f["L0_xattn_b_out"].reshape(1, DIM))
    gu = np.zeros((2, 3 * 128, DIM), np.float32)
    gu[0, :352], gu[1, :352] = f["L1_ffn_w_gate"], f["L1_ffn_w_up"]
    d["q_gu"] = c(gu.reshape(6, 128, DIM).transpose(1, 0, 2))
    down = np.zeros((DIM, 3 * 128), np.float32)
    down[:, :352] = f["L1_ffn_w_down"]
    d["q_d"] = down
    d["q_clips"] = c(np.broadcast_to(np.concatenate([f["L1_ffn_clip_x"], f["L1_ffn_clip_down"]]), (128, 2)))
    for n in ("Wk1", "Wq1", "Wv1", "Wk2", "Wq2", "Wv2", "W1", "W2"):
        d["a_" + n] = c(f["L2_xattn_" + n])
    d["a_rows"] = c(np.broadcast_to(np.stack([f["L2_xattn_gamma"], f["L2_xattn_beta"], f["L2_xattn_b2"]]), (128, 3, DIM)))
    d["a_b1"] = c(f["L2_xattn_b1"].reshape(DIM, 1))
    d["causal"] = np.where(np.arange(128)[None, :] > np.arange(128)[:, None], -1e30, 0.0).astype(np.float32)
    d["g_fc"] = c(f["L2_ffn_W_fc"].T)
    d["g_proj"] = c(f["L2_ffn_W_proj"].T.reshape(4, 128, DIM).transpose(1, 0, 2)).reshape(128, 4 * DIM)
    d["g_affine"] = c(np.stack([f["L2_ffn_ln_w"], f["L2_ffn_ln_b"]]).reshape(2, 4, 128).transpose(2, 0, 1))
    d["y_W"] = c(f["L3_xattn_W"])
    d["y_b"] = c(f["L3_xattn_b"].reshape(DIM, 1))
    d["e_Ws"] = c(f["L3_ffn_Ws"])
    d["e_bs"] = c(f["L3_ffn_bs"].reshape(1, EXPERTS))
    d["e_W1"] = c(f["L3_ffn_W1"].transpose(1, 0, 2))
    d["e_W2"] = c(f["L3_ffn_W2"].reshape(EXPERTS, CHUNKS, 128, DIM).transpose(2, 0, 1, 3))
    d["e_b1"] = c(f["L3_ffn_b1"].reshape(EXPERTS * CHUNKS, 128).T)
    d["e_b2"] = c(f["L3_ffn_b2"])
    d["k_proj"] = c(f["L1_xattn_projection"].T)
    return d


def kernel(**inputs):
    import concourse.bacc as _bacc
    from concourse.bass_utils import run_bass_kernel_spmd as _run

    nc = _bacc.Bacc("TRN2", target_bir_lowering=False, num_devices=1)
    arrays = lay_out(inputs)
    aps = {n: nc.dram_tensor("in_" + n, a.shape, mybir.dt.from_np(a.dtype), kind="ExternalInput").ap() for n, a in arrays.items()}
    out = nc.dram_tensor("out", (128, TILES * DIM), F32, kind="ExternalOutput").ap()
    build(nc, aps, out)
    r = _run(nc, [{"in_" + n: a for n, a in arrays.items()}], core_ids=[0])
    y = np.asarray(r.results[0]["out"]).reshape(128, TILES, DIM)
    return np.ascontiguousarray(y.transpose(1, 0, 2)).reshape(BATCH, SEQ, DIM)
```
